# Optimizing a Trainium2 kernel written in Bass

```python
import numpy as np
import jax
import jax.numpy as jnp

def _softmax(x, axis=-1):
    return jax.nn.softmax(x, axis=axis)

def _gelu(x):
    return jax.nn.gelu(x, approximate=True)

def _silu(x):
    return jax.nn.silu(x)

def _sigmoid(x):
    return jax.nn.sigmoid(x)

def _layernorm(x, axis=-1, eps=1e-05):
    m = jnp.mean(x, axis=axis, keepdims=True)
    v = jnp.var(x, axis=axis, keepdims=True)
    return (x - m) / jnp.sqrt(v + eps)

def _scatter_add(tgt, idx, src, axis=0):
    return tgt.at[idx].add(src)

def _segment_sum(src, seg, n):
    return jax.ops.segment_sum(src, seg, n)
kernel_name = 'mk_decoder_preln_d2_seqx_r8_97f2d3'

def setup_inputs(seed: int=0):
    np.random.seed(seed)
    _w = jnp.asarray

    def _rec_inputs():
        import jax
        import jax.numpy as jnp
        _rk = jax.random.key(seed)
        x = 7.22e-05 + 1 * jax.random.normal(jax.random.fold_in(_rk, 1), (64, 128, 128), jnp.float32)
        _lenS = 128 - jax.random.randint(jax.random.fold_in(_rk, 7), (64,), 0, max(1, 128 // 4) + 1, jnp.int32)
        _lenS2 = 77 - jax.random.randint(jax.random.fold_in(_rk, 8), (64,), 0, max(1, 77 // 4) + 1, jnp.int32)
        _ctx_1024P = jax.random.normal(jax.random.fold_in(_rk, 11), (64, 16, 128), jnp.float32)
        _ctx_1024c = jax.random.dirichlet(jax.random.fold_in(_rk, 511), 0.3 * jnp.ones((16,), jnp.float32), (64, 77))
        _ctx_1024t = jnp.einsum('bsk,bkd->bsd', _ctx_1024c, _ctx_1024P)
        _ctx_1024t = _ctx_1024t * jax.lax.rsqrt(jnp.mean(jnp.square(_ctx_1024t)) + 1e-12) * 0.953939
        ctx_1024 = 4.13588e-05 + 0.999923 * (_ctx_1024t + 0.3 * jax.random.normal(jax.random.fold_in(_rk, 611), (64, 77, 128), jnp.float32))
        _validS = jnp.arange(128)[None, :] < _lenS[:, None]
        _validS2 = jnp.arange(77)[None, :] < _lenS2[:, None]
        _causal = jnp.tril(jnp.ones((128, 128), dtype=bool))
        mask_Bx1x1xS2_bk0 = jnp.logical_not(jnp.broadcast_to(_validS2[:, None, None, :], (64, 1, 1, 77)))
        return (x, ctx_1024, mask_Bx1x1xS2_bk0)
    x, ctx_1024, mask_Bx1x1xS2_bk0 = _rec_inputs()

    def _L0_attn_setup():
        import jax, jax.numpy as jnp
        import numpy as np
        B, S, HID = (4, 128, 128)
        H = 8
        HD = HID // H
        NQ = 8
        RATIO = 0.5
        FF = 4 * HID
        EPS_COS = 1e-08
        LN_EPS = 1e-05

        def _layernorm(x, g, b):
            m = jnp.mean(x, axis=-1, keepdims=True)
            v = jnp.var(x, axis=-1, keepdims=True)
            return (x - m) * jax.lax.rsqrt(v + LN_EPS) * g + b
        key = jax.random.key(seed)
        ks = jax.random.split(key, 24)
        sc = 0.02
        inp = {'x': jax.random.normal(ks[0], (B, S, HID), jnp.float32), 'Wq': jax.random.normal(ks[1], (H, HID, HD)) * sc, 'bq': jnp.zeros((H, HD)), 'Wk': jax.random.normal(ks[2], (H, HID, HD)) * sc, 'bk': jnp.zeros((H, HD)), 'Wv': jax.random.normal(ks[3], (H, HID, HD)) * sc, 'bv': jnp.zeros((H, HD)), 'Wc2q': jax.random.normal(ks[4], (H, HD, NQ)) * sc, 'bc2q': jnp.zeros((H, NQ)), 'Wo': jax.random.normal(ks[5], (HID, HID)) * sc, 'bo': jnp.zeros((HID,)), 'g1': jnp.ones((HID,)), 'beta1': jnp.zeros((HID,)), 'g2': jnp.ones((HID,)), 'beta2': jnp.zeros((HID,)), 'W1': jax.random.normal(ks[6], (HID, FF)) * sc, 'b1': jnp.zeros((FF,)), 'Wm': jax.random.normal(ks[7], (FF, NQ)) * sc, 'bm': jnp.zeros((NQ,)), 'Wqo': jax.random.normal(ks[8], (NQ, FF)) * sc, 'bqo': jnp.zeros((FF,)), 'W2': jax.random.normal(ks[9], (FF, HID)) * sc, 'b2': jnp.zeros((HID,))}
        return inp
    _L0_attn_all = _L0_attn_setup()
    _L0_attn_in = {k: v for k, v in _L0_attn_all.items() if k in ('Wq', 'bq', 'Wk', 'bk', 'Wv', 'bv', 'Wc2q', 'bc2q', 'Wo', 'bo', 'g1', 'beta1', 'g2', 'beta2', 'W1', 'b1', 'Wm', 'bm', 'Wqo', 'bqo', 'W2', 'b2')}
    del _L0_attn_all

    def _L0_xattn_setup():
        import jax, jax.numpy as jnp
        import numpy as np
        D_MODEL = 128
        NUM_HEADS = 16
        HEAD_DIM = D_MODEL // NUM_HEADS
        B, S = (4, 256)
        key = jax.random.key(seed)
        ks = jax.random.split(key, 11)
        sc = 1.0 / np.sqrt(D_MODEL)
        inp = {'query': jax.random.normal(ks[0], (B, S, D_MODEL), jnp.float32), 'key': jax.random.normal(ks[1], (B, S, D_MODEL), jnp.float32), 'value': jax.random.normal(ks[2], (B, S, D_MODEL), jnp.float32), 'Wq': jax.random.normal(ks[3], (D_MODEL, D_MODEL), jnp.float32) * sc, 'bq': jnp.zeros((D_MODEL,), jnp.float32), 'Wk': jax.random.normal(ks[4], (D_MODEL, D_MODEL), jnp.float32) * sc, 'bk': jnp.zeros((D_MODEL,), jnp.float32), 'Wv': jax.random.normal(ks[5], (D_MODEL, D_MODEL), jnp.float32) * sc, 'bv': jnp.zeros((D_MODEL,), jnp.float32), 'Wo': jax.random.normal(ks[6], (D_MODEL, D_MODEL), jnp.float32) * sc, 'bo': jnp.zeros((D_MODEL,), jnp.float32)}
        return inp
    _L0_xattn_all = _L0_xattn_setup()
    _L0_xattn_in = {k: v for k, v in _L0_xattn_all.items() if k in ('Wq', 'bq', 'Wk', 'bk', 'Wv', 'bv', 'Wo', 'bo')}
    del _L0_xattn_all

    def _L0_ffn_setup():
        import jax, jax.numpy as jnp
        import numpy as np
        S, B, H, I, E = (64, 2, 128, 352, 8)
        key = jax.random.key(seed)
        ks = jax.random.split(key, 5)
        return {'hidden_states': jax.random.normal(ks[0], (S, B, H), dtype=jnp.float32), 'router_w': jax.random.normal(ks[1], (E, H), dtype=jnp.float32) * 0.02, 'gate_w': jax.random.normal(ks[2], (E, I, H), dtype=jnp.float32) * 0.02, 'up_w': jax.random.normal(ks[3], (E, I, H), dtype=jnp.float32) * 0.02, 'down_w': jax.random.normal(ks[4], (E, H, I), dtype=jnp.float32) * 0.02}
    _L0_ffn_all = _L0_ffn_setup()
    _L0_ffn_in = {k: v for k, v in _L0_ffn_all.items() if k in ('router_w', 'gate_w', 'up_w', 'down_w')}
    del _L0_ffn_all

    def _L1_attn_setup():
        import jax, jax.numpy as jnp
        import numpy as np
        NUM_HEADS = 16
        PAD_ID = 0.0
        key = jax.random.key(seed)
        ks = jax.random.split(key, 9)
        B, T, C = (2, 256, 128)
        x = jax.random.normal(ks[0], (B, T, C), dtype=jnp.float32)
        lim = (6.0 / (C + C)) ** 0.5

        def w(k):
            return jax.random.uniform(k, (C, C), dtype=jnp.float32, minval=-lim, maxval=lim)

        def b(k):
            return jax.random.uniform(k, (C,), dtype=jnp.float32)
        return {'x': x, 'wq_w': w(ks[1]), 'wq_b': b(ks[2]), 'wk_w': w(ks[3]), 'wk_b': b(ks[4]), 'wv_w': w(ks[5]), 'wv_b': b(ks[6]), 'wo_w': w(ks[7]), 'wo_b': b(ks[8])}
    _L1_attn_all = _L1_attn_setup()
    _L1_attn_in = {k: v for k, v in _L1_attn_all.items() if k in ('wq_w', 'wq_b', 'wk_w', 'wk_b', 'wv_w', 'wv_b', 'wo_w', 'wo_b')}
    del _L1_attn_all

    def _L1_xattn_setup():
        import jax, jax.numpy as jnp
        import numpy as np
        B, S, D, H = (4, 256, 128, 16)
        DK = D // H
        MASK_VALUE = -1e+30
        key = jax.random.key(seed)
        ks = jax.random.split(key, 12)
        scale = 1.0 / np.sqrt(D)
        inp = {'q': jax.random.normal(ks[0], (B, S, D), jnp.float32), 'k': jax.random.normal(ks[1], (B, S, D), jnp.float32), 'v': jax.random.normal(ks[2], (B, S, D), jnp.float32), 'mask': jax.random.uniform(ks[3], (B, 1, 1, S)) < 0.1, 'Wq': jax.random.normal(ks[4], (D, D), jnp.float32) * scale, 'bq': jnp.zeros((D,), jnp.float32), 'Wk': jax.random.normal(ks[5], (D, D), jnp.float32) * scale, 'bk': jnp.zeros((D,), jnp.float32), 'Wv': jax.random.normal(ks[6], (D, D), jnp.float32) * scale, 'bv': jnp.zeros((D,), jnp.float32), 'Wc': jax.random.normal(ks[7], (D, D), jnp.float32) * scale, 'bc': jnp.zeros((D,), jnp.float32)}
        return inp
    _L1_xattn_all = _L1_xattn_setup()
    _L1_xattn_in = {k: v for k, v in _L1_xattn_all.items() if k in ('Wq', 'bq', 'Wk', 'bk', 'Wv', 'bv', 'Wc', 'bc')}
    del _L1_xattn_all

    def _L1_ffn_setup():
        import jax, jax.numpy as jnp
        import numpy as np
        EPS = 1e-05

        def rmsnorm(x):
            return x * jax.lax.rsqrt(jnp.mean(x * x, axis=-1, keepdims=True) + EPS)

        def act_quant(x):
            scale = 127.0 / jnp.clip(jnp.max(jnp.abs(x), axis=-1, keepdims=True), 1e-05)
            q = jnp.clip(jnp.round(x * scale), -128.0, 127.0) / scale
            return x + jax.lax.stop_gradient(q - x)

        def weight_quant(w):
            scale = 1.0 / jnp.clip(jnp.mean(jnp.abs(w)), 1e-05)
            q = jnp.clip(jnp.round(w * scale), -1.0, 1.0) / scale
            return w + jax.lax.stop_gradient(q - w)

        def bitlinear(x, w, b):
            xq = act_quant(rmsnorm(x))
            wq = weight_quant(w)
            return jnp.einsum('bsd,fd->bsf', xq, wq) + b
        key = jax.random.key(seed)
        k0, k1, k2 = jax.random.split(key, 3)
        B, S, D, F = (2, 1024, 128, 512)
        x = jax.random.normal(k0, (B, S, D), dtype=jnp.float32)
        w1 = jax.random.normal(k1, (F, D), dtype=jnp.float32) * (1.0 / np.sqrt(D))
        b1 = jnp.zeros((F,), dtype=jnp.float32)
        w2 = jax.random.normal(k2, (D, F), dtype=jnp.float32) * (1.0 / np.sqrt(F))
        b2 = jnp.zeros((D,), dtype=jnp.float32)
        return {'x': x, 'w1': w1, 'b1': b1, 'w2': w2, 'b2': b2}
    _L1_ffn_all = _L1_ffn_setup()
    _L1_ffn_in = {k: v for k, v in _L1_ffn_all.items() if k in ('w1', 'b1', 'w2', 'b2')}
    del _L1_ffn_all
    return {'x': x, 'ctx_1024': ctx_1024, 'mask_Bx1x1xS2_bk0': mask_Bx1x1xS2_bk0, 'L0_attn_Wq': _L0_attn_in['Wq'], 'L0_attn_bq': _L0_attn_in['bq'], 'L0_attn_Wk': _L0_attn_in['Wk'], 'L0_attn_bk': _L0_attn_in['bk'], 'L0_attn_Wv': _L0_attn_in['Wv'], 'L0_attn_bv': _L0_attn_in['bv'], 'L0_attn_Wc2q': _L0_attn_in['Wc2q'], 'L0_attn_bc2q': _L0_attn_in['bc2q'], 'L0_attn_Wo': _L0_attn_in['Wo'], 'L0_attn_bo': _L0_attn_in['bo'], 'L0_attn_g1': _L0_attn_in['g1'], 'L0_attn_beta1': _L0_attn_in['beta1'], 'L0_attn_g2': _L0_attn_in['g2'], 'L0_attn_beta2': _L0_attn_in['beta2'], 'L0_attn_W1': _L0_attn_in['W1'], 'L0_attn_b1': _L0_attn_in['b1'], 'L0_attn_Wm': _L0_attn_in['Wm'], 'L0_attn_bm': _L0_attn_in['bm'], 'L0_attn_Wqo': _L0_attn_in['Wqo'], 'L0_attn_bqo': _L0_attn_in['bqo'], 'L0_attn_W2': _L0_attn_in['W2'], 'L0_attn_b2': _L0_attn_in['b2'], 'L0_xattn_Wq': _L0_xattn_in['Wq'], 'L0_xattn_bq': _L0_xattn_in['bq'], 'L0_xattn_Wk': _L0_xattn_in['Wk'], 'L0_xattn_bk': _L0_xattn_in['bk'], 'L0_xattn_Wv': _L0_xattn_in['Wv'], 'L0_xattn_bv': _L0_xattn_in['bv'], 'L0_xattn_Wo': _L0_xattn_in['Wo'], 'L0_xattn_bo': _L0_xattn_in['bo'], 'L0_ffn_router_w': _L0_ffn_in['router_w'], 'L0_ffn_gate_w': _L0_ffn_in['gate_w'], 'L0_ffn_up_w': _L0_ffn_in['up_w'], 'L0_ffn_down_w': _L0_ffn_in['down_w'], 'L1_attn_wq_w': _L1_attn_in['wq_w'], 'L1_attn_wq_b': _L1_attn_in['wq_b'], 'L1_attn_wk_w': _L1_attn_in['wk_w'], 'L1_attn_wk_b': _L1_attn_in['wk_b'], 'L1_attn_wv_w': _L1_attn_in['wv_w'], 'L1_attn_wv_b': _L1_attn_in['wv_b'], 'L1_attn_wo_w': _L1_attn_in['wo_w'], 'L1_attn_wo_b': _L1_attn_in['wo_b'], 'L1_xattn_Wq': _L1_xattn_in['Wq'], 'L1_xattn_bq': _L1_xattn_in['bq'], 'L1_xattn_Wk': _L1_xattn_in['Wk'], 'L1_xattn_bk': _L1_xattn_in['bk'], 'L1_xattn_Wv': _L1_xattn_in['Wv'], 'L1_xattn_bv': _L1_xattn_in['bv'], 'L1_xattn_Wc': _L1_xattn_in['Wc'], 'L1_xattn_bc': _L1_xattn_in['bc'], 'L1_ffn_w1': _L1_ffn_in['w1'], 'L1_ffn_b1': _L1_ffn_in['b1'], 'L1_ffn_w2': _L1_ffn_in['w2'], 'L1_ffn_b2': _L1_ffn_in['b2']}

def reference(x, ctx_1024, mask_Bx1x1xS2_bk0, L0_attn_Wq, L0_attn_bq, L0_attn_Wk, L0_attn_bk, L0_attn_Wv, L0_attn_bv, L0_attn_Wc2q, L0_attn_bc2q, L0_attn_Wo, L0_attn_bo, L0_attn_g1, L0_attn_beta1, L0_attn_g2, L0_attn_beta2, L0_attn_W1, L0_attn_b1, L0_attn_Wm, L0_attn_bm, L0_attn_Wqo, L0_attn_bqo, L0_attn_W2, L0_attn_b2, L0_xattn_Wq, L0_xattn_bq, L0_xattn_Wk, L0_xattn_bk, L0_xattn_Wv, L0_xattn_bv, L0_xattn_Wo, L0_xattn_bo, L0_ffn_router_w, L0_ffn_gate_w, L0_ffn_up_w, L0_ffn_down_w, L1_attn_wq_w, L1_attn_wq_b, L1_attn_wk_w, L1_attn_wk_b, L1_attn_wv_w, L1_attn_wv_b, L1_attn_wo_w, L1_attn_wo_b, L1_xattn_Wq, L1_xattn_bq, L1_xattn_Wk, L1_xattn_bk, L1_xattn_Wv, L1_xattn_bv, L1_xattn_Wc, L1_xattn_bc, L1_ffn_w1, L1_ffn_b1, L1_ffn_w2, L1_ffn_b2):
    import jax
    import jax.numpy as jnp

    def _L0_attn_ref(x, Wq, bq, Wk, bk, Wv, bv, Wc2q, bc2q, Wo, bo, g1, beta1, g2, beta2, W1, b1, Wm, bm, Wqo, bqo, W2, b2):
        import jax, jax.numpy as jnp
        import numpy as np
        B, S, HID = (4, 128, 128)
        H = 8
        HD = HID // H
        NQ = 8
        RATIO = 0.5
        FF = 4 * HID
        EPS_COS = 1e-08
        LN_EPS = 1e-05

        def _layernorm(x, g, b):
            m = jnp.mean(x, axis=-1, keepdims=True)
            v = jnp.var(x, axis=-1, keepdims=True)
            return (x - m) * jax.lax.rsqrt(v + LN_EPS) * g + b
        Q = jnp.einsum('bsh,nhd->bnsd', x, Wq) + bq[None, :, None, :]
        K = jnp.einsum('bsh,nhd->bnsd', x, Wk) + bk[None, :, None, :]
        V = jnp.einsum('bsh,nhd->bnsd', x, Wv) + bv[None, :, None, :]
        qq = jnp.einsum('bnsd,ndq->bnsq', Q, Wc2q) + bc2q[None, :, None, :]
        kq = jnp.einsum('bnsd,ndq->bnsq', K, Wc2q) + bc2q[None, :, None, :]
        qn = jnp.linalg.norm(qq, axis=-1)
        kn = jnp.linalg.norm(kq, axis=-1)
        dots = jnp.einsum('bnsq,bntq->bnst', qq, kq)
        fid = dots / jnp.maximum(qn[..., :, None] * kn[..., None, :], EPS_COS)
        qw = fid * (1.0 + 0.1 * jnp.sin(fid * jnp.pi))
        cw = jnp.einsum('bnsd,bntd->bnst', Q, K) / np.sqrt(HD).astype(np.float32)
        aw = RATIO * qw + (1.0 - RATIO) * cw
        probs = jax.nn.softmax(aw, axis=-1)
        heads = jnp.einsum('bnst,bntd->bnsd', probs, V)
        attn = heads.transpose(0, 2, 1, 3).reshape(x.shape[0], x.shape[1], HID)
        attn = attn @ Wo + bo
        x1 = _layernorm(x + attn, g1, beta1)
        h = x1 @ W1 + b1
        qm = h @ Wm + bm
        qe = jnp.tanh(qm) * jnp.cos(qm * (jnp.pi / 4))
        ha = qe @ Wqo + bqo
        ff = ha @ W2 + b2
        out = _layernorm(x1 + ff, g2, beta2)
        return out

    def _L0_xattn_ref(query, key, value, Wq, bq, Wk, bk, Wv, bv, Wo, bo):
        import jax, jax.numpy as jnp
        import numpy as np
        D_MODEL = 128
        NUM_HEADS = 16
        HEAD_DIM = D_MODEL // NUM_HEADS
        B, S = (4, 256)

        def split_heads(x):
            b, s, _ = x.shape
            return x.reshape(b, s, NUM_HEADS, HEAD_DIM).transpose(0, 2, 1, 3)
        q = split_heads(query @ Wq + bq)
        k = split_heads(key @ Wk + bk)
        v = split_heads(value @ Wv + bv)
        scores = jnp.einsum('bhqd,bhkd->bhqk', q, k) / jnp.sqrt(jnp.float32(HEAD_DIM))
        weights = jax.nn.softmax(scores, axis=-1)
        attn = jnp.einsum('bhqk,bhkd->bhqd', weights, v)
        attn = attn.transpose(0, 2, 1, 3).reshape(query.shape[0], query.shape[1], D_MODEL)
        return attn @ Wo + bo

    def _L0_ffn_ref(hidden_states, router_w, gate_w, up_w, down_w):
        import jax, jax.numpy as jnp
        import numpy as np
        S, B, H, I, E = (64, 2, 128, 352, 8)
        router_logits = jnp.einsum('sbh,eh->sbe', hidden_states, router_w)
        routing_indices = jnp.argmax(router_logits, axis=-1)
        out = jnp.zeros_like(hidden_states)
        for e in range(E):
            mask = (routing_indices == e)[..., None]
            xe = jnp.where(mask, hidden_states, 0.0)
            g = jnp.einsum('sbh,ih->sbi', xe, gate_w[e])
            u = jnp.einsum('sbh,ih->sbi', xe, up_w[e])
            ye = jnp.einsum('sbi,hi->sbh', jax.nn.silu(g) * u, down_w[e])
            out = out + jnp.where(mask, ye, 0.0)
        return out

    def _L1_attn_ref(x, wq_w, wq_b, wk_w, wk_b, wv_w, wv_b, wo_w, wo_b):
        import jax, jax.numpy as jnp
        import numpy as np
        NUM_HEADS = 16
        PAD_ID = 0.0
        B, T, C = x.shape
        H = NUM_HEADS
        Dh = C // H
        scale = Dh ** (-0.5)
        q = (x @ wq_w.T + wq_b).reshape(B, T, H, Dh)
        k = (x @ wk_w.T + wk_b).reshape(B, T, H, Dh)
        v = (x @ wv_w.T + wv_b).reshape(B, T, H, Dh)
        scores = jnp.einsum('bthd,bshd->bhts', q, k) * scale
        key_mask = (x[:, :, 0] != PAD_ID)[:, None, None, :]
        scores = jnp.where(key_mask, scores, -jnp.inf)
        attn = jax.nn.softmax(scores, axis=-1)
        out = jnp.einsum('bhts,bshd->bthd', attn, v).reshape(B, T, C)
        return out @ wo_w.T + wo_b

    def _L1_xattn_ref(q, k, v, mask, Wq, bq, Wk, bk, Wv, bv, Wc, bc):
        import jax, jax.numpy as jnp
        import numpy as np
        B, S, D, H = (4, 256, 128, 16)
        DK = D // H
        MASK_VALUE = -1e+30
        b, sq, _ = q.shape
        sk = k.shape[1]
        qh = (q @ Wq.T + bq).reshape(b, sq, H, DK).transpose(0, 2, 1, 3)
        kh = (k @ Wk.T + bk).reshape(b, sk, H, DK).transpose(0, 2, 1, 3)
        vh = (v @ Wv.T + bv).reshape(b, sk, H, DK).transpose(0, 2, 1, 3)
        scores = jnp.einsum('bhqd,bhkd->bhqk', qh, kh) / jnp.sqrt(jnp.float32(DK))
        scores = jnp.where(mask, MASK_VALUE, scores)
        weights = jax.nn.softmax(scores, axis=-1)
        ctx = jnp.einsum('bhqk,bhkd->bhqd', weights, vh)
        ctx = ctx.transpose(0, 2, 1, 3).reshape(b, sq, D)
        return ctx @ Wc.T + bc

    def _L1_ffn_ref(x, w1, b1, w2, b2):
        import jax, jax.numpy as jnp
        import numpy as np
        EPS = 1e-05

        def rmsnorm(x):
            return x * jax.lax.rsqrt(jnp.mean(x * x, axis=-1, keepdims=True) + EPS)

        def act_quant(x):
            scale = 127.0 / jnp.clip(jnp.max(jnp.abs(x), axis=-1, keepdims=True), 1e-05)
            q = jnp.clip(jnp.round(x * scale), -128.0, 127.0) / scale
            return x + jax.lax.stop_gradient(q - x)

        def weight_quant(w):
            scale = 1.0 / jnp.clip(jnp.mean(jnp.abs(w)), 1e-05)
            q = jnp.clip(jnp.round(w * scale), -1.0, 1.0) / scale
            return w + jax.lax.stop_gradient(q - w)

        def bitlinear(x, w, b):
            xq = act_quant(rmsnorm(x))
            wq = weight_quant(w)
            return jnp.einsum('bsd,fd->bsf', xq, wq) + b
        h = bitlinear(x, w1, b1)
        h = jax.nn.gelu(h, approximate=False)
        return bitlinear(h, w2, b2)
    x = x + _L0_attn_ref(_layernorm(x, axis=-1), L0_attn_Wq, L0_attn_bq, L0_attn_Wk, L0_attn_bk, L0_attn_Wv, L0_attn_bv, L0_attn_Wc2q, L0_attn_bc2q, L0_attn_Wo, L0_attn_bo, L0_attn_g1, L0_attn_beta1, L0_attn_g2, L0_attn_beta2, L0_attn_W1, L0_attn_b1, L0_attn_Wm, L0_attn_bm, L0_attn_Wqo, L0_attn_bqo, L0_attn_W2, L0_attn_b2)
    x = x + _L0_xattn_ref(_layernorm(x, axis=-1), ctx_1024, ctx_1024, L0_xattn_Wq, L0_xattn_bq, L0_xattn_Wk, L0_xattn_bk, L0_xattn_Wv, L0_xattn_bv, L0_xattn_Wo, L0_xattn_bo)
    x = x + _L0_ffn_ref(_layernorm(x, axis=-1), L0_ffn_router_w, L0_ffn_gate_w, L0_ffn_up_w, L0_ffn_down_w)
    x = x + _L1_attn_ref(_layernorm(x, axis=-1), L1_attn_wq_w, L1_attn_wq_b, L1_attn_wk_w, L1_attn_wk_b, L1_attn_wv_w, L1_attn_wv_b, L1_attn_wo_w, L1_attn_wo_b)
    x = x + _L1_xattn_ref(_layernorm(x, axis=-1), ctx_1024, ctx_1024, mask_Bx1x1xS2_bk0, L1_xattn_Wq, L1_xattn_bq, L1_xattn_Wk, L1_xattn_bk, L1_xattn_Wv, L1_xattn_bv, L1_xattn_Wc, L1_xattn_bc)
    x = x + _L1_ffn_ref(_layernorm(x, axis=-1), L1_ffn_w1, L1_ffn_b1, L1_ffn_w2, L1_ffn_b2)
    return x

_drawn_inputs = setup_inputs


def setup_inputs(seed=0):
    import zlib

    import numpy as np

    out = dict(_drawn_inputs(seed))
    spreads = {'L0_attn_bq': (0.0, 0.8),
     'L0_attn_bk': (0.0, 0.8),
     'L0_attn_bv': (0.0, 0.706),
     'L0_attn_bc2q': (0.0, 0.8),
     'L0_attn_bo': (0.0, 0.1),
     'L0_attn_g1': (1.0, 0.2),
     'L0_attn_beta1': (0.0, 0.1),
     'L0_attn_g2': (1.0, 0.2),
     'L0_attn_beta2': (0.0, 0.1),
     'L0_attn_b1': (0.0, 0.8),
     'L0_attn_bm': (0.0, 0.8),
     'L0_attn_bqo': (0.0, 0.356),
     'L0_attn_b2': (0.0, 0.1),
     'L0_xattn_bq': (0.0, 0.598),
     'L0_xattn_bk': (0.0, 2.0),
     'L0_xattn_bv': (0.0, 0.1),
     'L0_xattn_bo': (0.0, 0.1),
     'L1_xattn_bq': (0.0, 2.0),
     'L1_xattn_bk': (0.0, 2.0),
     'L1_xattn_bv': (0.0, 0.566),
     'L1_xattn_bc': (0.0, 0.584),
     'L1_ffn_b1': (0.0, 0.512),
     'L1_ffn_b2': (0.0, 0.505)}
    factors = {'L0_attn_Wq': 8.0,
     'L0_attn_Wk': 8.0,
     'L0_attn_Wv': 8.0,
     'L0_attn_Wc2q': 8.0,
     'L0_attn_Wo': 5.401,
     'L0_attn_W1': 8.0,
     'L0_attn_Wm': 8.0,
     'L0_attn_Wqo': 8.0,
     'L0_attn_W2': 2.773,
     'L0_ffn_router_w': 8.0,
     'L0_ffn_gate_w': 8.0,
     'L0_ffn_up_w': 8.0,
     'L0_ffn_down_w': 8.0,
     'L1_attn_wq_b': 2.771,
     'L1_attn_wk_b': 64.0}
    for name, (base, spread) in spreads.items():
        noise = np.random.default_rng([zlib.crc32(name.encode()), seed]).standard_normal(out[name].shape)
        drawn = base * np.exp(spread * noise) if base else spread * noise
        out[name] = jnp.asarray(drawn.astype(out[name].dtype))
    for name, factor in factors.items():
        out[name] = (out[name] * factor).astype(out[name].dtype)
    return out
```

```python
import math
from contextlib import ExitStack

import numpy as np

import concourse.bass as bass
from concourse import mybir

F32 = mybir.dt.float32
BF16 = mybir.dt.bfloat16
ALU = mybir.AluOpType
ACT = mybir.ActivationFunctionType
AX = mybir.AxisListType

P = 128
D = 128
S = 128
GB = 4
T = GB * S
LN_EPS = 1e-5
H16, HD8 = 16, 8
TERMS = 6
ROWS = HD8 * TERMS
HALF = 64
MASKED = -(2.0 ** 100)


def counted(value):
    return not isinstance(value, int) or value > 0


def groups_loop(eng, n_groups, iteration, after=0):
    first = 3 if after else 2
    for g in range(-2, first):
        iteration(g, g % 3)
    rounds = max(0, (n_groups - 2 - first) // 3)
    if rounds > 1:
        with eng.Fori(0, rounds) as r:
            for j in range(3):
                iteration(3 * r + (first + j), (first + j) % 3)
    else:
        for g in range(first, first + 3 * rounds):
            iteration(g, g % 3)
    for g in range(first + 3 * rounds, n_groups + after):
        iteration(g, g % 3)


def does(g, ahead, n_groups):
    return not isinstance(g, int) or 0 <= g + ahead < n_groups


def plain_attention(nc, env, name, n_groups, cross, w, mask):
    x, ident, QST, KST = env["x"], env["ident"], env["QST"], env["KST"]
    TK = 77 if cross else S
    NK = GB * TK
    chunks = [(0, 6), (6, 12), (12, 16)] if cross else [(0, 4), (4, 8), (8, 12), (12, 16)]
    NCH = len(chunks)
    PAIRS = H16 // 2
    ctx = ExitStack()
    with ctx:
        def sb(n, shape, dt=F32):
            return ctx.enter_context(nc.sbuf_tensor(f"{name}_{n}", shape, dt))

        def ps(n, shape):
            return ctx.enter_context(nc.psum_tensor(f"{name}_{n}", shape, F32))

        def sem(n):
            return nc.alloc_semaphore(f"{name}_{n}")

        wq, wk, wv, wo = (sb(n, [D, D]) for n in ("wq", "wk", "wv", "wo"))
        bq, bk = sb("bq", [D, 1]), sb("bk", [D, 1])
        bqs = sb("bqs", [D, 1])
        bv, bo = sb("bv", [P, D]), sb("bo", [P, D])
        stat6 = sb("stat6", [P, GB, 6])
        mv = sb("mv", [P, GB, 2])
        vare = sb("vare", [P, GB])
        minus_half = sb("minus_half", [P, GB])
        eps = sb("eps", [P, GB])
        rstd = sb("rstd", [P, GB])
        xn = sb("xn", [P, GB, D])
        xnT = sb("xnT", [D, T])
        qf, kf = sb("qf", [D, T]), sb("kf", [D, NK])
        r1q, r1k = sb("r1q", [D, T]), sb("r1k", [D, NK])
        q3, k3 = sb("q3", [D, 3, T], BF16), sb("k3", [D, 3, NK], BF16)
        V9 = sb("V9", [P, 3, GB, H16, HD8 + 1])
        negm = sb("negm", [P, 2, H16, GB])
        mT = sb("mT", [GB * H16, 2, S], BF16)
        PR = sb("PR", [P, GB, H16, S])
        rs = sb("rs", [P, 2, H16])
        On = sb("On", [P, GB, H16, HD8])
        oT = sb("oT", [D, T])
        zero2 = sb("zero2", [2, T], BF16)
        mrow = sb("mrow", [1, T], BF16) if mask == "zero_key" else None
        if cross:
            cx = sb("cx", [TK, GB, D])
            cT = sb("cT", [D, NK])
        if mask == "given":
            mask_u8 = sb("mask_u8", [1, n_groups * NK], mybir.dt.uint8)
            mask_bf = sb("mask_bf", [1, n_groups * NK], BF16)

        s1 = [ps(f"s1{i}", [P, 512]) for i in range(2)]
        s2 = [ps(f"s2{i}", [P, 8, S]) for i in range(2)]
        mA, mB = ps("mA", [P, 512]), ps("mB", [P, 512])

        Dq = nc.dram_tensor(f"{name}_Dq", [D, TERMS, T], BF16, kind="Internal").ap()
        Dk = nc.dram_tensor(f"{name}_Dk", [D, TERMS, NK], BF16, kind="Internal").ap()
        Dm = nc.dram_tensor(f"{name}_Dm", [H16, 2, GB, S], BF16, kind="Internal").ap()
        Dq_rows = Dq.rearrange("(g p i) r n -> p (i r) g n", p=2, i=HD8)
        Dk_rows = Dk.rearrange("(g p i) r n -> p (i r) g n", p=2, i=HD8)
        Dm_rows = Dm.rearrange("(g p) j b s -> p j g (b s)", p=2)

        weights_in = sem("weights_in")
        sp_waits_met = sem("sp_waits_met")
        pool_set = sem("pool_set")
        setup = sem("setup")
        ones_in = sem("ones_in")
        ctx_in = sem("ctx_in")
        bn_done, stats, var_ready, rstd_ready, xn_ready = (sem(n) for n in ("bn_done", "stats", "var_ready", "rstd_ready", "xn_ready"))
        xnT_ps, xnT_sb, cT_ps, cT_sb = (sem(n) for n in ("xnT_ps", "xnT_sb", "cT_ps", "cT_sb"))
        q_ps, q_sb, k_ps, k_sb, v_ps, v_sb = (sem(n) for n in ("q_ps", "q_sb", "k_ps", "k_sb", "v_ps", "v_sb"))
        q_split, k_split, q_written, k_written, q_stacked, k_stacked = (sem(n) for n in ("q_split", "k_split", "q_written", "k_written", "q_stacked", "k_stacked"))
        mask_row = sem("mask_row")
        s1_ps, s1_max = sem("s1_ps"), sem("s1_max")
        m_ps, m_sb, m_written, m_stacked = (sem(n) for n in ("m_ps", "m_sb", "m_written", "m_stacked"))
        s2_ps, p_sb = sem("s2_ps"), sem("p_sb")
        o_ps, o_rs, o_sb, oT_ps, oT_sb, y_ps, x_biased, x_out = (sem(n) for n in ("o_ps", "o_rs", "o_sb", "oT_ps", "oT_sb", "y_ps", "x_biased", "x_out"))

        N_WEIGHTS = 8
        N_SETUP = 5 if mask == "given" else 4
        Q_READS = 4
        K_READS = 4 if mask else 2

        with nc.Block() as block:

            @block.sync
            def _(sp):
                for dst, src in ((wq, w["wq"]), (wk, w["wk"]), (wv, w["wv"]), (wo, w["wo"]), (bq, w["bq"]), (bk, w["bk"])):
                    sp.dma_start(dst[:, :], src).then_inc(weights_in, 16)
                for dst, src in ((bv, w["bv"]), (bo, w["bo"])):
                    sp.dma_start(dst[:, :], src.broadcast_to([P, D])).then_inc(weights_in, 16)
                if mask == "given":
                    sp.dma_start(mask_u8[:, :], w["mask"]).then_inc(ones_in, 16)

                def iteration(g, k):
                    a, ka, kb = g + 2, (k + 2) % 3, (k + 1) % 3
                    if does(g, 2, n_groups):
                        sp.wait_ge(q_split, 3 * a + 3)
                        sp.sem_inc(sp_waits_met, 1)
                        sp.dma_start(Dq[:, 0:3, :], q3[:, 0:1, :].broadcast_to([D, 3, T])).then_inc(q_written, 16)
                        sp.dma_start(Dq[:, 3:5, :], q3[:, 1:2, :].broadcast_to([D, 2, T])).then_inc(q_written, 16)
                        sp.dma_start(Dq[:, 5:6, :], q3[:, 2:3, :]).then_inc(q_written, 16)
                    if does(g, 1, n_groups):
                        sp.wait_ge(m_sb, 2 * (g + 1) + 2)
                        sp.sem_inc(sp_waits_met, 1)
                        for j in range(2):
                            sp.dma_start(Dm[:, j, :, :], mT[:, j, :]).then_inc(m_written, 16)
                    if does(g, 2, n_groups):
                        if counted(8 * g):
                            sp.wait_ge(s2_ps, 8 * g)
                            sp.sem_inc(sp_waits_met, 1)
                        if counted(16 * Q_READS * a):
                            sp.wait_ge(q_stacked, 16 * Q_READS * a)
                            sp.sem_inc(sp_waits_met, 1)
                        sp.wait_ge(q_written, 48 * a + 48)
                        sp.sem_inc(sp_waits_met, 1)
                        for p in range(2):
                            r = HALF * p
                            sp.dma_start(QST[r:r + ROWS, ka, p::2, :], Dq_rows[p]).then_inc(q_stacked, 16)
                            sp.dma_start(QST[r + ROWS:r + ROWS + 2, ka, p::2, :],
                                         zero2[:, :].unsqueeze(1).broadcast_to([2, PAIRS, T])).then_inc(q_stacked, 16)
                    if does(g, 1, n_groups):
                        if counted(32 * (g + 1)):
                            sp.wait_ge(m_stacked, 32 * (g + 1))
                            sp.sem_inc(sp_waits_met, 1)
                        sp.wait_ge(m_written, 32 * (g + 1) + 32)
                        sp.sem_inc(sp_waits_met, 1)
                        for p in range(2):
                            r = HALF * p + ROWS
                            sp.dma_start(QST[r:r + 2, kb, p::2, :], Dm_rows[p]).then_inc(m_stacked, 16)
                    if does(g, 2, n_groups):
                        sp.wait_ge(k_split, 3 * a + 3)
                        sp.sem_inc(sp_waits_met, 1)
                        sp.dma_start(Dk[:, 0:3, :], k3[:, 0:3, :]).then_inc(k_written, 16)
                        sp.dma_start(Dk[:, 3:5, :], k3[:, 0:2, :]).then_inc(k_written, 16)
                        sp.dma_start(Dk[:, 5:6, :], k3[:, 0:1, :]).then_inc(k_written, 16)
                        if mask == "zero_key":
                            sp.wait_ge(mask_row, a + 1)
                            sp.sem_inc(sp_waits_met, 1)
                        if counted(16 * K_READS * a):
                            sp.wait_ge(k_stacked, 16 * K_READS * a)
                            sp.sem_inc(sp_waits_met, 1)
                        sp.wait_ge(k_written, 48 * a + 48)
                        sp.sem_inc(sp_waits_met, 1)
                        for p in range(2):
                            r = HALF * p
                            sp.dma_start(KST[r:r + ROWS, ka, :, 0:NK], Dk_rows[p]).then_inc(k_stacked, 16)
                            if mask:
                                src = mrow[:, :] if mask == "zero_key" else mask_bf[:, bass.ds(NK * a, NK)]
                                sp.dma_start(KST[r + ROWS + 2:r + ROWS + 3, ka, :, 0:NK],
                                             src.unsqueeze(1).broadcast_to([1, PAIRS, NK])).then_inc(k_stacked, 16)
    
                sp.wait_ge(setup, N_SETUP)
                groups_loop(sp, n_groups, iteration)

            @block.gpsimd
            def _(pool):
                nc.gpsimd.memset(minus_half[:, :], -0.5).then_inc(pool_set, 1)
                nc.gpsimd.memset(eps[:, :], LN_EPS).then_inc(pool_set, 1)
                nc.gpsimd.memset(zero2[:, :], 0.0).then_inc(setup, 1)
                pool.wait_ge(pool_set, 2)
                if mask == "given":
                    pool.wait_ge(ones_in, 16)
                    nc.gpsimd.tensor_scalar(mask_bf[:, :], mask_u8[:, :], MASKED, 0.0, ALU.mult, ALU.add).then_inc(setup, 1)
                pool.wait_ge(weights_in, 16 * N_WEIGHTS)
                def split(first, full, rest, parts, done, g):
                    pool.wait_ge(first, 2 * g + 2)
                    nc.gpsimd.tensor_tensor(rest[:, :], full[:, :], parts[:, 0, :], ALU.subtract).then_inc(done, 1)
                    nc.gpsimd.tensor_tensor(parts[:, 1, :], full[:, :], parts[:, 0, :], ALU.subtract).then_inc(done, 1)
                    pool.wait_ge(done, 3 * g + 2)
                    nc.gpsimd.tensor_tensor(parts[:, 2, :], rest[:, :], parts[:, 1, :], ALU.subtract).then_inc(done, 1)

                def iteration(g, k):
                    a = g + 2
                    if does(g, 2, n_groups):
                        if cross:
                            if counted(a):
                                pool.wait_ge(cT_ps, a)
                            pool.dma_start(cx[:, :, :], w["context"][bass.ds(GB * a, GB), :, :].rearrange("b t c -> t b c")).then_inc(ctx_in, 16)
                        pool.wait_ge(stats, a + 1)
                        nc.gpsimd.tensor_tensor(vare[:, :], mv[:, :, 1], eps[:, :], ALU.add).then_inc(var_ready, 1)
                        pool.wait_ge(var_ready, a + 1)
                        nc.gpsimd.tensor_tensor(rstd[:, :], vare[:, :], minus_half[:, :], ALU.pow).then_inc(rstd_ready, 1)
                    if does(g, 0, n_groups):
                        pool.wait_ge(xn_ready, g + 1)
                        xg = x[:, bass.ds(GB * g, GB), :]
                        nc.gpsimd.tensor_tensor(xg, xg, bo[:, :].unsqueeze(1).broadcast_to([P, GB, D]), ALU.add).then_inc(x_biased, 1)
                    if does(g, 2, n_groups):
                        split(q_sb, qf, r1q, q3, q_split, a)
                        split(k_sb, kf, r1k, k3, k_split, a)

                groups_loop(pool, n_groups, iteration)

            @block.scalar
            def _(act):
                act.wait_ge(weights_in, 16 * N_WEIGHTS)
                scale = 1.0 / math.sqrt(HD8)
                nc.scalar.activation(bqs[:, :], bq[:, :], ACT.Copy, scale=scale).then_inc(setup, 1)
                act.wait_ge(setup, N_SETUP)

                def exps(g, b):
                    for h in range(2):
                        n = 8 * g + 2 * b + h
                        act.wait_ge(s2_ps, n + 1)
                        if h == 0 and b % 2 == 0:
                            if counted(2 * g - 1 + b // 2):
                                act.wait_ge(o_ps, 2 * g - 1 + b // 2)
                        nc.scalar.activation(PR[0:TK, b, 8 * h:8 * h + 8, :], s2[h][0:TK, :, :], ACT.Exp).then_inc(p_sb, 1)

                def iteration(g, k):
                    a = g + 2
                    A, C = does(g, 2, n_groups), does(g, 0, n_groups)
                    if C:
                        exps(g, 0)
                    if A:
                        act.wait_ge(xnT_ps, a + 1)
                        if counted(a):
                            act.wait_ge(v_ps if not cross else q_ps, a)
                        nc.scalar.activation(xnT[:, :], mA[:, :], ACT.Copy).then_inc(xnT_sb, 1)
                        if cross:
                            act.wait_ge(cT_ps, a + 1)
                            if counted(a):
                                act.wait_ge(v_ps, a)
                            nc.scalar.activation(cT[:, :], mB[:, 0:NK], ACT.Copy).then_inc(cT_sb, 1)
                        act.wait_ge(q_ps, a + 1)
                        if counted(3 * a):
                            act.wait_ge(q_split, 3 * a)
                        if counted(48 * a):
                            act.wait_ge(q_written, 48 * a)
                        nc.scalar.activation(q3[:, 0, :], mA[:, :], ACT.Identity, bias=bqs[:, 0:1], scale=scale).then_inc(q_sb, 1)
                        nc.scalar.activation(qf[:, :], mA[:, :], ACT.Identity, bias=bqs[:, 0:1], scale=scale).then_inc(q_sb, 1)
                    if C:
                        exps(g, 1)
                    if A:
                        act.wait_ge(k_ps, a + 1)
                        if counted(3 * a):
                            act.wait_ge(k_split, 3 * a)
                        if counted(48 * a):
                            act.wait_ge(k_written, 48 * a)
                        nc.scalar.activation(k3[:, 0, :], mB[:, 0:NK], ACT.Identity, bias=bk[:, 0:1], scale=1.0).then_inc(k_sb, 1)
                        nc.scalar.activation(kf[:, :], mB[:, 0:NK], ACT.Identity, bias=bk[:, 0:1], scale=1.0).then_inc(k_sb, 1)
                    if C:
                        exps(g, 2)
                        exps(g, 3)
                        act.wait_ge(oT_ps, g + 1)
                        if counted(g):
                            act.wait_ge(y_ps, g)
                        nc.scalar.activation(oT[:, :], mA[:, :], ACT.Copy).then_inc(oT_sb, 1)

                groups_loop(act, n_groups, iteration)

            @block.vector
            def _(dve):
                nc.vector.memset(negm[:, 1, :, :], 0.0).then_inc(setup, 1)
                nc.vector.memset(V9[:, :, :, :, HD8:HD8 + 1], 1.0).then_inc(setup, 1)
                dve.wait_ge(weights_in, 16 * N_WEIGHTS)

                def maxima(g, b):
                    for c, (h0, h1) in enumerate(chunks):
                        n = NCH * (GB * g + b) + c
                        dve.wait_ge(s1_ps, n + 1)
                        if b == 0 and c == 0:
                            if counted(g):
                                dve.wait_ge(m_ps, g)
                        nc.vector.tensor_reduce(negm[:, 0, h0:h1, b],
                                                s1[(NCH * b + c) % 2][:, 0:(h1 - h0) * TK].rearrange("p (h t) -> p h t", t=TK),
                                                axis=AX.X, op=ALU.max, negate=True).then_inc(s1_max, 1)

                def heads_out(g, j):
                    bank = (mA if j == 0 else mB)[:, 0:2 * H16 * (HD8 + 1)].rearrange("p (b h e) -> p b h e", b=2, h=H16)
                    n = 2 * g + j
                    dve.wait_ge(o_ps, n + 1)
                    if counted(g):
                        dve.wait_ge(oT_ps, g)
                    if counted(n):
                        dve.wait_ge(o_sb, n)
                    nc.vector.reciprocal(rs[:, :, :], bank[:, :, :, HD8]).then_inc(o_rs, 1)
                    dve.wait_ge(o_rs, n + 1)
                    nc.vector.tensor_tensor(On[:, 2 * j:2 * j + 2, :, :].rearrange("p b h e -> p (b h) e"),
                                            bank[:, :, :, 0:HD8].rearrange("p b h e -> p (b h) e"),
                                            rs[:, :, :].rearrange("p b h -> p (b h)").unsqueeze(2).broadcast_to([P, 2 * H16, HD8]),
                                            ALU.mult).then_inc(o_sb, 1)

                def iteration(g, k):
                    a, ka = g + 2, (k + 2) % 3
                    A, B, C = does(g, 2, n_groups), does(g, 1, n_groups), does(g, 0, n_groups)
                    if A:
                        for b in range(GB):
                            last = nc.vector.bn_stats(stat6[:, b, :], x[:, bass.ds(GB * a + b, 1), :].rearrange("p o c -> p (o c)"))
                        last.then_inc(bn_done, 1)
                        dve.wait_ge(bn_done, a + 1)
                        if counted(a):
                            dve.wait_ge(rstd_ready, a)
                    if B:
                        maxima(g + 1, 0)
                    if A:
                        for b in range(GB):
                            last = nc.vector.bn_aggr(mv[:, b, :], stat6[:, b, :])
                        last.then_inc(stats, 1)
                    if B:
                        maxima(g + 1, 1)
                    if A:
                        dve.wait_ge(rstd_ready, a + 1)
                        if counted(a):
                            dve.wait_ge(xnT_ps, a)
                        for b in range(GB):
                            last = nc.vector.tensor_scalar(xn[:, b, :], x[:, bass.ds(GB * a + b, 1), :].rearrange("p o c -> p (o c)"),
                                                           mv[:, b, 0:1], rstd[:, b:b + 1], ALU.subtract, ALU.mult)
                        last.then_inc(xn_ready, 1)
                    if A and mask == "zero_key":
                        dve.wait_ge(xnT_sb, a + 1)
                        if counted(16 * K_READS * a):
                            dve.wait_ge(k_stacked, 16 * K_READS * a)
                        nc.vector.tensor_scalar(mrow[:, :], xnT[0:1, :], 0.0, MASKED, ALU.is_equal, ALU.mult).then_inc(mask_row, 1)
                    if B:
                        maxima(g + 1, 2)
                        maxima(g + 1, 3)
                        dve.wait_ge(m_ps, g + 2)
                        if counted(32 * (g + 1)):
                            dve.wait_ge(m_written, 32 * (g + 1))
                        nc.vector.tensor_copy(mT[:, 0, :], mA[0:GB * H16, 0:S]).then_inc(m_sb, 1)
                        dve.wait_ge(m_sb, 2 * (g + 1) + 1)
                        nc.vector.tensor_tensor(mT[:, 1, :], mA[0:GB * H16, 0:S], mT[:, 0, :], ALU.subtract).then_inc(m_sb, 1)
                    if C:
                        heads_out(g, 0)
                    if A:
                        dve.wait_ge(v_ps, a + 1)
                        nc.vector.tensor_tensor(V9[0:TK, ka, :, :, 0:HD8],
                                                mB[0:TK, :].rearrange("p (b h e) -> p b h e", b=GB, h=H16),
                                                bv[0:TK, :].rearrange("p (h e) -> p h e", h=H16).unsqueeze(1).broadcast_to([TK, GB, H16, HD8]),
                                                ALU.add).then_inc(v_sb, 1)
                    if C:
                        heads_out(g, 1)
                        dve.wait_ge(y_ps, g + 1)
                        dve.wait_ge(x_biased, g + 1)
                        xg = x[:, bass.ds(GB * g, GB), :]
                        nc.vector.tensor_tensor(xg, mB[:, :].rearrange("p (b c) -> p b c", b=GB), xg, ALU.add).then_inc(x_out, 1)

                groups_loop(dve, n_groups, iteration)
                dve.wait_ge(x_out, n_groups)

            @block.tensor
            def _(pe):
                pe.wait_ge(weights_in, 16 * N_WEIGHTS)
                pe.wait_ge(setup, N_SETUP)

                def scores_rows(g, k, b):
                    if b == 0:
                        if counted(16 * Q_READS * (g + 1)):
                            pe.wait_ge(q_stacked, 16 * Q_READS * (g + 1))
                        if counted(16 * K_READS * (g + 1)):
                            pe.wait_ge(k_stacked, 16 * K_READS * (g + 1))
                    for c, (h0, h1) in enumerate(chunks):
                        n = NCH * (GB * g + b) + c
                        if counted(n - 1):
                            pe.wait_ge(s1_max, n - 1)
                        for h in range(h0, h1):
                            last = nc.tensor.matmul(s1[(NCH * b + c) % 2][:, (h - h0) * TK:(h - h0 + 1) * TK],
                                                    QST[:, k, h, b * S:(b + 1) * S], KST[:, k, h // 2, b * TK:(b + 1) * TK],
                                                    start=True, stop=True)
                        last.then_inc(s1_ps, 1)

                def scores_keys(g, k, b):
                    if b == 0:
                        if counted(32 * (g + 1)):
                            pe.wait_ge(m_stacked, 32 * (g + 1))
                    for h in range(2):
                        n = 8 * g + 2 * b + h
                        if counted(n - 1):
                            pe.wait_ge(p_sb, n - 1)
                        for j in range(4):
                            pair = 4 * h + j
                            last = nc.tensor.matmul(s2[h][0:TK, 2 * j:2 * j + 2, :], KST[:, k, pair, b * TK:(b + 1) * TK],
                                                    QST[:, k, 2 * pair:2 * pair + 2, b * S:(b + 1) * S], start=True, stop=True)
                        last.then_inc(s2_ps, 1)

                def values(g, k, j):
                    bank = (mA if j == 0 else mB)[:, 0:2 * H16 * (HD8 + 1)].rearrange("p (b h e) -> p b h e", b=2, h=H16)
                    pe.wait_ge(v_sb, g + 1)
                    for b in range(2):
                        bb = 2 * j + b
                        pe.wait_ge(p_sb, 8 * g + 2 * bb + 2)
                        for h in range(H16):
                            last = nc.tensor.matmul(bank[:, b, h, :], PR[0:TK, bb, h, :], V9[0:TK, k, bb, h, :], start=True, stop=True)
                    last.then_inc(o_ps, 1)

                def iteration(g, k):
                    a, ka, kb = g + 2, (k + 2) % 3, (k + 1) % 3
                    A, B, C = does(g, 2, n_groups), does(g, 1, n_groups), does(g, 0, n_groups)
                    if B:
                        scores_rows(g + 1, kb, 0)
                    if C:
                        scores_keys(g, k, 0)
                    if B:
                        scores_rows(g + 1, kb, 1)
                    if A:
                        pe.wait_ge(xn_ready, a + 1)
                        if counted(g):
                            pe.wait_ge(oT_sb, g)
                        if isinstance(g, int) and g < 1:
                            if counted(2 * a):
                                pe.wait_ge(q_sb, 2 * a)
                            if counted(2 * (g + 1)):
                                pe.wait_ge(m_sb, 2 * (g + 1))
                        for b in range(GB):
                            last = nc.tensor.transpose(mA[:, b * S:(b + 1) * S], xn[:, b, :], ident[:, :])
                        last.then_inc(xnT_ps, 1)
                        if cross:
                            pe.wait_ge(ctx_in, 16 * (a + 1))
                            if counted(g):
                                pe.wait_ge(x_out, g)
                            if isinstance(g, int) and g < 1:
                                if counted(a):
                                    pe.wait_ge(v_sb, a)
                            for b in range(GB):
                                last = nc.tensor.transpose(mB[:, b * TK:(b + 1) * TK], cx[:, b, :], ident[0:TK, 0:TK])
                            last.then_inc(cT_ps, 1)
                    if A:
                        pe.wait_ge(xnT_sb, a + 1)
                        nc.tensor.matmul(mA[:, :], wq[:, :], xnT[:, :], start=True, stop=True).then_inc(q_ps, 1)
                    if B:
                        scores_rows(g + 1, kb, 2)
                    if C:
                        scores_keys(g, k, 1)
                    if A:
                        if cross:
                            pe.wait_ge(cT_sb, a + 1)
                        else:
                            if counted(g):
                                pe.wait_ge(x_out, g)
                            if isinstance(g, int) and g < 1:
                                if counted(a):
                                    pe.wait_ge(v_sb, a)
                        nc.tensor.matmul(mB[:, 0:NK], wk[:, :], (cT if cross else xnT)[:, :], start=True, stop=True).then_inc(k_ps, 1)
                    if B:
                        scores_rows(g + 1, kb, 3)
                        if A:
                            pe.wait_ge(q_sb, 2 * a + 2)
                        if counted(NCH * GB * (g + 2)):
                            pe.wait_ge(s1_max, NCH * GB * (g + 2))
                        nc.tensor.transpose(mA[:, 0:S], negm[:, :, :, :].rearrange("p r h b -> p (r h b)"), ident[:, :]).then_inc(m_ps, 1)
                    if C:
                        if B:
                            pe.wait_ge(m_sb, 2 * (g + 1) + 2)
                        else:
                            if counted(g):
                                pe.wait_ge(oT_sb, g)
                        values(g, k, 0)
                        scores_keys(g, k, 2)
                    if A:
                        pe.wait_ge(k_sb, 2 * a + 2)
                        src = cT if cross else xnT
                        for b in range(GB):
                            last = nc.tensor.matmul(mB[0:TK, b * D:(b + 1) * D], src[:, b * TK:(b + 1) * TK], wv[:, :], start=True, stop=True)
                        last.then_inc(v_ps, 1)
                    if C:
                        scores_keys(g, k, 3)
                        if A:
                            pe.wait_ge(v_sb, a + 1)
                        else:
                            if counted(g):
                                pe.wait_ge(x_out, g)
                        values(g, k, 1)
                        pe.wait_ge(o_sb, 2 * g + 2)
                        for b in range(GB):
                            last = nc.tensor.transpose(mA[:, b * S:(b + 1) * S], On[:, b, :, :].rearrange("p h e -> p (h e)"), ident[:, :])
                        last.then_inc(oT_ps, 1)
                        pe.wait_ge(oT_sb, g + 1)
                        for b in range(GB):
                            last = nc.tensor.matmul(mB[:, b * D:(b + 1) * D], oT[:, b * S:(b + 1) * S], wo[:, :], start=True, stop=True)
                        last.then_inc(y_ps, 1)

                groups_loop(pe, n_groups, iteration)


MAGIC = 1.5 * 2.0 ** 23
FF = 512
FCH = FF // P
QMAX = 127.0
CLIP = 1e-5


def ternary_ffn(nc, env, n_groups, w):
    x, ident = env["x"], env["ident"]
    ctx = ExitStack()
    with ctx:
        def sb(n, shape, dt=F32):
            return ctx.enter_context(nc.sbuf_tensor(f"ffn_{n}", shape, dt))

        def ps(n, shape, dt=F32):
            return ctx.enter_context(nc.psum_tensor(f"ffn_{n}", shape, dt))

        def sem(n):
            return nc.alloc_semaphore(f"ffn_{n}")

        w1f, w2f = sb("w1f", [D, FF]), sb("w2f", [P, FCH, D])
        w1r, w2r = sb("w1r", [D, FF]), sb("w2r", [P, FCH * D])
        w1i, w2i = sb("w1i", [D, FF], BF16), sb("w2i", [P, FCH, D], BF16)
        b1, b2 = sb("b1", [P, FF]), sb("b2", [P, D])
        ones = sb("ones", [P, P])
        identb = sb("identb", [P, P], BF16)
        wabs = sb("wabs", [P, 2])
        wmean = sb("wmean", [P, 2])
        winv = sb("winv", [P, 2])
        stat6 = sb("stat6", [P, GB, 6])
        mv = sb("mv", [P, GB, 2])
        vare, rstd = sb("vare", [P, GB]), sb("rstd", [P, GB])
        minus_half, eps, inv_ff = sb("minus_half", [P, GB]), sb("eps", [P, GB]), sb("inv_ff", [P, GB])
        xn = sb("xn", [P, GB, D])
        m1, q1s, r1, a1, i1, f1 = (sb(n, [P, GB]) for n in ("m1", "q1s", "r1", "a1", "i1", "f1"))
        m2, q2s, q2m, r2, a2, i2, f2 = (sb(n, [P, GB]) for n in ("m2", "q2s", "q2m", "r2", "a2", "i2", "f2"))
        vare2, spare = sb("vare2", [P, GB]), sb("spare", [P, 1])
        out1, out2 = sb("out1", [P, 3, GB]), sb("out2", [P, 3, GB])
        big1, int1 = sb("big1", [P, GB, D]), sb("int1", [P, GB, D], BF16)
        int1T = sb("int1T", [D, 3, T], BF16)
        pre = sb("pre", [P, GB, FF])
        hid = sb("hid", [P, GB, FF])
        sq = sb("sq", [P, FF])
        big2 = sb("big2", [P, GB, FF])
        int2 = sb("int2", [P, 3, GB, FF], BF16)
        int2T = sb("int2T", [P, 2, FF], BF16)

        xT_bank = ps("xT", [P, T], BF16)
        h_bank = [ps(f"h{i}", [P, FF]) for i in range(2)]
        t_bank = [ps(f"t{i}", [P, FF], BF16) for i in range(2)]
        y_bank = ps("y", [P, GB, D])
        w_bank = ps("w", [P, 2])

        weights_in, consts, w_abs, w_sum, w_inv, w_round, w_ready = (sem(n) for n in ("weights_in", "consts", "w_abs", "w_sum", "w_inv", "w_round", "w_ready"))
        bn_done, stats, var_ready, rstd_ready, xn_done, q1_ready, r1_ready, chain1, int1_ready, xT_ps, xT_sb = (
            sem(n) for n in ("bn_done", "stats", "var_ready", "rstd_ready", "xn_done", "q1_ready", "r1_ready", "chain1", "int1_ready", "xT_ps", "xT_sb"))
        h_ps, pre_sb, hid_sb, sq_sb, max2, q2_ready, r2_ready, chain2, int2_ready = (
            sem(n) for n in ("h_ps", "pre_sb", "hid_sb", "sq_sb", "max2", "q2_ready", "r2_ready", "chain2", "int2_ready"))
        max1, big1_ready, big2_ready = sem("max1"), sem("big1_ready"), sem("big2_ready")
        t_ps, t_sb, y_ps, x_biased, x_out = (sem(n) for n in ("t_ps", "t_sb", "y_ps", "x_biased", "x_out"))

        with nc.Block() as block:

            @block.sync
            def _(sp):
                sp.dma_start(w1f[:, :], w["w1"]).then_inc(weights_in, 16)
                sp.dma_start(w2f[:, :, :], w["w2"].rearrange("(c p) n -> p c n", p=P)).then_inc(weights_in, 16)
                sp.dma_start(b1[:, :], w["b1"].broadcast_to([P, FF])).then_inc(weights_in, 16)
                sp.dma_start(b2[:, :], w["b2"].broadcast_to([P, D])).then_inc(weights_in, 16)
                sp.wait_ge(weights_in, 64)

            @block.gpsimd
            def _(pool):
                for t, v in ((minus_half, -0.5), (eps, LN_EPS), (inv_ff, 1.0 / FF), (ones, 1.0)):
                    nc.gpsimd.memset(t[:, :], v).then_inc(consts, 1)
                pool.wait_ge(consts, 6)
                pool.wait_ge(weights_in, 64)

                def iteration(g, k):
                    a, b = g + 2, g + 1
                    if does(g, 2, n_groups):
                        pool.wait_ge(stats, a + 1)
                        nc.gpsimd.tensor_tensor(vare[:, :], mv[:, :, 1], eps[:, :], ALU.add).then_inc(var_ready, 1)
                        pool.wait_ge(var_ready, 3 * a + 1)
                        nc.gpsimd.tensor_tensor(rstd[:, :], vare[:, :], minus_half[:, :], ALU.pow).then_inc(rstd_ready, 1)
                        pool.wait_ge(rstd_ready, a + 1)
                        nc.gpsimd.tensor_tensor(q1s[:, :], rstd[:, :], rstd[:, :], ALU.mult).then_inc(var_ready, 1)
                        pool.wait_ge(var_ready, 3 * a + 2)
                        nc.gpsimd.tensor_tensor(r1[:, :], q1s[:, :], mv[:, :, 1], ALU.mult).then_inc(var_ready, 1)
                        pool.wait_ge(var_ready, 3 * a + 3)
                        nc.gpsimd.tensor_tensor(q1s[:, :], r1[:, :], eps[:, :], ALU.add).then_inc(q1_ready, 1)
                        pool.wait_ge(q1_ready, a + 1)
                        if counted(a):
                            pool.wait_ge(int1_ready, a)
                        nc.gpsimd.tensor_tensor(r1[:, :], q1s[:, :], minus_half[:, :], ALU.pow).then_inc(r1_ready, 1)
                    if does(g, 0, n_groups):
                        pool.wait_ge(xn_done, g + 1)
                        xg = x[:, bass.ds(GB * g, GB), :]
                        nc.gpsimd.tensor_tensor(xg, xg, b2[:, :].unsqueeze(1).broadcast_to([P, GB, D]), ALU.add).then_inc(x_biased, 1)
                    if does(g, 1, n_groups):
                        pool.wait_ge(sq_sb, GB * b + GB)
                        nc.gpsimd.tensor_tensor(q2m[:, :], q2s[:, :], inv_ff[:, :], ALU.mult).then_inc(q2_ready, 1)
                        pool.wait_ge(q2_ready, 2 * b + 1)
                        nc.gpsimd.tensor_tensor(vare2[:, :], q2m[:, :], eps[:, :], ALU.add).then_inc(q2_ready, 1)
                        pool.wait_ge(q2_ready, 2 * b + 2)
                        if counted(b):
                            pool.wait_ge(int2_ready, b)
                        nc.gpsimd.tensor_tensor(r2[:, :], vare2[:, :], minus_half[:, :], ALU.pow).then_inc(r2_ready, 1)

                groups_loop(pool, n_groups, iteration)

            @block.scalar
            def _(act):
                act.wait_ge(weights_in, 64)

                def iteration(g, k):
                    a, b = g + 2, g + 1
                    A, B, C = does(g, 2, n_groups), does(g, 1, n_groups), does(g, 0, n_groups)
                    for j in range(GB):
                        if B:
                            n = GB * b + j
                            act.wait_ge(pre_sb, n + 1)
                            if counted(b):
                                act.wait_ge(int2_ready, b)
                            nc.scalar.activation(hid[:, j, :], pre[:, j, :], ACT.Gelu).then_inc(hid_sb, 1)
                        if C:
                            n = GB * g + j
                            act.wait_ge(t_ps, n + 1)
                            if counted(n - 1):
                                act.wait_ge(y_ps, n - 1)
                            nc.scalar.activation(int2T[:, j % 2, :], t_bank[j % 2][:, :], ACT.Copy).then_inc(t_sb, 1)
                    if A:
                        act.wait_ge(xT_ps, a + 1)
                        if counted(GB * (a - 2)):
                            act.wait_ge(h_ps, GB * (a - 2))
                        nc.scalar.activation(int1T[:, (k + 2) % 3, :], xT_bank[:, :], ACT.Copy).then_inc(xT_sb, 1)
                    if B:
                        for j in range(GB):
                            act.wait_ge(hid_sb, GB * b + j + 1)
                            if j == 0:
                                if counted(2 * b):
                                    act.wait_ge(q2_ready, 2 * b)
                            if counted(GB * b + j):
                                act.wait_ge(sq_sb, GB * b + j)
                            nc.scalar.activation(sq[:, :], hid[:, j, :], ACT.Square, accum_out=q2s[:, j:j + 1]).then_inc(sq_sb, 1)

                groups_loop(act, n_groups, iteration)

            @block.vector
            def _(dve):
                dve.wait_ge(weights_in, 64)
                nc.vector.tensor_reduce(wabs[:, 0:1], w1f[:, :], axis=AX.X, op=ALU.add, apply_absolute_value=True).then_inc(w_abs, 1)
                nc.vector.tensor_reduce(wabs[:, 1:2], w2f[:, :, :].rearrange("p c n -> p (c n)"), axis=AX.X, op=ALU.add, apply_absolute_value=True).then_inc(w_abs, 1)
                nc.vector.tensor_copy(identb[:, :], ident[:, :]).then_inc(consts, 1)
                dve.wait_ge(w_sum, 1)
                nc.vector.tensor_scalar(wmean[:, :], w_bank[:, :], 1.0 / (FF * D), CLIP, ALU.mult, ALU.max).then_inc(w_inv, 1)
                dve.wait_ge(w_inv, 1)
                nc.vector.reciprocal(winv[:, :], wmean[:, :]).then_inc(w_inv, 1)
                dve.wait_ge(w_inv, 2)
                for i, (full, rounded, whole) in enumerate(((w1f[:, :], w1r, w1i[:, :]),
                                                            (w2f[:, :, :].rearrange("p c n -> p (c n)"), w2r, w2i[:, :, :].rearrange("p c n -> p (c n)")))):
                    nc.vector.tensor_scalar(rounded[:, :], full, winv[:, i:i + 1], MAGIC, ALU.mult, ALU.add).then_inc(w_round, 1)
                    dve.wait_ge(w_round, 2 * i + 1)
                    nc.vector.tensor_scalar(full, rounded[:, :], MAGIC, 1.0, ALU.subtract, ALU.min).then_inc(w_round, 1)
                    dve.wait_ge(w_round, 2 * i + 2)
                    nc.vector.tensor_scalar(whole, full, -1.0, 0.0, ALU.max, ALU.add).then_inc(w_ready, 1)
                nc.vector.tensor_scalar(wabs[:, :], wmean[:, :], 1.0 / QMAX, 0.0, ALU.mult, ALU.add).then_inc(consts, 1)
                dve.wait_ge(consts, 6)

                def factors(first, peak, rec, clipped, inverse, factor, outs, k, i, chain, n):
                    dve.wait_ge(first, n + 1)
                    nc.vector.tensor_tensor(clipped[:, :], peak[:, :], rec[:, :], ALU.mult).then_inc(chain, 1)
                    dve.wait_ge(chain, 4 * n + 1)
                    nc.vector.tensor_scalar(inverse[:, :], clipped[:, :], CLIP, 1.0, ALU.max, ALU.mult).then_inc(chain, 1)
                    dve.wait_ge(chain, 4 * n + 2)
                    nc.vector.tensor_scalar(outs[:, k, :], inverse[:, :], wabs[:, i:i + 1], None, ALU.mult)
                    nc.vector.reciprocal(clipped[:, :], inverse[:, :]).then_inc(chain, 1)
                    dve.wait_ge(chain, 4 * n + 3)
                    nc.vector.scalar_tensor_tensor(factor[:, :], clipped[:, :], QMAX, rec[:, :], ALU.mult, ALU.mult).then_inc(chain, 1)
                    dve.wait_ge(chain, 4 * n + 4)

                def iteration(g, k):
                    a, b, ka, kb = g + 2, g + 1, (k + 2) % 3, (k + 1) % 3
                    A, B, C = does(g, 2, n_groups), does(g, 1, n_groups), does(g, 0, n_groups)
                    if A:
                        if counted(a):
                            dve.wait_ge(r1_ready, a)
                        for j in range(GB):
                            last = nc.vector.bn_stats(stat6[:, j, :], x[:, bass.ds(GB * a + j, 1), :].rearrange("p o c -> p (o c)"))
                        last.then_inc(bn_done, 1)
                        dve.wait_ge(bn_done, a + 1)
                    if B:
                        for j in range(GB):
                            n = GB * b + j
                            dve.wait_ge(h_ps, n + 1)
                            if counted(n - GB + 1):
                                dve.wait_ge(hid_sb, n - GB + 1)
                            nc.vector.scalar_tensor_tensor(pre[:, j, :], h_bank[j % 2][:, :], out1[:, kb, j:j + 1], b1[:, :], ALU.mult, ALU.add).then_inc(pre_sb, 1)
                    if A:
                        if not B:
                            nc.vector.tensor_copy(spare[:, :], stat6[:, 0, 0:1])
                        for j in range(GB):
                            last = nc.vector.bn_aggr(mv[:, j, :], stat6[:, j, :])
                        last.then_inc(stats, 1)
                    if B:
                        for j in range(GB):
                            dve.wait_ge(hid_sb, GB * b + j + 1)
                            last = nc.vector.tensor_reduce(m2[:, j:j + 1], hid[:, j, :], axis=AX.X, op=ALU.max, apply_absolute_value=True)
                        last.then_inc(max2, 1)
                    if A:
                        dve.wait_ge(rstd_ready, a + 1)
                        for j in range(GB):
                            last = nc.vector.tensor_scalar(xn[:, j, :], x[:, bass.ds(GB * a + j, 1), :].rearrange("p o c -> p (o c)"),
                                                           mv[:, j, 0:1], rstd[:, j:j + 1], ALU.subtract, ALU.mult)
                        last.then_inc(xn_done, 1)
                        dve.wait_ge(xn_done, a + 1)
                        nc.vector.tensor_reduce(m1[:, :], xn[:, :, :], axis=AX.X, op=ALU.max, apply_absolute_value=True).then_inc(max1, 1)
                        dve.wait_ge(max1, a + 1)
                        factors(r1_ready, m1, r1, a1, i1, f1, out1, ka, 0, chain1, a)
                        for j in range(GB):
                            last = nc.vector.tensor_scalar(big1[:, j, :], xn[:, j, :], f1[:, j:j + 1], MAGIC, ALU.mult, ALU.add)
                        last.then_inc(big1_ready, 1)
                        dve.wait_ge(big1_ready, a + 1)
                        if counted(a):
                            dve.wait_ge(xT_ps, a)
                        nc.vector.tensor_scalar(int1[:, :, :], big1[:, :, :], MAGIC, QMAX, ALU.subtract, ALU.min).then_inc(int1_ready, 1)
                    if B:
                        dve.wait_ge(max2, b + 1)
                        factors(r2_ready, m2, r2, a2, i2, f2, out2, kb, 1, chain2, b)
                        for j in range(GB):
                            last = nc.vector.tensor_scalar(big2[:, j, :], hid[:, j, :], f2[:, j:j + 1], MAGIC, ALU.mult, ALU.add)
                        last.then_inc(big2_ready, 1)
                        dve.wait_ge(big2_ready, b + 1)
                        if counted(GB * (b - 2)):
                            dve.wait_ge(t_ps, GB * (b - 2))
                        nc.vector.tensor_scalar(int2[:, kb, :, :], big2[:, :, :], MAGIC, QMAX, ALU.subtract, ALU.min).then_inc(int2_ready, 1)
                    if C:
                        dve.wait_ge(x_biased, g + 1)
                        if counted(GB * g + GB):
                            dve.wait_ge(y_ps, GB * g + GB)
                        for j in range(GB):
                            xj = x[:, bass.ds(GB * g + j, 1), :].rearrange("p o c -> p (o c)")
                            last = nc.vector.scalar_tensor_tensor(xj, y_bank[:, j, :], out2[:, k, j:j + 1], xj, ALU.mult, ALU.add)
                        last.then_inc(x_out, 1)

                groups_loop(dve, n_groups, iteration)
                dve.wait_ge(x_out, n_groups)

            @block.tensor
            def _(pe):
                pe.wait_ge(w_abs, 2)
                pe.wait_ge(consts, 5)
                nc.tensor.matmul(w_bank[:, :], ones[:, :], wabs[:, :], start=True, stop=True).then_inc(w_sum, 1)
                pe.wait_ge(w_ready, 2)
                pe.wait_ge(consts, 6)

                def iteration(g, k):
                    a, b, ka, kb = g + 2, g + 1, (k + 2) % 3, (k + 1) % 3
                    A, B, C = does(g, 2, n_groups), does(g, 1, n_groups), does(g, 0, n_groups)
                    for j in range(GB):
                        if B:
                            n = GB * b + j
                            pe.wait_ge(xT_sb, b + 1)
                            if counted(n - 1):
                                pe.wait_ge(pre_sb, n - 1)
                            nc.tensor.matmul(h_bank[j % 2][:, :], int1T[:, kb, j * S:(j + 1) * S], w1i[:, :], start=True, stop=True).then_inc(h_ps, 1)
                        if C:
                            n = GB * g + j
                            pe.wait_ge(int2_ready, g + 1)
                            if counted(n - 1):
                                pe.wait_ge(t_sb, n - 1)
                            for c in range(FCH):
                                last = nc.tensor.transpose(t_bank[j % 2][:, c * P:(c + 1) * P], int2[:, k, j, c * P:(c + 1) * P], identb[:, :])
                            last.then_inc(t_ps, 1)
                            pe.wait_ge(t_sb, n + 1)
                            if j == 0:
                                if counted(g):
                                    pe.wait_ge(x_out, g)
                            for c in range(FCH):
                                last = nc.tensor.matmul(y_bank[:, j, :], int2T[:, j % 2, c * P:(c + 1) * P], w2i[:, c, :], start=(c == 0), stop=(c == FCH - 1))
                            last.then_inc(y_ps, 1)
                    if A:
                        pe.wait_ge(int1_ready, a + 1)
                        if counted(a):
                            pe.wait_ge(xT_sb, a)
                        for j in range(GB):
                            last = nc.tensor.transpose(xT_bank[:, j * S:(j + 1) * S], int1[:, j, :], identb[:, :])
                        last.then_inc(xT_ps, 1)

                groups_loop(pe, n_groups, iteration)


def before(g, ahead, n_groups):
    return min(max(g + ahead, 0), n_groups) if isinstance(g, int) else g + ahead


def through(g, ahead, n_groups):
    return before(g + 1, ahead, n_groups)


def quantum_composites(nc, env, q):
    QFF, NQ = 512, 8
    CH = QFF // P
    ctx = ExitStack()
    with ctx:
        def sb(n, shape, dt=F32):
            return ctx.enter_context(nc.sbuf_tensor(f"comp_{n}", shape, dt))

        w1T = sb("w1T", [P, CH, D])
        wm = sb("wm", [P, CH, NQ])
        b1 = sb("b1", [P, CH])
        bqo = sb("bqo", [P, CH])
        bm, b2 = sb("bm", [P, NQ]), sb("b2", [P, D])
        w2 = sb("w2", [P, CH, D])
        wqoT = sb("wqoT", [P, CH, GB * NQ])
        b1w, bqow = sb("b1w", [P, CH, P]), sb("bqow", [P, CH, P])
        out_sb = sb("out_sb", [GB * NQ, D])
        banks = [ctx.enter_context(nc.psum_tensor(f"comp_ps{i}", [P, 512], F32)) for i in range(4)]
        loaded, spread, product, read, zeroed, placed = (nc.alloc_semaphore(f"comp_{n}")
                                                         for n in ("loaded", "spread", "product", "read", "zeroed", "placed"))
        with nc.Block() as block:

            @block.sync
            def _(sp):
                sp.dma_start(w1T[:, :, :], q["W1T"].rearrange("(c p) n -> p c n", p=P)).then_inc(loaded, 16)
                sp.dma_start(wm[:, :, :], q["Wm"].rearrange("(c p) n -> p c n", p=P)).then_inc(loaded, 16)
                sp.dma_start(w2[:, :, :], q["W2"].rearrange("(c p) n -> p c n", p=P)).then_inc(loaded, 16)
                for dst, src in ((b1, q["b1"]), (bqo, q["bqo"])):
                    for c in range(CH):
                        sp.dma_start(dst[:, c:c + 1], src[c * P:(c + 1) * P].unsqueeze(1)).then_inc(loaded, 16)
                sp.dma_start(bm[:, :], q["bm"].unsqueeze(0).broadcast_to([P, NQ])).then_inc(loaded, 16)
                sp.dma_start(b2[:, :], q["b2"].unsqueeze(0).broadcast_to([P, D])).then_inc(loaded, 16)
                for j in range(GB):
                    sp.dma_start(wqoT[:, :, NQ * j:NQ * (j + 1)], q["WqoT"].rearrange("(c p) n -> p c n", p=P)).then_inc(loaded, 16)
                sp.wait_ge(read, 4)
                sp.wait_ge(zeroed, 1)
                for j in range(GB):
                    sp.dma_start(env["w_out"][NQ * j:NQ * (j + 1), j, :], out_sb[NQ * j:NQ * (j + 1), :]).then_inc(placed, 16)
                sp.wait_ge(placed, 16 * GB)

            @block.vector
            def _(dve):
                nc.vector.memset(env["w_out"][:, :, :], 0.0).then_inc(zeroed, 1)
                dve.wait_ge(loaded, 16 * 17)
                nc.vector.tensor_copy(b1w[:, :, :], b1[:, :].unsqueeze(2).broadcast_to([P, CH, P])).then_inc(spread, 1)
                nc.vector.tensor_copy(bqow[:, :, :], bqo[:, :].unsqueeze(2).broadcast_to([P, CH, P])).then_inc(spread, 1)
                dve.wait_ge(product, 4)
                nc.vector.tensor_copy(env["w_in"][:, :], banks[0][:, 0:NQ]).then_inc(read, 1)
                nc.vector.tensor_tensor(env["b_in"][:, :], banks[1][:, 0:NQ], bm[:, :], ALU.add).then_inc(read, 1)
                nc.vector.tensor_tensor(env["b_out"][:, :], banks[3][:, 0:D], b2[:, :], ALU.add).then_inc(read, 1)
                nc.vector.tensor_copy(out_sb[:, :], banks[2][0:GB * NQ, 0:D]).then_inc(read, 1)
                dve.wait_ge(read, 4)

            @block.tensor
            def _(pe):
                pe.wait_ge(loaded, 16 * 17)
                pe.wait_ge(spread, 2)
                for bank, left, right, rows, cols in ((banks[0], w1T, wm, P, NQ), (banks[1], b1w, wm, P, NQ),
                                                      (banks[2], wqoT, w2, GB * NQ, D), (banks[3], bqow, w2, P, D)):
                    for c in range(CH):
                        last = nc.tensor.matmul(bank[0:rows, 0:cols], left[:, c, :], right[:, c, :], start=(c == 0), stop=(c == CH - 1))
                    last.then_inc(product, 1)


def quantum_block(nc, env, n_groups, q):
    x, ident = env["x"], env["ident"]
    H, HD, NQ = 8, 16, 8
    TINY = 1e-30
    EPS_COS = 1e-8
    MAGIC = 1.5 * 2.0 ** 23
    PI_BELOW = float(np.nextafter(np.float32(np.pi), np.float32(0)))
    ctx = ExitStack()
    with ctx:
        def sb(n, shape, dt=F32):
            return ctx.enter_context(nc.sbuf_tensor(f"a0_{n}", shape, dt))

        def ps(n, shape):
            return ctx.enter_context(nc.psum_tensor(f"a0_{n}", shape, F32))

        def sem(n):
            return nc.alloc_semaphore(f"a0_{n}")

        env = dict(env)
        env.update(w_in=sb("w_in", [D, NQ]), b_in=sb("b_in", [P, NQ]), w_out=sb("w_out", [P, GB, D]), b_out=sb("b_out", [P, D]))
        quantum_composites(nc, env, q)

        wq, wk, wv, wo, wc, blocks = (sb(n, [D, D]) for n in ("wq", "wk", "wv", "wo", "wc", "blocks"))
        bq, bk, bc = sb("bq", [D, 1]), sb("bk", [D, 1]), sb("bc", [D, 1])
        bv, bo, g1, beta1, g2, beta2 = (sb(n, [P, D]) for n in ("bv", "bo", "g1", "beta1", "g2", "beta2"))
        half_pi = sb("half_pi", [P, 1])
        minus_half, eps = sb("minus_half", [P, GB]), sb("eps", [P, GB])
        norms = [dict(stat6=sb(f"stat6_{i}", [P, GB, 6]), mv=sb(f"mv_{i}", [P, GB, 2]), vare=sb(f"vare_{i}", [P, GB]), rstd=sb(f"rstd_{i}", [P, GB]),
                      bn=sem(f"bn_{i}"), stats=sem(f"stats_{i}"), var=sem(f"var_{i}"), ready=sem(f"rstd_ready_{i}")) for i in range(3)]
        xn = sb("xn", [P, 3, GB, D])
        xnT = sb("xnT", [D, T])
        qf, kf, qqn, qn = (sb(n, [D, 3, T]) for n in ("qf", "kf", "qqn", "qn"))
        V = sb("V", [P, 3, GB, D])
        qqf, kqf, rq, rk, kn16 = (sb(n, [D, T]) for n in ("qqf", "kqf", "rq", "rk", "kn16"))
        K_spread, C_spread, N_spread = (sb(n, [D, H, T]) for n in ("K_spread", "C_spread", "N_spread"))
        F, sn = sb("F", [P, GB, H, S]), sb("sn", [P, GB, H, S])
        Pr = sb("Pr", [P, 2, H, S])
        PT = sb("PT", [P, H, S])
        nm, nm8, rsum, rrec = sb("nm", [P, H]), sb("nm8", [P, 2, H]), sb("rsum", [P, 2, H]), sb("rrec", [P, H])
        on = sb("on", [P, GB, H, HD])
        oT, resid, r, x1, x1b, x1T, y, yh = (sb(n, [P, GB, D]) for n in ("oT", "resid", "r", "x1", "x1b", "x1T", "y", "yh"))
        qm, u, v, th, cs = (sb(n, [P, GB, NQ]) for n in ("qm", "u", "v", "th", "cs"))
        qe, qeT = sb("qe", [P, P]), sb("qeT", [P, P])

        cos_b, den_b = ps("cos_b", [P, 4, S]), ps("den_b", [P, 4, S])
        s_b = ps("s_b", [P, H, S])
        pt_b, o_b, mA, mB = ps("pt_b", [P, 4, S]), ps("o_b", [P, GB, H, HD]), ps("mA", [P, 512]), ps("mB", [P, 512])

        weights_in, zeroed, placed = sem("weights_in"), sem("zeroed"), sem("placed")
        (sp_waits_met, xn_ready, xnT_ps, xnT_sb, q_ps, q_sb, k_ps, k_sb, v_ps, v_sb, qq_ps, qq_sb, kq_ps, kq_sb, q2_ready, k2_ready, ssq_ps, qn_sb,
         ssk_ps, kn_sb, norm_chain, qqn_ready, kqn_ready, C_in, N_in, K_in, cos_sb, cd_ps, f_sb, f_clamped, sn_sb) = (sem(n) for n in (
             "sp_waits_met", "xn_ready", "xnT_ps", "xnT_sb", "q_ps", "q_sb", "k_ps", "k_sb", "v_ps", "v_sb", "qq_ps", "qq_sb", "kq_ps", "kq_sb", "q2_ready",
             "k2_ready", "ssq_ps", "qn_sb", "ssk_ps", "kn_sb", "norm_chain", "qqn_ready", "kqn_ready", "C_in", "N_in", "K_in", "cos_sb", "cd_ps", "f_sb", "f_clamped", "sn_sb"))
        (s_ps, g_sb, a_sb, nm_sb, nm8_sb, p_sb, t_ps, pt_sb, o_ps, rr_sb, o_sb, resid_ready, oT_ps, oT_sb, wo_ps, r_ready, xh_ready, x1_scaled, x1_ready,
         x1b_ready, xt_ps, xt_sb, qm_ps, qm_sb, v_chain, trig, qe_ready, qe_ps, qeT_sb, ff_ps, y_ready, yh_ready, z_chain, x_out) = (sem(n) for n in (
             "s_ps", "g_sb", "a_sb", "nm_sb", "nm8_sb", "p_sb", "t_ps", "pt_sb", "o_ps", "rr_sb", "o_sb", "resid_ready", "oT_ps", "oT_sb", "wo_ps", "r_ready",
             "xh_ready", "x1_scaled", "x1_ready", "x1b_ready", "xt_ps", "xt_sb", "qm_ps", "qm_sb", "v_chain", "trig", "qe_ready", "qe_ps", "qeT_sb", "ff_ps",
             "y_ready", "yh_ready", "z_chain", "x_out"))

        N_WEIGHTS = 12
        N_ZEROED = 11
        N = n_groups

        def loop(eng, iteration):
            groups_loop(eng, N, iteration, after=2)

        with nc.Block() as block:

            @block.sync
            def _(sp):
                for dst, src in ((wq, q["Wq"]), (wk, q["Wk"]), (wv, q["Wv"]), (wo, q["Wo"]), (bq, q["bq"]), (bk, q["bk"])):
                    sp.dma_start(dst[:, :], src).then_inc(weights_in, 16)
                for dst, src in ((bv, q["bv"]), (bo, q["bo"]), (g1, q["g1"]), (beta1, q["beta1"]), (g2, q["g2"]), (beta2, q["beta2"])):
                    sp.dma_start(dst[:, :], src.broadcast_to([P, D])).then_inc(weights_in, 16)
                sp.wait_ge(zeroed, N_ZEROED)
                for h in range(H):
                    r0 = HD * h
                    sp.dma_start(wc[r0:r0 + HD, r0:r0 + NQ], q["Wc2q"][h]).then_inc(placed, 16)
                    sp.dma_start(bc[r0:r0 + NQ, :], q["bc2q"][h].unsqueeze(1)).then_inc(placed, 16)
                    sp.dma_start(blocks[r0:r0 + HD, r0:r0 + HD], rq[0:HD, 0:HD]).then_inc(placed, 16)

                def spread(dst, src, done):
                    for h in range(H):
                        sp.dma_start(dst[HD * h:HD * (h + 1), h, :], src[HD * h:HD * (h + 1), :]).then_inc(done, 16)

                def iteration(g, k):
                    a, b, ka, kb = g + 2, g + 1, (k + 2) % 3, (k + 1) % 3
                    if does(g, 1, N):
                        sp.wait_ge(k_sb, b + 1)
                        sp.sem_inc(sp_waits_met, 1)
                        if counted(4 * b):
                            sp.wait_ge(s_ps, 4 * b)
                            sp.sem_inc(sp_waits_met, 1)
                        if counted(16 * H * b):
                            sp.wait_ge(K_in, 16 * H * b)
                            sp.sem_inc(sp_waits_met, 1)
                        spread(K_spread, kf[:, kb, :], K_in)
                    if does(g, 2, N):
                        sp.wait_ge(kn_sb, a + 1)
                        sp.sem_inc(sp_waits_met, 1)
                        if counted(8 * a):
                            sp.wait_ge(cd_ps, 8 * a)
                            sp.sem_inc(sp_waits_met, 1)
                        if counted(16 * H * a):
                            sp.wait_ge(N_in, 16 * H * a)
                            sp.sem_inc(sp_waits_met, 1)
                        spread(N_spread, kn16[:, :], N_in)
                        sp.wait_ge(kqn_ready, a + 1)
                        sp.sem_inc(sp_waits_met, 1)
                        if counted(16 * H * a):
                            sp.wait_ge(C_in, 16 * H * a)
                            sp.sem_inc(sp_waits_met, 1)
                        spread(C_spread, kqf[:, :], C_in)

                loop(sp, iteration)

            def inverse_deviation(pool, n, norm):
                pool.wait_ge(norm['stats'], n + 1)
                nc.gpsimd.tensor_tensor(norm["vare"][:, :], norm["mv"][:, :, 1], eps[:, :], ALU.add).then_inc(norm["var"], 1)
                pool.wait_ge(norm['var'], n + 1)
                nc.gpsimd.tensor_tensor(norm["rstd"][:, :], norm["vare"][:, :], minus_half[:, :], ALU.pow).then_inc(norm["ready"], 1)

            def statistics(dve, n, norm, src, src_ready, normed):
                dve.wait_ge(src_ready, n + 1)
                if counted(n):
                    dve.wait_ge(normed, n)
                for j in range(GB):
                    last = nc.vector.bn_stats(norm["stat6"][:, j, :], src[:, j, :])
                last.then_inc(norm["bn"], 1)
                dve.wait_ge(norm['bn'], n + 1)
                nc.vector.tensor_copy(spare[:, :], norm["stat6"][:, 0, 0:1])
                for j in range(GB):
                    last = nc.vector.bn_aggr(norm["mv"][:, j, :], norm["stat6"][:, j, :])
                last.then_inc(norm["stats"], 1)

            def normalise(norm, dst, src, done):
                for j in range(GB):
                    last = nc.vector.tensor_scalar(dst[:, j, :], src[:, j, :], norm["mv"][:, j, 0:1], norm["rstd"][:, j:j + 1], ALU.subtract, ALU.mult)
                last.then_inc(done, 1)

            spare = sb("spare", [P, 1])

            @block.gpsimd
            def _(pool):
                nc.gpsimd.memset(minus_half[:, :], -0.5).then_inc(zeroed, 1)
                nc.gpsimd.memset(eps[:, :], LN_EPS).then_inc(zeroed, 1)
                nc.gpsimd.memset(half_pi[:, :], math.pi / 2).then_inc(zeroed, 1)
                nc.gpsimd.memset(wc[:, :], 0.0).then_inc(zeroed, 1)
                nc.gpsimd.memset(bc[:, :], 0.0).then_inc(zeroed, 1)
                nc.gpsimd.memset(blocks[:, :], 0.0).then_inc(zeroed, 1)
                nc.gpsimd.memset(rq[:, :], 1.0).then_inc(zeroed, 1)
                nc.gpsimd.memset(qe[:, :], 0.0).then_inc(zeroed, 1)
                pool.wait_ge(weights_in, 16 * N_WEIGHTS)
                pool.wait_ge(placed, 16 * 3 * H)
                pool.wait_ge(zeroed, N_ZEROED)

                def by_channel(row):
                    return row[:, :].unsqueeze(1).broadcast_to([P, GB, D])

                def iteration(g, k):
                    a, d, e, ka = g + 2, g - 1, g - 2, (k + 2) % 3
                    if does(g, 2, N):
                        inverse_deviation(pool, a, norms[0])
                    if does(g, -1, N):
                        inverse_deviation(pool, d, norms[1])
                    if does(g, -2, N):
                        inverse_deviation(pool, e, norms[2])
                    if does(g, -1, N):
                        pool.wait_ge(xh_ready, d + 1)
                        if counted(d):
                            pool.wait_ge(xt_ps, d)
                        nc.gpsimd.tensor_tensor(x1[:, :, :], r[:, :, :], by_channel(g1), ALU.mult).then_inc(x1_scaled, 1)
                        pool.wait_ge(x1_scaled, d + 1)
                        nc.gpsimd.tensor_tensor(x1[:, :, :], x1[:, :, :], by_channel(beta1), ALU.add).then_inc(x1_ready, 1)
                        pool.wait_ge(x1_ready, d + 1)
                        if counted(d):
                            pool.wait_ge(y_ready, d)
                        nc.gpsimd.tensor_tensor(x1b[:, :, :], x1[:, :, :], by_channel(env["b_out"]), ALU.add).then_inc(x1b_ready, 1)
                    if does(g, 0, N):
                        if counted(g):
                            pool.wait_ge(r_ready, g)
                        nc.gpsimd.tensor_tensor(resid[:, :, :], xn[:, k, :, :], by_channel(bo), ALU.add).then_inc(resid_ready, 1)
                    if does(g, -2, N):
                        pool.wait_ge(yh_ready, e + 1)
                        nc.gpsimd.tensor_tensor(yh[:, :, :], yh[:, :, :], by_channel(g2), ALU.mult).then_inc(z_chain, 1)
                        pool.wait_ge(z_chain, 2 * e + 1)
                        nc.gpsimd.tensor_tensor(yh[:, :, :], yh[:, :, :], by_channel(beta2), ALU.add).then_inc(z_chain, 1)
                        pool.wait_ge(z_chain, 2 * e + 2)
                        xg = x[:, bass.ds(GB * e, GB), :]
                        nc.gpsimd.tensor_tensor(xg, xg, yh[:, :, :], ALU.add).then_inc(x_out, 1)
                    if does(g, 2, N):
                        pool.wait_ge(qq_sb, a + 1)
                        if counted(a):
                            pool.wait_ge(qqn_ready, a)
                        nc.gpsimd.tensor_tensor(rq[:, :], qqf[:, :], qqf[:, :], ALU.mult).then_inc(q2_ready, 1)
                        pool.wait_ge(kq_sb, a + 1)
                        if counted(a):
                            pool.wait_ge(kqn_ready, a)
                        nc.gpsimd.tensor_tensor(rk[:, :], kqf[:, :], kqf[:, :], ALU.mult).then_inc(k2_ready, 1)

                loop(pool, iteration)
                pool.wait_ge(x_out, N)



            @block.scalar
            def _(act):
                act.wait_ge(weights_in, 16 * N_WEIGHTS)
                act.wait_ge(placed, 16 * 3 * H)
                act.wait_ge(zeroed, N_ZEROED)

                def cosines(g, b, j, half):
                    n = 8 * b + 2 * j + half
                    act.wait_ge(cd_ps, n + 1)
                    if counted(GB * g + j + 1):
                        act.wait_ge(g_sb, GB * g + j + 1)
                    nc.scalar.activation(F[:, j, 4 * half:4 * half + 4, :], cos_b[:, :, :], ACT.Copy).then_inc(cos_sb, 1)

                def iteration(g, k):
                    a, b, d, e, ka = g + 2, g + 1, g - 1, g - 2, (k + 2) % 3
                    A, B, C, DD, E = (does(g, s, N) for s in (2, 1, 0, -1, -2))
                    for j in range(GB):
                        if B:
                            cosines(g, b, j, 0)
                        if C:
                            n = GB * g + j
                            act.wait_ge(nm8_sb, n + 1)
                            if counted(n - 1):
                                act.wait_ge(o_sb, n - 1)
                            for h in range(H):
                                last = nc.scalar.activation(Pr[:, j % 2, h, :], Pr[:, j % 2, h, :], ACT.Exp, bias=nm8[:, j % 2, h:h + 1], scale=0.125,
                                                            accum_out=rsum[:, j % 2, h:h + 1])
                            last.then_inc(p_sb, 1)
                            for half in range(2):
                                act.wait_ge(t_ps, 2 * n + half + 1)
                                if half == 0:
                                    if counted(n):
                                        act.wait_ge(o_ps, n)
                                nc.scalar.activation(PT[:, 4 * half:4 * half + 4, :], pt_b[:, :, :], ACT.Copy).then_inc(pt_sb, 1)
                        if B:
                            cosines(g, b, j, 1)
                        if j == 0:
                            if DD:
                                act.wait_ge(oT_ps, d + 1)
                                if counted(d):
                                    act.wait_ge(wo_ps, d)
                                nc.scalar.activation(oT[:, :, :].rearrange("p a b -> p (a b)"), mB[:, :], ACT.Copy).then_inc(oT_sb, 1)
                            if A:
                                act.wait_ge(xnT_ps, a + 1)
                                if counted(a):
                                    act.wait_ge(v_ps, a)
                                nc.scalar.activation(xnT[:, :], mA[:, :], ACT.Copy).then_inc(xnT_sb, 1)
                            if E:
                                act.wait_ge(qe_ps, e + 1)
                                if counted(e):
                                    act.wait_ge(ff_ps, e)
                                nc.scalar.activation(qeT[:, :], mA[:, 0:P], ACT.Copy).then_inc(qeT_sb, 1)
                        if j == 1 and A:
                            act.wait_ge(q_ps, a + 1)
                            if counted(4 * (a - 2)):
                                act.wait_ge(s_ps, 4 * (a - 2))
                            nc.scalar.activation(qf[:, ka, :], mB[:, :], ACT.Identity, bias=bq[:, 0:1]).then_inc(q_sb, 1)
                            act.wait_ge(k_ps, a + 1)
                            if counted(16 * H * (a - 2)):
                                act.wait_ge(K_in, 16 * H * (a - 2))
                            nc.scalar.activation(kf[:, ka, :], mA[:, :], ACT.Identity, bias=bk[:, 0:1]).then_inc(k_sb, 1)
                        if j == 2:
                            if A:
                                act.wait_ge(qq_ps, a + 1)
                                if counted(a):
                                    act.wait_ge(qqn_ready, a)
                                nc.scalar.activation(qqf[:, :], mA[:, :], ACT.Identity, bias=bc[:, 0:1]).then_inc(qq_sb, 1)
                                act.wait_ge(kq_ps, a + 1)
                                if counted(16 * H * a):
                                    act.wait_ge(C_in, 16 * H * a)
                                nc.scalar.activation(kqf[:, :], mA[:, :], ACT.Identity, bias=bc[:, 0:1]).then_inc(kq_sb, 1)
                            if DD:
                                act.wait_ge(xt_ps, d + 1)
                                if counted(d):
                                    act.wait_ge(qm_ps, d)
                                nc.scalar.activation(x1T[:, :, :].rearrange("p a b -> p (a b)"), mB[:, :], ACT.Copy).then_inc(xt_sb, 1)
                        if j == 3 and A:
                            act.wait_ge(ssq_ps, a + 1)
                            if counted(8 * (a - 2)):
                                act.wait_ge(cd_ps, 8 * (a - 2))
                            nc.scalar.activation(qn[:, ka, :], mA[:, :], ACT.Sqrt).then_inc(qn_sb, 1)
                            act.wait_ge(ssk_ps, a + 1)
                            if counted(16 * H * a):
                                act.wait_ge(N_in, 16 * H * a)
                            if counted(a):
                                act.wait_ge(kqn_ready, a)
                            nc.scalar.activation(kn16[:, :], mB[:, :], ACT.Sqrt, scale=2.0 ** -8).then_inc(kn_sb, 1)
                    if DD:
                        act.wait_ge(v_chain, 4 * d + 4)
                        if counted(d):
                            act.wait_ge(qe_ready, d)
                        nc.scalar.activation(th[:, :, :], qm[:, :, :], ACT.Tanh).then_inc(trig, 1)
                        nc.scalar.activation(cs[:, :, :], v[:, :, :], ACT.Sin, bias=half_pi[:, 0:1], scale=-2 * math.pi).then_inc(trig, 1)
                    if B:
                        for j in range(GB):
                            act.wait_ge(f_clamped, GB * b + j + 1)
                            if counted(GB * g + j + 1):
                                act.wait_ge(a_sb, GB * g + j + 1)
                            nc.scalar.activation(sn[:, j, :, :], F[:, j, :, :], ACT.Sin, scale=PI_BELOW).then_inc(sn_sb, 1)

                loop(act, iteration)

            @block.vector
            def _(dve):
                for t in (K_spread, C_spread, N_spread):
                    nc.vector.memset(t[:, :, :], 0.0).then_inc(zeroed, 1)
                dve.wait_ge(weights_in, 16 * N_WEIGHTS)
                dve.wait_ge(placed, 16 * 3 * H)
                dve.wait_ge(zeroed, N_ZEROED)

                def prepare_rows(g, j):
                    n = GB * g + j
                    dve.wait_ge(sn_sb, n + 1)
                    nc.vector.scalar_tensor_tensor(sn[:, j, :, :], sn[:, j, :, :], 10.0, F[:, j, :, :], ALU.add, ALU.mult).then_inc(g_sb, 1)
                    dve.wait_ge(g_sb, n + 1)
                    dve.wait_ge(s_ps, n + 1)
                    if counted(2 * (n - 1)):
                        dve.wait_ge(t_ps, 2 * (n - 1))
                    nc.vector.scalar_tensor_tensor(Pr[:, j % 2, :, :], sn[:, j, :, :], 0.4, s_b[:, :, :], ALU.mult, ALU.add).then_inc(a_sb, 1)
                    dve.wait_ge(a_sb, n + 1)
                    if counted(n):
                        dve.wait_ge(nm8_sb, n)
                    nc.vector.tensor_reduce(nm[:, :], Pr[:, j % 2, :, :], axis=AX.X, op=ALU.max, negate=True).then_inc(nm_sb, 1)
                    dve.wait_ge(nm_sb, n + 1)
                    if counted(n - 1):
                        dve.wait_ge(p_sb, n - 1)
                    nc.vector.tensor_scalar(nm8[:, j % 2, :], nm[:, :], 0.125, 0.0, ALU.mult, ALU.add).then_inc(nm8_sb, 1)

                def fidelity(g, b, j, half):
                    n = 8 * b + 2 * j + half
                    fh = F[:, j, 4 * half:4 * half + 4, :]
                    dve.wait_ge(cos_sb, n + 1)
                    nc.vector.scalar_tensor_tensor(fh, den_b[:, :, :], EPS_COS, fh, ALU.min, ALU.mult).then_inc(f_sb, 1)

                def iteration(g, k):
                    a, b, d, e, ka = g + 2, g + 1, g - 1, g - 2, (k + 2) % 3
                    A, B, C, DD, E = (does(g, s, N) for s in (2, 1, 0, -1, -2))
                    if A:
                        if counted(a):
                            dve.wait_ge(xn_ready, a)
                        for j in range(GB):
                            last = nc.vector.bn_stats(norms[0]["stat6"][:, j, :], x[:, bass.ds(GB * a + j, 1), :].rearrange("p o c -> p (o c)"))
                        last.then_inc(norms[0]["bn"], 1)
                        dve.wait_ge(norms[0]['bn'], a + 1)
                        nc.vector.tensor_copy(spare[:, :], norms[0]["stat6"][:, 0, 0:1])
                        for j in range(GB):
                            last = nc.vector.bn_aggr(norms[0]["mv"][:, j, :], norms[0]["stat6"][:, j, :])
                        last.then_inc(norms[0]["stats"], 1)
                    if E:
                        dve.wait_ge(trig, 2 * e + 2)
                        if counted(e):
                            dve.wait_ge(qe_ps, e)
                        nc.vector.tensor_tensor(qe[:, 0:GB * NQ].rearrange("p (a b) -> p a b", a=GB), th[:, :, :], cs[:, :, :], ALU.mult).then_inc(qe_ready, 1)
                    if C:
                        prepare_rows(g, 0)
                    if A:
                        dve.wait_ge(norms[0]['ready'], a + 1)
                        if counted(a - 2):
                            dve.wait_ge(resid_ready, a - 2)
                        for j in range(GB):
                            last = nc.vector.tensor_scalar(xn[:, ka, j, :], x[:, bass.ds(GB * a + j, 1), :].rearrange("p o c -> p (o c)"),
                                                           norms[0]["mv"][:, j, 0:1], norms[0]["rstd"][:, j:j + 1], ALU.subtract, ALU.mult)
                        last.then_inc(xn_ready, 1)
                    for j in range(GB):
                        if j == 2:
                            if DD:
                                dve.wait_ge(norms[1]['ready'], d + 1)
                                normalise(norms[1], r, r, xh_ready)
                            if E:
                                dve.wait_ge(norms[2]['ready'], e + 1)
                                if counted(e):
                                    dve.wait_ge(x_out, e)
                                normalise(norms[2], yh, y, yh_ready)
                        if B:
                            fidelity(g, b, j, 0)
                        if C and j < 3:
                            prepare_rows(g, j + 1)
                        if B:
                            fidelity(g, b, j, 1)
                            dve.wait_ge(f_sb, 8 * b + 2 * j + 2)
                            nc.vector.tensor_scalar(F[:, j, :, :], F[:, j, :, :], 1.0, -1.0, ALU.min, ALU.max).then_inc(f_clamped, 1)
                        if j == 1:
                            if DD:
                                dve.wait_ge(wo_ps, d + 1)
                                dve.wait_ge(resid_ready, d + 1)
                                if counted(d):
                                    dve.wait_ge(x1_scaled, d)
                                nc.vector.tensor_tensor(r[:, :, :], mB[:, :].rearrange("p (a b) -> p a b", a=GB), resid[:, :, :], ALU.add).then_inc(r_ready, 1)
                                statistics(dve, d, norms[1], r, r_ready, xh_ready)
                            if E:
                                dve.wait_ge(ff_ps, e + 1)
                                dve.wait_ge(x1b_ready, e + 1)
                                if counted(e):
                                    dve.wait_ge(yh_ready, e)
                                nc.vector.tensor_tensor(y[:, :, :], mA[:, :].rearrange("p (a b) -> p a b", a=GB), x1b[:, :, :], ALU.add).then_inc(y_ready, 1)
                                statistics(dve, e, norms[2], y, y_ready, yh_ready)
                        if j == 2 and A:
                            dve.wait_ge(v_ps, a + 1)
                            if counted(4 * (a - 2)):
                                dve.wait_ge(o_ps, 4 * (a - 2))
                            nc.vector.tensor_tensor(V[:, ka, :, :], mB[:, :].rearrange("p (a b) -> p a b", a=GB),
                                                    bv[:, :].unsqueeze(1).broadcast_to([P, GB, D]), ALU.add).then_inc(v_sb, 1)
                        if j == 3 and DD:
                            dve.wait_ge(qm_ps, d + 1)
                            if counted(2 * d):
                                dve.wait_ge(trig, 2 * d)
                            nc.vector.tensor_tensor(qm[:, :, :], mB[:, 0:GB * NQ].rearrange("p (a b) -> p a b", a=GB),
                                                    env["b_in"][:, :].unsqueeze(1).broadcast_to([P, GB, NQ]), ALU.add).then_inc(qm_sb, 1)
                            dve.wait_ge(qm_sb, d + 1)
                            nc.vector.tensor_scalar(u[:, :, :], qm[:, :, :], 0.125, MAGIC, ALU.mult, ALU.add).then_inc(v_chain, 1)
                            dve.wait_ge(v_chain, 4 * d + 1)
                            nc.vector.tensor_scalar(u[:, :, :], u[:, :, :], MAGIC, 0.0, ALU.subtract, ALU.add).then_inc(v_chain, 1)
                            dve.wait_ge(v_chain, 4 * d + 2)
                            nc.vector.scalar_tensor_tensor(u[:, :, :], qm[:, :, :], 0.125, u[:, :, :], ALU.mult, ALU.subtract).then_inc(v_chain, 1)
                            dve.wait_ge(v_chain, 4 * d + 3)
                            nc.vector.scalar_tensor_tensor(v[:, :, :], u[:, :, :], -1.0, u[:, :, :], ALU.mult, ALU.max).then_inc(v_chain, 1)
                        if C:
                            n = GB * g + j
                            dve.wait_ge(p_sb, n + 1)
                            if counted(n):
                                dve.wait_ge(o_sb, n)
                            nc.vector.reciprocal(rrec[:, :], rsum[:, j % 2, :]).then_inc(rr_sb, 1)
                            dve.wait_ge(rr_sb, n + 1)
                            dve.wait_ge(o_ps, n + 1)
                            if counted(g):
                                dve.wait_ge(oT_ps, g)
                            nc.vector.tensor_tensor(on[:, j, :, :], o_b[:, j, :, :], rrec[:, :].unsqueeze(2).broadcast_to([P, H, HD]), ALU.mult).then_inc(o_sb, 1)
                    if A:
                        dve.wait_ge(qn_sb, a + 1)
                        nc.vector.tensor_scalar(rq[:, :], qn[:, ka, :], TINY, 1.0, ALU.max, ALU.mult).then_inc(norm_chain, 1)
                        dve.wait_ge(kn_sb, a + 1)
                        nc.vector.tensor_scalar(rk[:, :], kn16[:, :], TINY, 1.0, ALU.max, ALU.mult).then_inc(norm_chain, 1)
                        dve.wait_ge(norm_chain, 4 * a + 2)
                        nc.vector.reciprocal(rq[:, :], rq[:, :]).then_inc(norm_chain, 1)
                        nc.vector.reciprocal(rk[:, :], rk[:, :]).then_inc(norm_chain, 1)
                        dve.wait_ge(norm_chain, 4 * a + 4)
                        nc.vector.scalar_tensor_tensor(kqf[:, :], kqf[:, :], 1.0 / (16 * EPS_COS), rk[:, :], ALU.mult, ALU.mult).then_inc(kqn_ready, 1)
                        nc.vector.tensor_tensor(qqn[:, ka, :], qqf[:, :], rq[:, :], ALU.mult).then_inc(qqn_ready, 1)

                loop(dve, iteration)

            @block.tensor
            def _(pe):
                pe.wait_ge(weights_in, 16 * N_WEIGHTS)
                pe.wait_ge(placed, 16 * 3 * H)
                pe.wait_ge(zeroed, N_ZEROED)

                def scores(g, k, j):
                    n = GB * g + j
                    if counted(16 * H * (g + 1)):
                        pe.wait_ge(K_in, 16 * H * (g + 1))
                    if counted(n):
                        pe.wait_ge(a_sb, n)
                    for half in range(2):
                        hs = slice(4 * half, 4 * half + 4)
                        last = nc.tensor.matmul(s_b[:, hs, :], qf[:, k, j * S:(j + 1) * S], K_spread[:, hs, j * S:(j + 1) * S], start=True, stop=True)
                    last.then_inc(s_ps, 1)

                def fidelity_products(b, kb, j, half):
                    pe.wait_ge(C_in, 16 * H * (b + 1))
                    pe.wait_ge(N_in, 16 * H * (b + 1))
                    pe.wait_ge(qqn_ready, b + 1)
                    if counted(8 * b + 2 * j + half):
                        pe.wait_ge(f_sb, 8 * b + 2 * j + half)
                    hs, js = slice(4 * half, 4 * half + 4), slice(j * S, (j + 1) * S)
                    nc.tensor.matmul(cos_b[:, :, :], qqn[:, kb, js], C_spread[:, hs, js], start=True, stop=True)
                    nc.tensor.matmul(den_b[:, :, :], qn[:, kb, js], N_spread[:, hs, js], start=True, stop=True).then_inc(cd_ps, 1)

                def transposed(g, j, half):
                    n = GB * g + j
                    pe.wait_ge(p_sb, n + 1)
                    if counted(2 * n + half):
                        pe.wait_ge(pt_sb, 2 * n + half)
                    for h in range(4):
                        last = nc.tensor.transpose(pt_b[:, h, :], Pr[:, j % 2, 4 * half + h, :], ident[:, :])
                    last.then_inc(t_ps, 1)

                def four_transposes(bank, src, done):
                    for j in range(GB):
                        last = nc.tensor.transpose(bank[:, j * S:(j + 1) * S], src[:, j, :], ident[:, :])
                    last.then_inc(done, 1)

                def iteration(g, k):
                    a, b, d, e, ka, kb = g + 2, g + 1, g - 1, g - 2, (k + 2) % 3, (k + 1) % 3
                    A, B, C, DD, E = (does(g, s, N) for s in (2, 1, 0, -1, -2))
                    A_done = through(g, 2, N)
                    D_done, E_done = through(g, -1, N), through(g, -2, N)
                    if C:
                        scores(g, k, 0)
                    for j in range(GB):
                        if B:
                            fidelity_products(b, kb, j, 0)
                        if C:
                            transposed(g, j, 0)
                            if j < 3:
                                scores(g, k, j + 1)
                            transposed(g, j, 1)
                        if B:
                            fidelity_products(b, kb, j, 1)
                        if j == 0:
                            if counted(before(g, 2, N)):
                                pe.wait_ge(qn_sb, before(g, 2, N))
                            if counted(before(g, 2, N)):
                                pe.wait_ge(kn_sb, before(g, 2, N))
                            if counted(before(g, -1, N)):
                                pe.wait_ge(qm_sb, before(g, -1, N))
                            if counted(before(g, -2, N)):
                                pe.wait_ge(y_ready, before(g, -2, N))
                            if DD:
                                pe.wait_ge(o_sb, GB * d + GB)
                                four_transposes(mB, on[:, :, :, :].rearrange("p a h c -> p a (h c)"), oT_ps)
                            if A:
                                pe.wait_ge(xn_ready, a + 1)
                                four_transposes(mA, xn[:, ka, :, :], xnT_ps)
                            if E:
                                pe.wait_ge(qe_ready, e + 1)
                                if counted(A_done):
                                    pe.wait_ge(xnT_sb, A_done)
                                nc.tensor.transpose(mA[:, 0:P], qe[:, :], ident[:, :]).then_inc(qe_ps, 1)
                        if j == 1:
                            if A:
                                pe.wait_ge(xnT_sb, a + 1)
                                if counted(D_done):
                                    pe.wait_ge(oT_sb, D_done)
                                nc.tensor.matmul(mB[:, :], wq[:, :], xnT[:, :], start=True, stop=True).then_inc(q_ps, 1)
                                if counted(E_done):
                                    pe.wait_ge(qeT_sb, E_done)
                                nc.tensor.matmul(mA[:, :], wk[:, :], xnT[:, :], start=True, stop=True).then_inc(k_ps, 1)
                            if DD:
                                pe.wait_ge(oT_sb, d + 1)
                                if counted(A_done):
                                    pe.wait_ge(q_sb, A_done)
                                for i in range(GB):
                                    last = nc.tensor.matmul(mB[:, i * D:(i + 1) * D], oT[:, i, :], wo[:, :], start=True, stop=True)
                                last.then_inc(wo_ps, 1)
                            if E:
                                pe.wait_ge(qeT_sb, e + 1)
                                if counted(A_done):
                                    pe.wait_ge(k_sb, A_done)
                                nc.tensor.matmul(mA[:, :], qeT[:, :], env["w_out"][:, :, :], start=True, stop=True).then_inc(ff_ps, 1)
                        if j == 2:
                            if A:
                                pe.wait_ge(q_sb, a + 1)
                                if counted(D_done):
                                    pe.wait_ge(r_ready, D_done)
                                for i in range(GB):
                                    last = nc.tensor.matmul(mB[:, i * D:(i + 1) * D], xnT[:, i * S:(i + 1) * S], wv[:, :], start=True, stop=True)
                                last.then_inc(v_ps, 1)
                                pe.wait_ge(k_sb, a + 1)
                                if counted(E_done):
                                    pe.wait_ge(y_ready, E_done)
                                nc.tensor.matmul(mA[:, :], wc[:, :], qf[:, ka, :], start=True, stop=True).then_inc(qq_ps, 1)
                                pe.wait_ge(qq_sb, a + 1)
                                nc.tensor.matmul(mA[:, :], wc[:, :], kf[:, ka, :], start=True, stop=True).then_inc(kq_ps, 1)
                            if DD:
                                pe.wait_ge(x1_ready, d + 1)
                                if counted(A_done):
                                    pe.wait_ge(v_sb, A_done)
                                pe.wait_ge(r_ready, d + 1)
                                four_transposes(mB, x1, xt_ps)
                        if j == 3:
                            if A:
                                pe.wait_ge(q2_ready, a + 1)
                                pe.wait_ge(kq_sb, a + 1)
                                nc.tensor.matmul(mA[:, :], blocks[:, :], rq[:, :], start=True, stop=True).then_inc(ssq_ps, 1)
                            if DD:
                                pe.wait_ge(xt_sb, d + 1)
                                for i in range(GB):
                                    last = nc.tensor.matmul(mB[:, i * NQ:(i + 1) * NQ], x1T[:, i, :], env["w_in"][:, :], start=True, stop=True)
                                last.then_inc(qm_ps, 1)
                            if A:
                                pe.wait_ge(k2_ready, a + 1)
                                pe.wait_ge(v_sb, a + 1)
                                if counted(D_done):
                                    pe.wait_ge(qm_sb, D_done)
                                nc.tensor.matmul(mB[:, :], blocks[:, :], rk[:, :], start=True, stop=True).then_inc(ssk_ps, 1)
                        if C:
                            n = GB * g + j
                            pe.wait_ge(pt_sb, 2 * n + 2)
                            pe.wait_ge(v_sb, g + 1)
                            if counted(n):
                                pe.wait_ge(o_sb, n)
                            for h in range(H):
                                last = nc.tensor.matmul(o_b[:, j, h, :], PT[:, h, :], V[:, k, j, h * HD:(h + 1) * HD], start=True, stop=True)
                            last.then_inc(o_ps, 1)

                loop(pe, iteration)


EXPERTS, INNER = 8, 352


def experts(nc, env, n_groups, w):
    x, ident = env["x"], env["ident"]
    rows = [min(P, INNER - P * c) for c in range(-(-INNER // P))]
    CH = len(rows)
    PARTS = EXPERTS * CH
    LAG = 2
    N = n_groups
    ctx = ExitStack()
    with ctx:
        def sb(n, shape, dt=F32):
            return ctx.enter_context(nc.sbuf_tensor(f"moe_{n}", shape, dt))

        def ps(n, shape, dt=F32):
            return ctx.enter_context(nc.psum_tensor(f"moe_{n}", shape, dt))

        def sem(n):
            return nc.alloc_semaphore(f"moe_{n}")

        gate, up = sb("gate", [D, EXPERTS, INNER]), sb("up", [D, EXPERTS, INNER])
        down = sb("down", [P, CH, EXPERTS, D])
        router = sb("router", [D, EXPERTS])
        pick = sb("pick", [P, EXPERTS, P], BF16)
        rank = sb("rank", [P, EXPERTS])
        minus_half, eps = sb("minus_half", [P, GB]), sb("eps", [P, GB])
        stat6, mv, vare, rstd, spare = sb("stat6", [P, GB, 6]), sb("mv", [P, GB, 2]), sb("vare", [P, GB]), sb("rstd", [P, GB]), sb("spare", [P, 1])
        xn = sb("xn", [P, GB, D])
        xnT = sb("xnT", [D, 3, T])
        top, score, first = sb("top", [P, GB]), sb("score", [P, GB, EXPERTS]), sb("first", [P, GB])
        chosen = sb("chosen", [P, GB, P])
        chosenT = sb("chosenT", [P, 3, T], BF16)
        mine = sb("mine", [D, 2, T])
        gated, hid = sb("gated", [P, 2, T]), sb("hid", [P, 4, T])
        yT = sb("yT", [D, GB, S])

        m_b, pick_b = ps("m_b", [P, 512]), ps("pick_b", [P, 512])
        g_b, u_b = [ps(f"g_b{i}", [P, 512]) for i in range(2)], [ps(f"u_b{i}", [P, 512]) for i in range(2)]
        y_b, out_b = ps("y_b", [P, 512]), ps("out_b", [P, GB, D])

        weights_in, consts, bn_done, stats, var_ready, rstd_ready, xn_ready = (
            sem(n) for n in ("weights_in", "consts", "bn_done", "stats", "var_ready", "rstd_ready", "xn_ready"))
        xnT_ps, xnT_sb, logits_ps, top_sb, score_sb, first_sb, chosen_sb, chosen_ps, chosenT_sb = (
            sem(n) for n in ("xnT_ps", "xnT_sb", "logits_ps", "top_sb", "score_sb", "first_sb", "chosen_sb", "chosen_ps", "chosenT_sb"))
        pick_ps, mine_sb, g_ps, u_ps, gated_sb, hid_sb, d_ps, yT_sb, y_ps, x_out = (
            sem(n) for n in ("pick_ps", "mine_sb", "g_ps", "u_ps", "gated_sb", "hid_sb", "d_ps", "yT_sb", "y_ps", "x_out"))
        N_WEIGHTS = 3 + CH

        with nc.Block() as block:

            @block.sync
            def _(sp):
                sp.dma_start(gate[:, :, :], w["gate"]).then_inc(weights_in, 16)
                sp.dma_start(up[:, :, :], w["up"]).then_inc(weights_in, 16)
                sp.dma_start(router[:, :], w["router"]).then_inc(weights_in, 16)
                for c in range(CH):
                    sp.dma_start(down[0:rows[c], c, :, :], w["down"][c * P:c * P + rows[c], :, :]).then_inc(weights_in, 16)
                sp.wait_ge(weights_in, 16 * N_WEIGHTS)

            @block.gpsimd
            def _(pool):
                nc.gpsimd.memset(minus_half[:, :], -0.5).then_inc(consts, 1)
                nc.gpsimd.memset(eps[:, :], LN_EPS).then_inc(consts, 1)
                for e in range(EXPERTS):
                    nc.gpsimd.memset(rank[:, e:e + 1], float(EXPERTS - e)).then_inc(consts, 1)
                pool.wait_ge(consts, 4 + EXPERTS)

                def iteration(g, k):
                    a = g + 1
                    if does(g, 1, N):
                        pool.wait_ge(stats, a + 1)
                        nc.gpsimd.tensor_tensor(vare[:, :], mv[:, :, 1], eps[:, :], ALU.add).then_inc(var_ready, 1)
                        pool.wait_ge(var_ready, a + 1)
                        nc.gpsimd.tensor_tensor(rstd[:, :], vare[:, :], minus_half[:, :], ALU.pow).then_inc(rstd_ready, 1)

                groups_loop(pool, N, iteration)

            @block.scalar
            def _(act):
                act.wait_ge(weights_in, 16 * N_WEIGHTS)

                def iteration(g, k):
                    a, ka = g + 1, (k + 1) % 3
                    A, B = does(g, 1, N), does(g, 0, N)
                    for m in range(PARTS):
                        n = PARTS * g + m
                        if B:
                            r = rows[m % CH]
                            act.wait_ge(g_ps, n + 1)
                            if counted(n - 1):
                                act.wait_ge(hid_sb, n - 1)
                            nc.scalar.activation(gated[0:r, m % 2, :], g_b[m % 2][0:r, :], ACT.Silu).then_inc(gated_sb, 1)
                        if A and m == 4:
                            act.wait_ge(xnT_ps, a + 1)
                            if counted(EXPERTS * (a - 2)):
                                act.wait_ge(mine_sb, EXPERTS * (a - 2))
                            nc.scalar.activation(xnT[:, ka, :], m_b[:, :], ACT.Copy).then_inc(xnT_sb, 1)
                        if A and m == 13:
                            act.wait_ge(chosen_ps, a + 1)
                            if counted(EXPERTS * (a - 2)):
                                act.wait_ge(pick_ps, EXPERTS * (a - 2))
                            nc.scalar.activation(chosenT[:, ka, :], m_b[:, :], ACT.Copy).then_inc(chosenT_sb, 1)
                    if B:
                        act.wait_ge(d_ps, PARTS * g + PARTS)
                        if counted(g):
                            act.wait_ge(y_ps, g)
                        nc.scalar.activation(yT[:, :, :].rearrange("p a b -> p (a b)"), y_b[:, :], ACT.Copy).then_inc(yT_sb, 1)

                groups_loop(act, N, iteration)

            @block.vector
            def _(dve):
                nc.vector.memset(chosen[:, :, :], 0.0).then_inc(consts, 1)
                nc.vector.tensor_copy(pick[:, :, :], ident[:, 0:EXPERTS].unsqueeze(2).broadcast_to([P, EXPERTS, P])).then_inc(consts, 1)
                dve.wait_ge(consts, 4 + EXPERTS)

                def take(n, e, k):
                    dve.wait_ge(pick_ps, n + 1)
                    if counted(CH * (n - 1)):
                        dve.wait_ge(u_ps, CH * (n - 1))
                    nc.vector.tensor_tensor(mine[:, e % 2, :], xnT[:, k, :], pick_b[:, :], ALU.mult).then_inc(mine_sb, 1)

                def iteration(g, k):
                    a, ka = g + 1, (k + 1) % 3
                    A, B = does(g, 1, N), does(g, 0, N)
                    for m in range(PARTS):
                        n = PARTS * g + m
                        if B and m % CH == 1 and m // CH + 1 < EXPERTS:
                            e = m // CH + 1
                            take(EXPERTS * g + e, e, k)
                        if A and m == 0:
                            if counted(a):
                                dve.wait_ge(xn_ready, a)
                            for j in range(GB):
                                last = nc.vector.bn_stats(stat6[:, j, :], x[:, bass.ds(GB * a + j, 1), :].rearrange("p o c -> p (o c)"))
                            last.then_inc(bn_done, 1)
                            dve.wait_ge(bn_done, a + 1)
                            nc.vector.tensor_copy(spare[:, :], stat6[:, 0, 0:1])
                            for j in range(GB):
                                last = nc.vector.bn_aggr(mv[:, j, :], stat6[:, j, :])
                            last.then_inc(stats, 1)
                        if A and m == 2:
                            dve.wait_ge(rstd_ready, a + 1)
                            if counted(a):
                                dve.wait_ge(xnT_ps, a)
                            for j in range(GB):
                                last = nc.vector.tensor_scalar(xn[:, j, :], x[:, bass.ds(GB * a + j, 1), :].rearrange("p o c -> p (o c)"),
                                                               mv[:, j, 0:1], rstd[:, j:j + 1], ALU.subtract, ALU.mult)
                            last.then_inc(xn_ready, 1)
                        if A and m == 8:
                            logits = m_b[:, 0:GB * EXPERTS].rearrange("p (a b) -> p a b", a=GB)
                            dve.wait_ge(logits_ps, a + 1)
                            nc.vector.tensor_reduce(top[:, :], logits, axis=AX.X, op=ALU.max).then_inc(top_sb, 1)
                            dve.wait_ge(top_sb, a + 1)
                            nc.vector.tensor_tensor(score[:, :, :], logits, top[:, :].unsqueeze(2).broadcast_to([P, GB, EXPERTS]), ALU.is_equal).then_inc(score_sb, 1)
                            dve.wait_ge(score_sb, 2 * a + 1)
                            nc.vector.tensor_tensor(score[:, :, :], score[:, :, :], rank[:, :].unsqueeze(1).broadcast_to([P, GB, EXPERTS]), ALU.mult).then_inc(score_sb, 1)
                            dve.wait_ge(score_sb, 2 * a + 2)
                            nc.vector.tensor_reduce(first[:, :], score[:, :, :], axis=AX.X, op=ALU.max).then_inc(first_sb, 1)
                            dve.wait_ge(first_sb, a + 1)
                            if counted(a):
                                dve.wait_ge(chosen_ps, a)
                            nc.vector.tensor_tensor(chosen[:, :, 0:EXPERTS], score[:, :, :], first[:, :].unsqueeze(2).broadcast_to([P, GB, EXPERTS]), ALU.is_equal).then_inc(chosen_sb, 1)
                        if B:
                            r = rows[m % CH]
                            dve.wait_ge(gated_sb, n + 1)
                            dve.wait_ge(u_ps, n + 1)
                            if counted(n - 3):
                                dve.wait_ge(d_ps, n - 3)
                            nc.vector.tensor_tensor(hid[0:r, m % 4, :], gated[0:r, m % 2, :], u_b[m % 2][0:r, :], ALU.mult).then_inc(hid_sb, 1)
                    if A:
                        take(EXPERTS * a, 0, ka)
                    if B:
                        dve.wait_ge(y_ps, g + 1)
                        xg = x[:, bass.ds(GB * g, GB), :]
                        nc.vector.tensor_tensor(xg, xg, out_b[:, :, :], ALU.add).then_inc(x_out, 1)

                groups_loop(dve, N, iteration)
                dve.wait_ge(x_out, N)

            @block.tensor
            def _(pe):
                pe.wait_ge(weights_in, 16 * N_WEIGHTS)
                pe.wait_ge(consts, 4 + EXPERTS)

                def pick_expert(n, e, k):
                    if counted(n):
                        pe.wait_ge(mine_sb, n)
                    nc.tensor.matmul(pick_b[:, :], pick[:, e, :], chosenT[:, k, :], start=True, stop=True).then_inc(pick_ps, 1)

                def lower(g, m):
                    r = rows[m % CH]
                    pe.wait_ge(hid_sb, PARTS * g + m + 1)
                    if m == 0:
                        if counted(g):
                            pe.wait_ge(yT_sb, g)
                    nc.tensor.matmul(y_b[:, :], down[0:r, m % CH, m // CH, :], hid[0:r, m % 4, :],
                                     start=(m == 0), stop=(m == PARTS - 1)).then_inc(d_ps, 1)

                def iteration(g, k):
                    a, ka = g + 1, (k + 1) % 3
                    A, B = does(g, 1, N), does(g, 0, N)
                    for m in range(PARTS):
                        n = PARTS * g + m
                        if B:
                            e, c = m // CH, m % CH
                            r = rows[c]
                            pe.wait_ge(mine_sb, EXPERTS * g + e + 1)
                            if counted(n - 1):
                                pe.wait_ge(gated_sb, n - 1)
                            nc.tensor.matmul(g_b[m % 2][0:r, :], gate[:, e, c * P:c * P + r], mine[:, e % 2, :], start=True, stop=True).then_inc(g_ps, 1)
                            if counted(n - 1):
                                pe.wait_ge(hid_sb, n - 1)
                            nc.tensor.matmul(u_b[m % 2][0:r, :], up[:, e, c * P:c * P + r], mine[:, e % 2, :], start=True, stop=True).then_inc(u_ps, 1)
                            if c == 0 and e + 1 < EXPERTS:
                                pick_expert(EXPERTS * g + e + 1, e + 1, k)
                            if m >= LAG:
                                lower(g, m - LAG)
                        if A and m == 3:
                            pe.wait_ge(xn_ready, a + 1)
                            if counted(a):
                                pe.wait_ge(chosenT_sb, a)
                            for j in range(GB):
                                last = nc.tensor.transpose(m_b[:, j * S:(j + 1) * S], xn[:, j, :], ident[:, :])
                            last.then_inc(xnT_ps, 1)
                        if A and m == 6:
                            pe.wait_ge(xnT_sb, a + 1)
                            for j in range(GB):
                                last = nc.tensor.matmul(m_b[:, j * EXPERTS:(j + 1) * EXPERTS], xnT[:, ka, j * S:(j + 1) * S], router[:, :], start=True, stop=True)
                            last.then_inc(logits_ps, 1)
                        if A and m == 12:
                            pe.wait_ge(chosen_sb, a + 1)
                            for j in range(GB):
                                last = nc.tensor.transpose(m_b[:, j * S:(j + 1) * S], chosen[:, j, :], ident[:, :])
                            last.then_inc(chosen_ps, 1)
                    if A:
                        pe.wait_ge(chosenT_sb, a + 1)
                        pick_expert(EXPERTS * a, 0, ka)
                    if B:
                        for m in range(PARTS - LAG, PARTS):
                            lower(g, m)
                        pe.wait_ge(yT_sb, g + 1)
                        if counted(g):
                            pe.wait_ge(x_out, g)
                        for j in range(GB):
                            last = nc.tensor.transpose(out_b[:, j, :], yT[:, j, :], ident[:, :])
                        last.then_inc(y_ps, 1)

                groups_loop(pe, N, iteration)


def load(nc, env, x_in, n_seqs):
    x, ident = env["x"], env["ident"]
    ctx = ExitStack()
    with ctx:
        loaded, ident_set = (nc.alloc_semaphore(f"load_{n}") for n in ("loaded", "ident_set"))
        with nc.Block() as block:

            @block.sync
            def _(sp):
                part = n_seqs // 8
                for i in range(8):
                    r = slice(i * part, (i + 1) * part)
                    sp.dma_start(x[:, r, :], x_in[r, :, :].rearrange("b s c -> s b c")).then_inc(loaded, 16)
                sp.wait_ge(loaded, 16 * 8)

            @block.gpsimd
            def _(pool):
                nc.gpsimd.memset(ident[:, :], 0.0).then_inc(ident_set, 1)
                pool.wait_ge(ident_set, 1)
                nc.gpsimd.affine_select(out=ident[:, :], in_=ident[:, :], compare_op=ALU.not_equal, fill=1.0,
                                        base=0, pattern=[[-1, P]], channel_multiplier=1).then_inc(ident_set, 1)
                pool.wait_ge(ident_set, 2)


def prepare_stacks(nc, env, name):
    QST, KST = env["QST"], env["KST"]
    ctx = ExitStack()
    with ctx:
        ones = ctx.enter_context(nc.sbuf_tensor(f"{name}_ones", [2, T], BF16))
        ones_set, stacks_zero, rows_set = (nc.alloc_semaphore(f"{name}_prepare_{n}") for n in ("ones_set", "stacks_zero", "rows_set"))
        with nc.Block() as block:

            @block.sync
            def _(sp):
                sp.wait_ge(ones_set, 1)
                sp.wait_ge(stacks_zero, 2)
                for p in range(2):
                    r = HALF * p + ROWS
                    sp.dma_start(KST[r:r + 2, :, :, :].rearrange("r a g n -> r (a g) n"),
                                 ones[:, :].unsqueeze(1).broadcast_to([2, 3 * H16 // 2, T])).then_inc(rows_set, 16)
                    sp.dma_start(QST[r + 2:r + 3, :, :, :].rearrange("r a h n -> r (a h) n")[:, p::2, :],
                                 ones[0:1, :].unsqueeze(1).broadcast_to([1, 3 * H16 // 2, T])).then_inc(rows_set, 16)
                sp.wait_ge(rows_set, 64)

            @block.gpsimd
            def _(pool):
                nc.gpsimd.memset(ones[:, :], 1.0).then_inc(ones_set, 1)
                pool.wait_ge(ones_set, 1)

            @block.vector
            def _(dve):
                nc.vector.memset(QST[:, :, :, :].rearrange("p a h n -> p (a h n)").bitcast(F32), 0.0).then_inc(stacks_zero, 1)
                nc.vector.memset(KST[:, :, :, :].rearrange("p a h n -> p (a h n)").bitcast(F32), 0.0).then_inc(stacks_zero, 1)
                dve.wait_ge(stacks_zero, 2)


def store(nc, env, out, n_seqs):
    x = env["x"]
    ctx = ExitStack()
    with ctx:
        stored = nc.alloc_semaphore("stored")
        with nc.Block() as block:

            @block.sync
            def _(sp):
                part = n_seqs // 8
                for i in range(8):
                    r = slice(i * part, (i + 1) * part)
                    sp.dma_start(out[r, :, :].rearrange("b s c -> s b c"), x[:, r, :]).then_inc(stored, 16)
                sp.wait_ge(stored, 16 * 8)


def plain_phase(nc, env, n_groups, name, a, names, cross, mask):
    wq, bq, wk, bk, wv, bv, wo, bo = names
    weights = dict(wq=a[wq], wk=a[wk], wv=a[wv], wo=a[wo], bq=a[bq].unsqueeze(1), bk=a[bk].unsqueeze(1), bv=a[bv].unsqueeze(0), bo=a[bo].unsqueeze(0))
    if cross:
        weights["context"] = a["ctx_1024"]
    if mask == "given":
        weights["mask"] = a["mask_Bx1x1xS2_bk0"].rearrange("b i j t -> i (b j t)")
    ctx = ExitStack()
    with ctx:
        env = dict(env)
        env["QST"] = ctx.enter_context(nc.sbuf_tensor(f"{name}_QST", [P, 3, H16, T], BF16))
        env["KST"] = ctx.enter_context(nc.sbuf_tensor(f"{name}_KST", [P, 3, H16 // 2, T], BF16))
        prepare_stacks(nc, env, name)
        plain_attention(nc, env, name, n_groups, cross, weights, mask)


def build(nc, a, out, n_seqs=64, phases=("a0", "x0", "moe", "a1", "x1", "ffn")):
    ctx = ExitStack()
    with ctx:
        env = {
            "x": ctx.enter_context(nc.sbuf_tensor("x", [P, n_seqs, D], F32)),
            "ident": ctx.enter_context(nc.sbuf_tensor("ident", [P, P], F32)),
        }
        n_groups = n_seqs // GB
        with nc.cleanup_on_exit():
            load(nc, env, a["x"], n_seqs)
        if "a0" in phases:
            with nc.cleanup_on_exit():
                w = {n: a[f"L0_attn_{n}"] for n in ("Wq", "Wk", "Wv", "Wo", "Wc2q", "bc2q", "Wm", "W2", "b1", "bqo", "bm", "b2")}
                w.update({n: a[f"L0_attn_{n}"].unsqueeze(0) for n in ("bo", "g1", "beta1", "g2", "beta2")})
                w.update(W1T=a["L0_attn_W1"], WqoT=a["L0_attn_Wqo"], bq=a["L0_attn_bq"].rearrange("h d -> (h d)").unsqueeze(1),
                         bk=a["L0_attn_bk"].rearrange("h d -> (h d)").unsqueeze(1), bv=a["L0_attn_bv"].rearrange("h d -> (h d)").unsqueeze(0))
                quantum_block(nc, env, n_groups, w)
        if "x0" in phases:
            with nc.cleanup_on_exit():
                plain_phase(nc, env, n_groups, "x0", a, [f"L0_xattn_{n}" for n in ("Wq", "bq", "Wk", "bk", "Wv", "bv", "Wo", "bo")], True, None)
        if "moe" in phases:
            with nc.cleanup_on_exit():
                experts(nc, env, n_groups, dict(router=a["L0_ffn_router_w"], gate=a["L0_ffn_gate_w"], up=a["L0_ffn_up_w"], down=a["L0_ffn_down_w"]))
        if "a1" in phases:
            with nc.cleanup_on_exit():
                plain_phase(nc, env, n_groups, "a1", a, [f"L1_attn_{n}" for n in ("wq_w", "wq_b", "wk_w", "wk_b", "wv_w", "wv_b", "wo_w", "wo_b")], False, "zero_key")
        if "x1" in phases:
            with nc.cleanup_on_exit():
                plain_phase(nc, env, n_groups, "x1", a, [f"L1_xattn_{n}" for n in ("Wq", "bq", "Wk", "bk", "Wv", "bv", "Wc", "bc")], True, "given")
        if "ffn" in phases:
            with nc.cleanup_on_exit():
                ternary_ffn(nc, env, n_groups, dict(w1=a["L1_ffn_w1"], w2=a["L1_ffn_w2"], b1=a["L1_ffn_b1"].unsqueeze(0), b2=a["L1_ffn_b2"].unsqueeze(0)))
        store(nc, env, out, n_seqs)


TRANSPOSED = {"L1_attn_wq_w", "L1_attn_wk_w", "L1_attn_wv_w", "L1_attn_wo_w", "L1_xattn_Wq", "L1_xattn_Wk", "L1_xattn_Wv", "L1_xattn_Wc",
              "L1_ffn_w1", "L1_ffn_w2", "L0_attn_W1", "L0_attn_Wqo", "L0_ffn_router_w"}


def layout(name, value):
    if name in TRANSPOSED:
        value = value.T
    elif name in ("L0_attn_Wq", "L0_attn_Wk", "L0_attn_Wv"):
        value = value.transpose(1, 0, 2).reshape(D, D)
    elif name in ("L0_ffn_gate_w", "L0_ffn_up_w"):
        value = value.transpose(2, 0, 1)
    elif name == "L0_ffn_down_w":
        value = value.transpose(2, 0, 1)
    return np.ascontiguousarray(value)


def kernel(**inputs):
    import concourse.bacc as bacc
    from concourse.bass_utils import run_bass_kernel_spmd

    nc = bacc.Bacc("TRN2", target_bir_lowering=False, num_devices=1)
    arrays, args = {}, {}
    for name, value in inputs.items():
        arrays[f"in_{name}"] = layout(name, np.asarray(value))
        args[name] = nc.dram_tensor(f"in_{name}", arrays[f"in_{name}"].shape, mybir.dt.from_np(arrays[f"in_{name}"].dtype), kind="ExternalInput").ap()
    shape = inputs["x"].shape
    out = nc.dram_tensor("out", shape, F32, kind="ExternalOutput").ap()
    build(nc, args, out, n_seqs=shape[0])
    return run_bass_kernel_spmd(nc, [arrays], core_ids=[0]).results[0]["out"]
```

```python
import math
from contextlib import ExitStack

import numpy as np

import concourse.bass as bass
from concourse import mybir

F32 = mybir.dt.float32
BF16 = mybir.dt.bfloat16
ALU = mybir.AluOpType
ACT = mybir.ActivationFunctionType
AX = mybir.AxisListType

P = 128
D = 128
S = 128
GB = 4
T = GB * S
LN_EPS = 1e-5
H16, HD8 = 16, 8
TERMS = 6
ROWS = HD8 * TERMS
HALF = 64
MASKED = -(2.0 ** 100)


def counted(value):
    return not isinstance(value, int) or value > 0


def groups_loop(eng, n_groups, iteration, ahead=2, after=0):
    first = max(2, 1 + after)
    for g in range(-ahead, first):
        iteration(g, g % 3)
    rounds = max(0, (n_groups - ahead - first) // 3)
    if rounds > 1:
        with eng.Fori(0, rounds) as r:
            for j in range(3):
                iteration(3 * r + (first + j), (first + j) % 3)
    else:
        for g in range(first, first + 3 * rounds):
            iteration(g, g % 3)
    for g in range(first + 3 * rounds, n_groups + after):
        iteration(g, g % 3)


def does(g, ahead, n_groups):
    return not isinstance(g, int) or 0 <= g + ahead < n_groups


def before(g, ahead, n_groups):
    return min(max(g + ahead, 0), n_groups) if isinstance(g, int) else g + ahead


def through(g, ahead, n_groups):
    return before(g + 1, ahead, n_groups)


def plain_attention(nc, env, name, n_groups, cross, w, mask):
    x, ident, QST, KST = env["x"], env["ident"], env["QST"], env["KST"]
    TK = 77 if cross else S
    NK = GB * TK
    chunks = [(0, 6), (6, 12), (12, 16)] if cross else [(0, 4), (4, 8), (8, 12), (12, 16)]
    NCH = len(chunks)
    PAIRS = H16 // 2
    ctx = ExitStack()
    with ctx:
        def sb(n, shape, dt=F32):
            return ctx.enter_context(nc.sbuf_tensor(f"{name}_{n}", shape, dt))

        def ps(n, shape):
            return ctx.enter_context(nc.psum_tensor(f"{name}_{n}", shape, F32))

        def sem(n):
            return nc.alloc_semaphore(f"{name}_{n}")

        wq, wk, wv, wo = (sb(n, [D, D]) for n in ("wq", "wk", "wv", "wo"))
        bq, bk = sb("bq", [D, 1]), sb("bk", [D, 1])
        bqs = sb("bqs", [D, 1])
        bv, bo = sb("bv", [P, D]), sb("bo", [P, D])
        stat6 = sb("stat6", [P, GB, 6])
        mv = sb("mv", [P, GB, 2])
        spare = sb("spare", [P, 1])
        vare = sb("vare", [P, GB])
        minus_half = sb("minus_half", [P, GB])
        eps = sb("eps", [P, GB])
        rstd = sb("rstd", [P, GB])
        xn = sb("xn", [P, GB, D])
        xnT = sb("xnT", [D, T])
        qf, kf = sb("qf", [D, T]), sb("kf", [D, NK])
        r1q, r1k = sb("r1q", [D, T]), sb("r1k", [D, NK])
        q3, k3 = sb("q3", [D, 3, T], BF16), sb("k3", [D, 3, NK], BF16)
        V9 = sb("V9", [P, 3, GB, H16, HD8 + 1])
        negm = sb("negm", [P, 2, H16, GB])
        mT = sb("mT", [GB * H16, 2, S], BF16)
        PR = sb("PR", [P, GB, H16, S])
        rs = sb("rs", [P, 2, H16])
        On = sb("On", [P, GB, H16, HD8])
        oT = sb("oT", [D, T])
        zero2 = sb("zero2", [2, T], BF16)
        mrow = sb("mrow", [1, 3, T], BF16) if mask == "zero_key" else None
        if cross:
            cx = sb("cx", [TK, GB, D])
            cT = sb("cT", [D, NK])
        if mask == "given":
            mask_u8 = sb("mask_u8", [1, n_groups * NK], mybir.dt.uint8)
            mask_bf = sb("mask_bf", [1, n_groups * NK], BF16)

        s1 = [ps(f"s1{i}", [P, 512]) for i in range(2)]
        s2 = [ps(f"s2{i}", [P, 8, S]) for i in range(2)]
        mA, mB = ps("mA", [P, 512]), ps("mB", [P, 512])

        Dq = [nc.dram_tensor(f"{name}_Dq{i}", [D, TERMS, T], BF16, kind="Internal").ap() for i in range(3)]
        Dk = [nc.dram_tensor(f"{name}_Dk{i}", [D, TERMS, NK], BF16, kind="Internal").ap() for i in range(3)]
        Dm = nc.dram_tensor(f"{name}_Dm", [H16, 2, GB, S], BF16, kind="Internal").ap()
        Dq_rows = [t.rearrange("(g p i) r n -> p (i r) g n", p=2, i=HD8) for t in Dq]
        Dk_rows = [t.rearrange("(g p i) r n -> p (i r) g n", p=2, i=HD8) for t in Dk]
        Dm_rows = Dm.rearrange("(g p) j b s -> p j g (b s)", p=2)

        weights_in = sem("weights_in")
        sp_waits_met = sem("sp_waits_met")
        pool_set = sem("pool_set")
        setup = sem("setup")
        ones_in = sem("ones_in")
        ctx_in = sem("ctx_in")
        bn_done, stats, var_ready, rstd_ready, xn_ready = (sem(n) for n in ("bn_done", "stats", "var_ready", "rstd_ready", "xn_ready"))
        xnT_ps, xnT_sb, cT_ps, cT_sb = (sem(n) for n in ("xnT_ps", "xnT_sb", "cT_ps", "cT_sb"))
        q_ps, q_sb, k_ps, k_sb, v_ps, v_sb = (sem(n) for n in ("q_ps", "q_sb", "k_ps", "k_sb", "v_ps", "v_sb"))
        q_split, k_split, q_written, k_written, q_stacked, k_stacked = (sem(n) for n in ("q_split", "k_split", "q_written", "k_written", "q_stacked", "k_stacked"))
        mask_row = sem("mask_row")
        s1_ps, s1_max = sem("s1_ps"), sem("s1_max")
        m_ps, m_sb, m_written, m_stacked = (sem(n) for n in ("m_ps", "m_sb", "m_written", "m_stacked"))
        s2_ps, p_sb = sem("s2_ps"), sem("p_sb")
        o_ps, o_rs, o_sb, oT_ps, oT_sb, y_ps, x_biased, x_out = (sem(n) for n in ("o_ps", "o_rs", "o_sb", "oT_ps", "oT_sb", "y_ps", "x_biased", "x_out"))

        N_WEIGHTS = 8
        N_SETUP = 5 if mask == "given" else 4
        Q_READS = 4
        K_READS = 4 if mask else 2

        with nc.Block() as block:

            @block.sync
            def _(sp):
                for dst, src in ((wq, w["wq"]), (wk, w["wk"]), (wv, w["wv"]), (wo, w["wo"]), (bq, w["bq"]), (bk, w["bk"])):
                    sp.dma_start(dst[:, :], src).then_inc(weights_in, 16)
                for dst, src in ((bv, w["bv"]), (bo, w["bo"])):
                    sp.dma_start(dst[:, :], src.broadcast_to([P, D])).then_inc(weights_in, 16)
                if mask == "given":
                    sp.dma_start(mask_u8[:, :], w["mask"]).then_inc(ones_in, 16)

                def iteration(g, k):
                    a, r, b, ka, kr, kb = g + 3, g + 2, g + 1, k, (k + 2) % 3, (k + 1) % 3
                    if does(g, 2, n_groups):
                        if counted(8 * g):
                            sp.wait_ge(s2_ps, 8 * g)
                            sp.sem_inc(sp_waits_met, 1)
                        if counted(16 * Q_READS * r):
                            sp.wait_ge(q_stacked, 16 * Q_READS * r)
                            sp.sem_inc(sp_waits_met, 1)
                        sp.wait_ge(q_written, 48 * r + 48)
                        sp.sem_inc(sp_waits_met, 1)
                        for p in range(2):
                            row = HALF * p
                            sp.dma_start(QST[row:row + ROWS, kr, p::2, :], Dq_rows[kr][p]).then_inc(q_stacked, 16)
                            sp.dma_start(QST[row + ROWS:row + ROWS + 2, kr, p::2, :],
                                         zero2[:, :].unsqueeze(1).broadcast_to([2, PAIRS, T])).then_inc(q_stacked, 16)
                        if counted(16 * K_READS * r):
                            sp.wait_ge(k_stacked, 16 * K_READS * r)
                            sp.sem_inc(sp_waits_met, 1)
                        sp.wait_ge(k_written, 48 * r + 48)
                        sp.sem_inc(sp_waits_met, 1)
                        if mask == "zero_key":
                            sp.wait_ge(mask_row, r + 1)
                            sp.sem_inc(sp_waits_met, 1)
                        for p in range(2):
                            row = HALF * p
                            sp.dma_start(KST[row:row + ROWS, kr, :, 0:NK], Dk_rows[kr][p]).then_inc(k_stacked, 16)
                            if mask:
                                src = mrow[:, kr, :] if mask == "zero_key" else mask_bf[:, bass.ds(NK * r, NK)]
                                sp.dma_start(KST[row + ROWS + 2:row + ROWS + 3, kr, :, 0:NK],
                                             src.unsqueeze(1).broadcast_to([1, PAIRS, NK])).then_inc(k_stacked, 16)
                    if does(g, 1, n_groups):
                        sp.wait_ge(m_sb, 2 * b + 2)
                        sp.sem_inc(sp_waits_met, 1)
                        for j in range(2):
                            sp.dma_start(Dm[:, j, :, :], mT[:, j, :]).then_inc(m_written, 16)
                        if counted(32 * b):
                            sp.wait_ge(m_stacked, 32 * b)
                            sp.sem_inc(sp_waits_met, 1)
                        sp.wait_ge(m_written, 32 * b + 32)
                        sp.sem_inc(sp_waits_met, 1)
                        for p in range(2):
                            row = HALF * p + ROWS
                            sp.dma_start(QST[row:row + 2, kb, p::2, :], Dm_rows[p]).then_inc(m_stacked, 16)
                    if does(g, 3, n_groups):
                        sp.wait_ge(q_split, 3 * a + 3)
                        sp.sem_inc(sp_waits_met, 1)
                        if counted(16 * Q_READS * (a - 2)):
                            sp.wait_ge(q_stacked, 16 * Q_READS * (a - 2))
                            sp.sem_inc(sp_waits_met, 1)
                        sp.dma_start(Dq[ka][:, 0:3, :], q3[:, 0:1, :].broadcast_to([D, 3, T])).then_inc(q_written, 16)
                        sp.dma_start(Dq[ka][:, 3:5, :], q3[:, 1:2, :].broadcast_to([D, 2, T])).then_inc(q_written, 16)
                        sp.dma_start(Dq[ka][:, 5:6, :], q3[:, 2:3, :]).then_inc(q_written, 16)
                        sp.wait_ge(k_split, 3 * a + 3)
                        sp.sem_inc(sp_waits_met, 1)
                        if counted(16 * K_READS * (a - 2)):
                            sp.wait_ge(k_stacked, 16 * K_READS * (a - 2))
                            sp.sem_inc(sp_waits_met, 1)
                        sp.dma_start(Dk[ka][:, 0:3, :], k3[:, 0:3, :]).then_inc(k_written, 16)
                        sp.dma_start(Dk[ka][:, 3:5, :], k3[:, 0:2, :]).then_inc(k_written, 16)
                        sp.dma_start(Dk[ka][:, 5:6, :], k3[:, 0:1, :]).then_inc(k_written, 16)

                sp.wait_ge(setup, N_SETUP)
                groups_loop(sp, n_groups, iteration, ahead=3, after=1)

            @block.gpsimd
            def _(pool):
                nc.gpsimd.memset(minus_half[:, :], -0.5).then_inc(pool_set, 1)
                nc.gpsimd.memset(eps[:, :], LN_EPS).then_inc(pool_set, 1)
                nc.gpsimd.memset(zero2[:, :], 0.0).then_inc(setup, 1)
                pool.wait_ge(pool_set, 2)
                if mask == "given":
                    pool.wait_ge(ones_in, 16)
                    nc.gpsimd.tensor_scalar(mask_bf[:, :], mask_u8[:, :], MASKED, 0.0, ALU.mult, ALU.add).then_inc(setup, 1)
                pool.wait_ge(weights_in, 16 * N_WEIGHTS)
                def split(first, full, rest, parts, done, g):
                    pool.wait_ge(first, 2 * g + 2)
                    nc.gpsimd.tensor_tensor(rest[:, :], full[:, :], parts[:, 0, :], ALU.subtract).then_inc(done, 1)
                    nc.gpsimd.tensor_tensor(parts[:, 1, :], full[:, :], parts[:, 0, :], ALU.subtract).then_inc(done, 1)
                    pool.wait_ge(done, 3 * g + 2)
                    nc.gpsimd.tensor_tensor(parts[:, 2, :], rest[:, :], parts[:, 1, :], ALU.subtract).then_inc(done, 1)

                def iteration(g, k):
                    a = g + 3
                    if does(g, 3, n_groups):
                        if cross:
                            if counted(a):
                                pool.wait_ge(cT_ps, a)
                            pool.dma_start(cx[:, :, :], w["context"][bass.ds(GB * a, GB), :, :].rearrange("b t c -> t b c")).then_inc(ctx_in, 16)
                        pool.wait_ge(stats, a + 1)
                        nc.gpsimd.tensor_tensor(vare[:, :], mv[:, :, 1], eps[:, :], ALU.add).then_inc(var_ready, 1)
                        pool.wait_ge(var_ready, a + 1)
                        nc.gpsimd.tensor_tensor(rstd[:, :], vare[:, :], minus_half[:, :], ALU.pow).then_inc(rstd_ready, 1)
                    if does(g, 0, n_groups):
                        pool.wait_ge(xn_ready, g + 1)
                        xg = x[:, bass.ds(GB * g, GB), :]
                        nc.gpsimd.tensor_tensor(xg, xg, bo[:, :].unsqueeze(1).broadcast_to([P, GB, D]), ALU.add).then_inc(x_biased, 1)
                    if does(g, 3, n_groups):
                        split(q_sb, qf, r1q, q3, q_split, a)
                        split(k_sb, kf, r1k, k3, k_split, a)

                groups_loop(pool, n_groups, iteration, ahead=3, after=1)

            @block.scalar
            def _(act):
                act.wait_ge(weights_in, 16 * N_WEIGHTS)
                scale = 1.0 / math.sqrt(HD8)
                nc.scalar.activation(bqs[:, :], bq[:, :], ACT.Copy, scale=scale).then_inc(setup, 1)
                act.wait_ge(setup, N_SETUP)

                def exps(g, b):
                    for h in range(2):
                        n = 8 * g + 2 * b + h
                        act.wait_ge(s2_ps, n + 1)
                        if h == 0 and b % 2 == 0:
                            if counted(2 * g - 1 + b // 2):
                                act.wait_ge(o_ps, 2 * g - 1 + b // 2)
                        nc.scalar.activation(PR[0:TK, b, 8 * h:8 * h + 8, :], s2[h][0:TK, :, :], ACT.Exp).then_inc(p_sb, 1)

                def iteration(g, k):
                    a = g + 3
                    A, C, OUT = does(g, 3, n_groups), does(g, 0, n_groups), does(g, -1, n_groups)
                    if OUT:
                        if counted(g):
                            act.wait_ge(oT_ps, g)
                        if counted(g - 1):
                            act.wait_ge(y_ps, g - 1)
                        nc.scalar.activation(oT[:, :], mA[:, :], ACT.Copy).then_inc(oT_sb, 1)
                    if A:
                        act.wait_ge(xnT_ps, a + 1)
                        if counted(a):
                            act.wait_ge(v_ps if not cross else q_ps, a)
                        nc.scalar.activation(xnT[:, :], mA[:, :], ACT.Copy).then_inc(xnT_sb, 1)
                    if C:
                        exps(g, 0)
                    if A and cross:
                        act.wait_ge(cT_ps, a + 1)
                        if counted(a):
                            act.wait_ge(v_ps, a)
                        nc.scalar.activation(cT[:, :], mB[:, 0:NK], ACT.Copy).then_inc(cT_sb, 1)
                    if C:
                        exps(g, 1)
                    if A:
                        act.wait_ge(q_ps, a + 1)
                        if counted(3 * a):
                            act.wait_ge(q_split, 3 * a)
                        if counted(48 * a):
                            act.wait_ge(q_written, 48 * a)
                        nc.scalar.activation(q3[:, 0, :], mA[:, :], ACT.Identity, bias=bqs[:, 0:1], scale=scale).then_inc(q_sb, 1)
                        nc.scalar.activation(qf[:, :], mA[:, :], ACT.Identity, bias=bqs[:, 0:1], scale=scale).then_inc(q_sb, 1)
                        act.wait_ge(k_ps, a + 1)
                        if counted(3 * a):
                            act.wait_ge(k_split, 3 * a)
                        if counted(48 * a):
                            act.wait_ge(k_written, 48 * a)
                        nc.scalar.activation(k3[:, 0, :], mB[:, 0:NK], ACT.Identity, bias=bk[:, 0:1], scale=1.0).then_inc(k_sb, 1)
                        nc.scalar.activation(kf[:, :], mB[:, 0:NK], ACT.Identity, bias=bk[:, 0:1], scale=1.0).then_inc(k_sb, 1)
                    if C:
                        exps(g, 2)
                        exps(g, 3)

                groups_loop(act, n_groups, iteration, ahead=3, after=1)

            @block.vector
            def _(dve):
                nc.vector.memset(negm[:, 1, :, :], 0.0).then_inc(setup, 1)
                nc.vector.memset(V9[:, :, :, :, HD8:HD8 + 1], 1.0).then_inc(setup, 1)
                dve.wait_ge(weights_in, 16 * N_WEIGHTS)

                def maxima(g, b):
                    for c, (h0, h1) in enumerate(chunks):
                        n = NCH * (GB * g + b) + c
                        dve.wait_ge(s1_ps, n + 1)
                        if b == 0 and c == 0:
                            if counted(g):
                                dve.wait_ge(m_ps, g)
                        nc.vector.tensor_reduce(negm[:, 0, h0:h1, b],
                                                s1[(NCH * b + c) % 2][:, 0:(h1 - h0) * TK].rearrange("p (h t) -> p h t", t=TK),
                                                axis=AX.X, op=ALU.max, negate=True).then_inc(s1_max, 1)

                def heads_out(g, j):
                    bank = (mA if j == 0 else mB)[:, 0:2 * H16 * (HD8 + 1)].rearrange("p (b h e) -> p b h e", b=2, h=H16)
                    n = 2 * g + j
                    dve.wait_ge(o_ps, n + 1)
                    if j == 0:
                        if counted(g):
                            dve.wait_ge(oT_ps, g)
                    if counted(n):
                        dve.wait_ge(o_sb, n)
                    nc.vector.reciprocal(rs[:, :, :], bank[:, :, :, HD8]).then_inc(o_rs, 1)
                    dve.wait_ge(o_rs, n + 1)
                    nc.vector.tensor_tensor(On[:, 2 * j:2 * j + 2, :, :].rearrange("p b h e -> p (b h) e"),
                                            bank[:, :, :, 0:HD8].rearrange("p b h e -> p (b h) e"),
                                            rs[:, :, :].rearrange("p b h -> p (b h)").unsqueeze(2).broadcast_to([P, 2 * H16, HD8]),
                                            ALU.mult).then_inc(o_sb, 1)

                def iteration(g, k):
                    a, r, ka, kr = g + 3, g + 2, k, (k + 2) % 3
                    A, R, B, C, OUT = (does(g, stage, n_groups) for stage in (3, 2, 1, 0, -1))
                    if A:
                        if counted(a):
                            dve.wait_ge(stats, a)
                        for b in range(GB):
                            last = nc.vector.bn_stats(stat6[:, b, :], x[:, bass.ds(GB * a + b, 1), :].rearrange("p o c -> p (o c)"))
                        last.then_inc(bn_done, 1)
                        dve.wait_ge(bn_done, a + 1)
                        if counted(a):
                            dve.wait_ge(rstd_ready, a)
                        nc.vector.tensor_copy(spare[:, :], stat6[:, 0, 0:1])
                        for b in range(GB):
                            last = nc.vector.bn_aggr(mv[:, b, :], stat6[:, b, :])
                        last.then_inc(stats, 1)
                    if B:
                        maxima(g + 1, 0)
                    if OUT:
                        heads_out(g - 1, 1)
                    if B:
                        maxima(g + 1, 1)
                    if R:
                        dve.wait_ge(v_ps, r + 1)
                        if counted(2 * g):
                            dve.wait_ge(o_ps, 2 * g)
                        nc.vector.tensor_tensor(V9[0:TK, kr, :, :, 0:HD8],
                                                mB[0:TK, :].rearrange("p (b h e) -> p b h e", b=GB, h=H16),
                                                bv[0:TK, :].rearrange("p (h e) -> p h e", h=H16).unsqueeze(1).broadcast_to([TK, GB, H16, HD8]),
                                                ALU.add).then_inc(v_sb, 1)
                    if A:
                        dve.wait_ge(rstd_ready, a + 1)
                        if counted(a):
                            dve.wait_ge(xnT_ps, a)
                        for b in range(GB):
                            last = nc.vector.tensor_scalar(xn[:, b, :], x[:, bass.ds(GB * a + b, 1), :].rearrange("p o c -> p (o c)"),
                                                           mv[:, b, 0:1], rstd[:, b:b + 1], ALU.subtract, ALU.mult)
                        last.then_inc(xn_ready, 1)
                    if OUT:
                        if counted(g):
                            dve.wait_ge(y_ps, g)
                        if counted(g):
                            dve.wait_ge(x_biased, g)
                        xg = x[:, bass.ds(GB * (g - 1), GB), :]
                        nc.vector.tensor_tensor(xg, mB[:, :].rearrange("p (b c) -> p b c", b=GB), xg, ALU.add).then_inc(x_out, 1)
                    if A and mask == "zero_key":
                        dve.wait_ge(xnT_sb, a + 1)
                        if counted(16 * K_READS * (a - 2)):
                            dve.wait_ge(k_stacked, 16 * K_READS * (a - 2))
                        nc.vector.tensor_scalar(mrow[:, ka, :], xnT[0:1, :], 0.0, MASKED, ALU.is_equal, ALU.mult).then_inc(mask_row, 1)
                    if B:
                        maxima(g + 1, 2)
                        maxima(g + 1, 3)
                        dve.wait_ge(m_ps, g + 2)
                        if counted(32 * (g + 1)):
                            dve.wait_ge(m_written, 32 * (g + 1))
                        nc.vector.tensor_copy(mT[:, 0, :], mA[0:GB * H16, 0:S]).then_inc(m_sb, 1)
                        dve.wait_ge(m_sb, 2 * (g + 1) + 1)
                        nc.vector.tensor_tensor(mT[:, 1, :], mA[0:GB * H16, 0:S], mT[:, 0, :], ALU.subtract).then_inc(m_sb, 1)
                    if C:
                        heads_out(g, 0)

                groups_loop(dve, n_groups, iteration, ahead=3, after=1)
                dve.wait_ge(x_out, n_groups)

            @block.tensor
            def _(pe):
                pe.wait_ge(weights_in, 16 * N_WEIGHTS)
                pe.wait_ge(setup, N_SETUP)

                def scores_rows(g, k, b):
                    if b == 0:
                        if counted(16 * Q_READS * (g + 1)):
                            pe.wait_ge(q_stacked, 16 * Q_READS * (g + 1))
                        if counted(16 * K_READS * (g + 1)):
                            pe.wait_ge(k_stacked, 16 * K_READS * (g + 1))
                    for c, (h0, h1) in enumerate(chunks):
                        n = NCH * (GB * g + b) + c
                        if counted(n - 1):
                            pe.wait_ge(s1_max, n - 1)
                        for h in range(h0, h1):
                            last = nc.tensor.matmul(s1[(NCH * b + c) % 2][:, (h - h0) * TK:(h - h0 + 1) * TK],
                                                    QST[:, k, h, b * S:(b + 1) * S], KST[:, k, h // 2, b * TK:(b + 1) * TK],
                                                    start=True, stop=True)
                        last.then_inc(s1_ps, 1)

                def scores_keys(g, k, b):
                    if b == 0:
                        if counted(32 * (g + 1)):
                            pe.wait_ge(m_stacked, 32 * (g + 1))
                    for h in range(2):
                        n = 8 * g + 2 * b + h
                        if counted(n - 1):
                            pe.wait_ge(p_sb, n - 1)
                        for j in range(4):
                            pair = 4 * h + j
                            last = nc.tensor.matmul(s2[h][0:TK, 2 * j:2 * j + 2, :], KST[:, k, pair, b * TK:(b + 1) * TK],
                                                    QST[:, k, 2 * pair:2 * pair + 2, b * S:(b + 1) * S], start=True, stop=True)
                        last.then_inc(s2_ps, 1)

                def values(g, k, j):
                    bank = (mA if j == 0 else mB)[:, 0:2 * H16 * (HD8 + 1)].rearrange("p (b h e) -> p b h e", b=2, h=H16)
                    pe.wait_ge(v_sb, g + 1)
                    for b in range(2):
                        bb = 2 * j + b
                        pe.wait_ge(p_sb, 8 * g + 2 * bb + 2)
                        for h in range(H16):
                            last = nc.tensor.matmul(bank[:, b, h, :], PR[0:TK, bb, h, :], V9[0:TK, k, bb, h, :], start=True, stop=True)
                    last.then_inc(o_ps, 1)

                def iteration(g, k):
                    a, r, kr, kb = g + 3, g + 2, (k + 2) % 3, (k + 1) % 3
                    A, R, B, C, OUT = (does(g, stage, n_groups) for stage in (3, 2, 1, 0, -1))
                    if B:
                        scores_rows(g + 1, kb, 0)
                    if counted(2 * before(g, 3, n_groups)):
                        pe.wait_ge(k_sb, 2 * before(g, 3, n_groups))
                    if counted(before(g, -1, n_groups)):
                        pe.wait_ge(x_out, before(g, -1, n_groups))
                    if OUT:
                        values(g - 1, kr, 1)
                    if B:
                        scores_rows(g + 1, kb, 1)
                    if OUT:
                        if counted(2 * g):
                            pe.wait_ge(o_sb, 2 * g)
                        for b in range(GB):
                            last = nc.tensor.transpose(mA[:, b * S:(b + 1) * S], On[:, b, :, :].rearrange("p h e -> p (h e)"), ident[:, :])
                        last.then_inc(oT_ps, 1)
                    if R:
                        src = cT if cross else xnT
                        if counted(2 * g):
                            pe.wait_ge(o_sb, 2 * g)
                        for b in range(GB):
                            last = nc.tensor.matmul(mB[0:TK, b * D:(b + 1) * D], src[:, b * TK:(b + 1) * TK], wv[:, :], start=True, stop=True)
                        last.then_inc(v_ps, 1)
                    if OUT:
                        if counted(g):
                            pe.wait_ge(oT_sb, g)
                        if counted(through(g, 2, n_groups)):
                            pe.wait_ge(v_sb, through(g, 2, n_groups))
                        for b in range(GB):
                            last = nc.tensor.matmul(mB[:, b * D:(b + 1) * D], oT[:, b * S:(b + 1) * S], wo[:, :], start=True, stop=True)
                        last.then_inc(y_ps, 1)
                    if A:
                        pe.wait_ge(xn_ready, a + 1)
                        if counted(g):
                            pe.wait_ge(oT_sb, g)
                        if isinstance(g, int) and g < 1:
                            if counted(2 * a):
                                pe.wait_ge(q_sb, 2 * a)
                            if counted(2 * (g + 1)):
                                pe.wait_ge(m_sb, 2 * (g + 1))
                        for b in range(GB):
                            last = nc.tensor.transpose(mA[:, b * S:(b + 1) * S], xn[:, b, :], ident[:, :])
                        last.then_inc(xnT_ps, 1)
                    if C:
                        scores_keys(g, k, 0)
                    if A:
                        if counted(g):
                            pe.wait_ge(x_out, g)
                        pe.wait_ge(v_sb, r + 1)
                        if cross:
                            pe.wait_ge(ctx_in, 16 * (a + 1))
                            for b in range(GB):
                                last = nc.tensor.transpose(mB[:, b * TK:(b + 1) * TK], cx[:, b, :], ident[0:TK, 0:TK])
                            last.then_inc(cT_ps, 1)
                    if B:
                        scores_rows(g + 1, kb, 2)
                    if C:
                        scores_keys(g, k, 1)
                    if A:
                        pe.wait_ge(xnT_sb, a + 1)
                        nc.tensor.matmul(mA[:, :], wq[:, :], xnT[:, :], start=True, stop=True).then_inc(q_ps, 1)
                    if B:
                        scores_rows(g + 1, kb, 3)
                    if A:
                        if cross:
                            pe.wait_ge(cT_sb, a + 1)
                        nc.tensor.matmul(mB[:, 0:NK], wk[:, :], (cT if cross else xnT)[:, :], start=True, stop=True).then_inc(k_ps, 1)
                    if B:
                        if A:
                            pe.wait_ge(q_sb, 2 * a + 2)
                        if counted(g):
                            pe.wait_ge(oT_sb, g)
                        if counted(NCH * GB * (g + 2)):
                            pe.wait_ge(s1_max, NCH * GB * (g + 2))
                        nc.tensor.transpose(mA[:, 0:S], negm[:, :, :, :].rearrange("p r h b -> p (r h b)"), ident[:, :]).then_inc(m_ps, 1)
                    if C:
                        scores_keys(g, k, 2)
                        if counted(2 * through(g, 1, n_groups)):
                            pe.wait_ge(m_sb, 2 * through(g, 1, n_groups))
                        if counted(g):
                            pe.wait_ge(oT_sb, g)
                        values(g, k, 0)
                        scores_keys(g, k, 3)

                groups_loop(pe, n_groups, iteration, ahead=3, after=1)


MAGIC = 1.5 * 2.0 ** 23
FF = 512
FCH = FF // P
QMAX = 127.0
CLIP = 1e-5


def ternary_ffn(nc, env, n_groups, w):
    x, ident = env["x"], env["ident"]
    ctx = ExitStack()
    with ctx:
        def sb(n, shape, dt=F32):
            return ctx.enter_context(nc.sbuf_tensor(f"ffn_{n}", shape, dt))

        def ps(n, shape, dt=F32):
            return ctx.enter_context(nc.psum_tensor(f"ffn_{n}", shape, dt))

        def sem(n):
            return nc.alloc_semaphore(f"ffn_{n}")

        w1f, w2f = sb("w1f", [D, FF]), sb("w2f", [P, FCH, D])
        w1r, w2r = sb("w1r", [D, FF]), sb("w2r", [P, FCH * D])
        w1i, w2i = sb("w1i", [D, FF], BF16), sb("w2i", [P, FCH, D], BF16)
        b1, b2 = sb("b1", [P, FF]), sb("b2", [P, D])
        ones = sb("ones", [P, P])
        identb = sb("identb", [P, P], BF16)
        wabs = sb("wabs", [P, 2])
        wmean = sb("wmean", [P, 2])
        winv = sb("winv", [P, 2])
        stat6 = sb("stat6", [P, GB, 6])
        mv = sb("mv", [P, GB, 2])
        vare, rstd = sb("vare", [P, GB]), sb("rstd", [P, GB])
        minus_half, eps, inv_ff = sb("minus_half", [P, GB]), sb("eps", [P, GB]), sb("inv_ff", [P, GB])
        xn = sb("xn", [P, GB, D])
        m1, q1s, r1, a1, i1, f1 = (sb(n, [P, GB]) for n in ("m1", "q1s", "r1", "a1", "i1", "f1"))
        m2, q2s, q2m, r2, a2, i2, f2 = (sb(n, [P, GB]) for n in ("m2", "q2s", "q2m", "r2", "a2", "i2", "f2"))
        vare2, spare = sb("vare2", [P, GB]), sb("spare", [P, 1])
        out1, out2 = sb("out1", [P, 3, GB]), sb("out2", [P, 3, GB])
        big1, int1 = sb("big1", [P, GB, D]), sb("int1", [P, GB, D], BF16)
        int1T = sb("int1T", [D, 3, T], BF16)
        pre = sb("pre", [P, GB, FF])
        hid = sb("hid", [P, GB, FF])
        sq = sb("sq", [P, FF])
        big2 = sb("big2", [P, GB, FF])
        int2 = sb("int2", [P, 3, GB, FF], BF16)
        int2T = sb("int2T", [P, 2, FF], BF16)

        xT_bank = ps("xT", [P, T], BF16)
        h_bank = [ps(f"h{i}", [P, FF]) for i in range(2)]
        t_bank = [ps(f"t{i}", [P, FF], BF16) for i in range(2)]
        y_bank = ps("y", [P, GB, D])
        w_bank = ps("w", [P, 2])

        weights_in, consts, w_abs, w_sum, w_inv, w_round, w_ready = (sem(n) for n in ("weights_in", "consts", "w_abs", "w_sum", "w_inv", "w_round", "w_ready"))
        bn_done, stats, var_ready, rstd_ready, xn_done, q1_ready, r1_ready, chain1, int1_ready, xT_ps, xT_sb = (
            sem(n) for n in ("bn_done", "stats", "var_ready", "rstd_ready", "xn_done", "q1_ready", "r1_ready", "chain1", "int1_ready", "xT_ps", "xT_sb"))
        h_ps, pre_sb, hid_sb, sq_sb, max2, q2_ready, r2_ready, chain2, int2_ready = (
            sem(n) for n in ("h_ps", "pre_sb", "hid_sb", "sq_sb", "max2", "q2_ready", "r2_ready", "chain2", "int2_ready"))
        max1, big1_ready, big2_ready = sem("max1"), sem("big1_ready"), sem("big2_ready")
        t_ps, t_sb, y_ps, x_biased, x_out = (sem(n) for n in ("t_ps", "t_sb", "y_ps", "x_biased", "x_out"))

        with nc.Block() as block:

            @block.sync
            def _(sp):
                sp.dma_start(w1f[:, :], w["w1"]).then_inc(weights_in, 16)
                sp.dma_start(w2f[:, :, :], w["w2"].rearrange("(c p) n -> p c n", p=P)).then_inc(weights_in, 16)
                sp.dma_start(b1[:, :], w["b1"].broadcast_to([P, FF])).then_inc(weights_in, 16)
                sp.dma_start(b2[:, :], w["b2"].broadcast_to([P, D])).then_inc(weights_in, 16)
                sp.wait_ge(weights_in, 64)

            @block.gpsimd
            def _(pool):
                for t, v in ((minus_half, -0.5), (eps, LN_EPS), (inv_ff, 1.0 / FF), (ones, 1.0)):
                    nc.gpsimd.memset(t[:, :], v).then_inc(consts, 1)
                pool.wait_ge(consts, 6)
                pool.wait_ge(weights_in, 64)

                def iteration(g, k):
                    a, b = g + 2, g + 1
                    if does(g, 2, n_groups):
                        pool.wait_ge(stats, a + 1)
                        nc.gpsimd.tensor_tensor(vare[:, :], mv[:, :, 1], eps[:, :], ALU.add).then_inc(var_ready, 1)
                        pool.wait_ge(var_ready, 3 * a + 1)
                        nc.gpsimd.tensor_tensor(rstd[:, :], vare[:, :], minus_half[:, :], ALU.pow).then_inc(rstd_ready, 1)
                        pool.wait_ge(rstd_ready, a + 1)
                        nc.gpsimd.tensor_tensor(q1s[:, :], rstd[:, :], rstd[:, :], ALU.mult).then_inc(var_ready, 1)
                        pool.wait_ge(var_ready, 3 * a + 2)
                        nc.gpsimd.tensor_tensor(r1[:, :], q1s[:, :], mv[:, :, 1], ALU.mult).then_inc(var_ready, 1)
                        pool.wait_ge(var_ready, 3 * a + 3)
                        nc.gpsimd.tensor_tensor(q1s[:, :], r1[:, :], eps[:, :], ALU.add).then_inc(q1_ready, 1)
                        pool.wait_ge(q1_ready, a + 1)
                        if counted(a):
                            pool.wait_ge(int1_ready, a)
                        nc.gpsimd.tensor_tensor(r1[:, :], q1s[:, :], minus_half[:, :], ALU.pow).then_inc(r1_ready, 1)
                    if does(g, 0, n_groups):
                        pool.wait_ge(xn_done, g + 1)
                        xg = x[:, bass.ds(GB * g, GB), :]
                        nc.gpsimd.tensor_tensor(xg, xg, b2[:, :].unsqueeze(1).broadcast_to([P, GB, D]), ALU.add).then_inc(x_biased, 1)
                    if does(g, 1, n_groups):
                        pool.wait_ge(sq_sb, GB * b + GB)
                        nc.gpsimd.tensor_tensor(q2m[:, :], q2s[:, :], inv_ff[:, :], ALU.mult).then_inc(q2_ready, 1)
                        pool.wait_ge(q2_ready, 2 * b + 1)
                        nc.gpsimd.tensor_tensor(vare2[:, :], q2m[:, :], eps[:, :], ALU.add).then_inc(q2_ready, 1)
                        pool.wait_ge(q2_ready, 2 * b + 2)
                        if counted(b):
                            pool.wait_ge(int2_ready, b)
                        nc.gpsimd.tensor_tensor(r2[:, :], vare2[:, :], minus_half[:, :], ALU.pow).then_inc(r2_ready, 1)

                groups_loop(pool, n_groups, iteration)

            @block.scalar
            def _(act):
                act.wait_ge(weights_in, 64)

                def iteration(g, k):
                    a, b = g + 2, g + 1
                    A, B, C = does(g, 2, n_groups), does(g, 1, n_groups), does(g, 0, n_groups)
                    for j in range(GB):
                        if B:
                            n = GB * b + j
                            act.wait_ge(pre_sb, n + 1)
                            if counted(b):
                                act.wait_ge(int2_ready, b)
                            nc.scalar.activation(hid[:, j, :], pre[:, j, :], ACT.Gelu).then_inc(hid_sb, 1)
                        if C:
                            n = GB * g + j
                            act.wait_ge(t_ps, n + 1)
                            if counted(n - 1):
                                act.wait_ge(y_ps, n - 1)
                            nc.scalar.activation(int2T[:, j % 2, :], t_bank[j % 2][:, :], ACT.Copy).then_inc(t_sb, 1)
                        if B:
                            act.wait_ge(hid_sb, GB * b + j + 1)
                            if j == 0:
                                if counted(2 * b):
                                    act.wait_ge(q2_ready, 2 * b)
                            if counted(GB * b + j):
                                act.wait_ge(sq_sb, GB * b + j)
                            nc.scalar.activation(sq[:, :], hid[:, j, :], ACT.Square, accum_out=q2s[:, j:j + 1]).then_inc(sq_sb, 1)
                    if A:
                        act.wait_ge(xT_ps, a + 1)
                        if counted(GB * (a - 2)):
                            act.wait_ge(h_ps, GB * (a - 2))
                        nc.scalar.activation(int1T[:, (k + 2) % 3, :], xT_bank[:, :], ACT.Copy).then_inc(xT_sb, 1)

                groups_loop(act, n_groups, iteration)

            @block.vector
            def _(dve):
                dve.wait_ge(weights_in, 64)
                nc.vector.tensor_reduce(wabs[:, 0:1], w1f[:, :], axis=AX.X, op=ALU.add, apply_absolute_value=True).then_inc(w_abs, 1)
                nc.vector.tensor_reduce(wabs[:, 1:2], w2f[:, :, :].rearrange("p c n -> p (c n)"), axis=AX.X, op=ALU.add, apply_absolute_value=True).then_inc(w_abs, 1)
                nc.vector.tensor_copy(identb[:, :], ident[:, :]).then_inc(consts, 1)
                dve.wait_ge(w_sum, 1)
                nc.vector.tensor_scalar(wmean[:, :], w_bank[:, :], 1.0 / (FF * D), CLIP, ALU.mult, ALU.max).then_inc(w_inv, 1)
                dve.wait_ge(w_inv, 1)
                nc.vector.reciprocal(winv[:, :], wmean[:, :]).then_inc(w_inv, 1)
                dve.wait_ge(w_inv, 2)
                for i, (full, rounded, whole) in enumerate(((w1f[:, :], w1r, w1i[:, :]),
                                                            (w2f[:, :, :].rearrange("p c n -> p (c n)"), w2r, w2i[:, :, :].rearrange("p c n -> p (c n)")))):
                    nc.vector.tensor_scalar(rounded[:, :], full, winv[:, i:i + 1], MAGIC, ALU.mult, ALU.add).then_inc(w_round, 1)
                    dve.wait_ge(w_round, 2 * i + 1)
                    nc.vector.tensor_scalar(full, rounded[:, :], MAGIC, 1.0, ALU.subtract, ALU.min).then_inc(w_round, 1)
                    dve.wait_ge(w_round, 2 * i + 2)
                    nc.vector.tensor_scalar(whole, full, -1.0, 0.0, ALU.max, ALU.add).then_inc(w_ready, 1)
                nc.vector.tensor_scalar(wabs[:, :], wmean[:, :], 1.0 / QMAX, 0.0, ALU.mult, ALU.add).then_inc(consts, 1)
                dve.wait_ge(consts, 6)

                def factors(first, peak, rec, clipped, inverse, factor, outs, k, i, chain, n):
                    dve.wait_ge(first, n + 1)
                    nc.vector.tensor_tensor(clipped[:, :], peak[:, :], rec[:, :], ALU.mult).then_inc(chain, 1)
                    dve.wait_ge(chain, 4 * n + 1)
                    nc.vector.tensor_scalar(inverse[:, :], clipped[:, :], CLIP, 1.0, ALU.max, ALU.mult).then_inc(chain, 1)
                    dve.wait_ge(chain, 4 * n + 2)
                    nc.vector.tensor_scalar(outs[:, k, :], inverse[:, :], wabs[:, i:i + 1], None, ALU.mult)
                    nc.vector.reciprocal(clipped[:, :], inverse[:, :]).then_inc(chain, 1)
                    dve.wait_ge(chain, 4 * n + 3)
                    nc.vector.scalar_tensor_tensor(factor[:, :], clipped[:, :], QMAX, rec[:, :], ALU.mult, ALU.mult).then_inc(chain, 1)
                    dve.wait_ge(chain, 4 * n + 4)

                def iteration(g, k):
                    a, b, ka, kb = g + 2, g + 1, (k + 2) % 3, (k + 1) % 3
                    A, B, C = does(g, 2, n_groups), does(g, 1, n_groups), does(g, 0, n_groups)
                    if C:
                        dve.wait_ge(max2, g + 1)
                        factors(r2_ready, m2, r2, a2, i2, f2, out2, k, 1, chain2, g)
                        for j in range(GB):
                            last = nc.vector.tensor_scalar(big2[:, j, :], hid[:, j, :], f2[:, j:j + 1], MAGIC, ALU.mult, ALU.add)
                        last.then_inc(big2_ready, 1)
                        dve.wait_ge(big2_ready, g + 1)
                        if counted(GB * (g - 1)):
                            dve.wait_ge(t_ps, GB * (g - 1))
                        nc.vector.tensor_scalar(int2[:, k, :, :], big2[:, :, :], MAGIC, QMAX, ALU.subtract, ALU.min).then_inc(int2_ready, 1)
                    if A:
                        if counted(a):
                            dve.wait_ge(r1_ready, a)
                        for j in range(GB):
                            last = nc.vector.bn_stats(stat6[:, j, :], x[:, bass.ds(GB * a + j, 1), :].rearrange("p o c -> p (o c)"))
                        last.then_inc(bn_done, 1)
                        dve.wait_ge(bn_done, a + 1)
                    if B:
                        for j in range(GB):
                            n = GB * b + j
                            dve.wait_ge(h_ps, n + 1)
                            if counted(n - GB + 1):
                                dve.wait_ge(hid_sb, n - GB + 1)
                            nc.vector.scalar_tensor_tensor(pre[:, j, :], h_bank[j % 2][:, :], out1[:, kb, j:j + 1], b1[:, :], ALU.mult, ALU.add).then_inc(pre_sb, 1)
                    if A:
                        if not B:
                            nc.vector.tensor_copy(spare[:, :], stat6[:, 0, 0:1])
                        for j in range(GB):
                            last = nc.vector.bn_aggr(mv[:, j, :], stat6[:, j, :])
                        last.then_inc(stats, 1)
                    if B:
                        for j in range(GB):
                            dve.wait_ge(hid_sb, GB * b + j + 1)
                            last = nc.vector.tensor_reduce(m2[:, j:j + 1], hid[:, j, :], axis=AX.X, op=ALU.max, apply_absolute_value=True)
                        last.then_inc(max2, 1)
                    if A:
                        dve.wait_ge(rstd_ready, a + 1)
                        for j in range(GB):
                            last = nc.vector.tensor_scalar(xn[:, j, :], x[:, bass.ds(GB * a + j, 1), :].rearrange("p o c -> p (o c)"),
                                                           mv[:, j, 0:1], rstd[:, j:j + 1], ALU.subtract, ALU.mult)
                        last.then_inc(xn_done, 1)
                        dve.wait_ge(xn_done, a + 1)
                        nc.vector.tensor_reduce(m1[:, :], xn[:, :, :], axis=AX.X, op=ALU.max, apply_absolute_value=True).then_inc(max1, 1)
                        dve.wait_ge(max1, a + 1)
                        factors(r1_ready, m1, r1, a1, i1, f1, out1, ka, 0, chain1, a)
                        for j in range(GB):
                            last = nc.vector.tensor_scalar(big1[:, j, :], xn[:, j, :], f1[:, j:j + 1], MAGIC, ALU.mult, ALU.add)
                        last.then_inc(big1_ready, 1)
                        dve.wait_ge(big1_ready, a + 1)
                        if counted(a):
                            dve.wait_ge(xT_ps, a)
                        nc.vector.tensor_scalar(int1[:, :, :], big1[:, :, :], MAGIC, QMAX, ALU.subtract, ALU.min).then_inc(int1_ready, 1)
                    if C:
                        dve.wait_ge(x_biased, g + 1)
                        if counted(GB * g + GB):
                            dve.wait_ge(y_ps, GB * g + GB)
                        for j in range(GB):
                            xj = x[:, bass.ds(GB * g + j, 1), :].rearrange("p o c -> p (o c)")
                            last = nc.vector.scalar_tensor_tensor(xj, y_bank[:, j, :], out2[:, k, j:j + 1], xj, ALU.mult, ALU.add)
                        last.then_inc(x_out, 1)

                groups_loop(dve, n_groups, iteration)
                dve.wait_ge(x_out, n_groups)

            @block.tensor
            def _(pe):
                pe.wait_ge(w_abs, 2)
                pe.wait_ge(consts, 5)
                nc.tensor.matmul(w_bank[:, :], ones[:, :], wabs[:, :], start=True, stop=True).then_inc(w_sum, 1)
                pe.wait_ge(w_ready, 2)
                pe.wait_ge(consts, 6)

                def output(g, j):
                    if counted(GB * g + j + 1):
                        pe.wait_ge(t_sb, GB * g + j + 1)
                    if j == 0:
                        if counted(g):
                            pe.wait_ge(x_out, g)
                    for c in range(FCH):
                        last = nc.tensor.matmul(y_bank[:, j, :], int2T[:, j % 2, c * P:(c + 1) * P], w2i[:, c, :], start=(c == 0), stop=(c == FCH - 1))
                    last.then_inc(y_ps, 1)

                def iteration(g, k):
                    a, b, ka, kb = g + 2, g + 1, (k + 2) % 3, (k + 1) % 3
                    A, B, C = does(g, 2, n_groups), does(g, 1, n_groups), does(g, 0, n_groups)
                    for j in range(GB):
                        if B:
                            n = GB * b + j
                            pe.wait_ge(xT_sb, b + 1)
                            if counted(n - 1):
                                pe.wait_ge(pre_sb, n - 1)
                            nc.tensor.matmul(h_bank[j % 2][:, :], int1T[:, kb, j * S:(j + 1) * S], w1i[:, :], start=True, stop=True).then_inc(h_ps, 1)
                        if C:
                            n = GB * g + j
                            pe.wait_ge(int2_ready, g + 1)
                            if counted(n - 1):
                                pe.wait_ge(t_sb, n - 1)
                            for c in range(FCH):
                                last = nc.tensor.transpose(t_bank[j % 2][:, c * P:(c + 1) * P], int2[:, k, j, c * P:(c + 1) * P], identb[:, :])
                            last.then_inc(t_ps, 1)
                            if j > 0:
                                output(g, j - 1)
                    if C:
                        output(g, GB - 1)
                    if A:
                        pe.wait_ge(int1_ready, a + 1)
                        if counted(a):
                            pe.wait_ge(xT_sb, a)
                        for j in range(GB):
                            last = nc.tensor.transpose(xT_bank[:, j * S:(j + 1) * S], int1[:, j, :], identb[:, :])
                        last.then_inc(xT_ps, 1)

                groups_loop(pe, n_groups, iteration)


def quantum_composites(nc, env, q):
    QFF, NQ = 512, 8
    CH = QFF // P
    ctx = ExitStack()
    with ctx:
        def sb(n, shape, dt=F32):
            return ctx.enter_context(nc.sbuf_tensor(f"comp_{n}", shape, dt))

        w1T = sb("w1T", [P, CH, D])
        wm = sb("wm", [P, CH, NQ])
        b1 = sb("b1", [P, CH])
        bqo = sb("bqo", [P, CH])
        bm, b2 = sb("bm", [P, NQ]), sb("b2", [P, D])
        w2 = sb("w2", [P, CH, D])
        wqoT = sb("wqoT", [P, CH, GB * NQ])
        b1w, bqow = sb("b1w", [P, CH, P]), sb("bqow", [P, CH, P])
        out_sb = sb("out_sb", [GB * NQ, D])
        banks = [ctx.enter_context(nc.psum_tensor(f"comp_ps{i}", [P, 512], F32)) for i in range(4)]
        loaded, spread, product, read, zeroed, placed = (nc.alloc_semaphore(f"comp_{n}")
                                                         for n in ("loaded", "spread", "product", "read", "zeroed", "placed"))
        with nc.Block() as block:

            @block.sync
            def _(sp):
                sp.dma_start(w1T[:, :, :], q["W1T"].rearrange("(c p) n -> p c n", p=P)).then_inc(loaded, 16)
                sp.dma_start(wm[:, :, :], q["Wm"].rearrange("(c p) n -> p c n", p=P)).then_inc(loaded, 16)
                sp.dma_start(w2[:, :, :], q["W2"].rearrange("(c p) n -> p c n", p=P)).then_inc(loaded, 16)
                for dst, src in ((b1, q["b1"]), (bqo, q["bqo"])):
                    for c in range(CH):
                        sp.dma_start(dst[:, c:c + 1], src[c * P:(c + 1) * P].unsqueeze(1)).then_inc(loaded, 16)
                sp.dma_start(bm[:, :], q["bm"].unsqueeze(0).broadcast_to([P, NQ])).then_inc(loaded, 16)
                sp.dma_start(b2[:, :], q["b2"].unsqueeze(0).broadcast_to([P, D])).then_inc(loaded, 16)
                for j in range(GB):
                    sp.dma_start(wqoT[:, :, NQ * j:NQ * (j + 1)], q["WqoT"].rearrange("(c p) n -> p c n", p=P)).then_inc(loaded, 16)
                sp.wait_ge(read, 4)
                sp.wait_ge(zeroed, 1)
                for j in range(GB):
                    sp.dma_start(env["w_out"][NQ * j:NQ * (j + 1), j, :], out_sb[NQ * j:NQ * (j + 1), :]).then_inc(placed, 16)
                sp.wait_ge(placed, 16 * GB)

            @block.vector
            def _(dve):
                nc.vector.memset(env["w_out"][:, :, :], 0.0).then_inc(zeroed, 1)
                dve.wait_ge(loaded, 16 * 17)
                nc.vector.tensor_copy(b1w[:, :, :], b1[:, :].unsqueeze(2).broadcast_to([P, CH, P])).then_inc(spread, 1)
                nc.vector.tensor_copy(bqow[:, :, :], bqo[:, :].unsqueeze(2).broadcast_to([P, CH, P])).then_inc(spread, 1)
                dve.wait_ge(product, 4)
                nc.vector.tensor_copy(env["w_in"][:, :], banks[0][:, 0:NQ]).then_inc(read, 1)
                nc.vector.tensor_tensor(env["b_in"][:, :], banks[1][:, 0:NQ], bm[:, :], ALU.add).then_inc(read, 1)
                nc.vector.tensor_tensor(env["b_out"][:, :], banks[3][:, 0:D], b2[:, :], ALU.add).then_inc(read, 1)
                nc.vector.tensor_copy(out_sb[:, :], banks[2][0:GB * NQ, 0:D]).then_inc(read, 1)
                dve.wait_ge(read, 4)

            @block.tensor
            def _(pe):
                pe.wait_ge(loaded, 16 * 17)
                pe.wait_ge(spread, 2)
                for bank, left, right, rows, cols in ((banks[0], w1T, wm, P, NQ), (banks[1], b1w, wm, P, NQ),
                                                      (banks[2], wqoT, w2, GB * NQ, D), (banks[3], bqow, w2, P, D)):
                    for c in range(CH):
                        last = nc.tensor.matmul(bank[0:rows, 0:cols], left[:, c, :], right[:, c, :], start=(c == 0), stop=(c == CH - 1))
                    last.then_inc(product, 1)


def quantum_block(nc, env, n_groups, q):
    x, ident = env["x"], env["ident"]
    H, HD, NQ = 8, 16, 8
    TINY = 1e-30
    EPS_COS = 1e-8
    MAGIC = 1.5 * 2.0 ** 23
    PI_BELOW = float(np.nextafter(np.float32(np.pi), np.float32(0)))
    ctx = ExitStack()
    with ctx:
        def sb(n, shape, dt=F32):
            return ctx.enter_context(nc.sbuf_tensor(f"a0_{n}", shape, dt))

        def ps(n, shape):
            return ctx.enter_context(nc.psum_tensor(f"a0_{n}", shape, F32))

        def sem(n):
            return nc.alloc_semaphore(f"a0_{n}")

        env = dict(env)
        env.update(w_in=sb("w_in", [D, NQ]), b_in=sb("b_in", [P, NQ]), w_out=sb("w_out", [P, GB, D]), b_out=sb("b_out", [P, D]))
        quantum_composites(nc, env, q)

        wq, wk, wv, wo, wc, blocks = (sb(n, [D, D]) for n in ("wq", "wk", "wv", "wo", "wc", "blocks"))
        bq, bk, bc = sb("bq", [D, 1]), sb("bk", [D, 1]), sb("bc", [D, 1])
        bv, bo, g1, beta1, g2, beta2 = (sb(n, [P, D]) for n in ("bv", "bo", "g1", "beta1", "g2", "beta2"))
        half_pi = sb("half_pi", [P, 1])
        minus_half, eps = sb("minus_half", [P, GB]), sb("eps", [P, GB])
        norms = [dict(stat6=sb(f"stat6_{i}", [P, GB, 6]), mv=sb(f"mv_{i}", [P, GB, 2]), vare=sb(f"vare_{i}", [P, GB]), rstd=sb(f"rstd_{i}", [P, GB]),
                      bn=sem(f"bn_{i}"), stats=sem(f"stats_{i}"), var=sem(f"var_{i}"), ready=sem(f"rstd_ready_{i}")) for i in range(3)]
        xn = sb("xn", [P, 3, GB, D])
        xnT = sb("xnT", [D, T])
        qf, kf, qqn, qn = (sb(n, [D, 3, T]) for n in ("qf", "kf", "qqn", "qn"))
        V = sb("V", [P, 3, GB, D])
        qqf, kqf, rq, rk, kn16 = (sb(n, [D, T]) for n in ("qqf", "kqf", "rq", "rk", "kn16"))
        K_spread, C_spread, N_spread = (sb(n, [D, H, T]) for n in ("K_spread", "C_spread", "N_spread"))
        F, sn = sb("F", [P, GB, H, S]), sb("sn", [P, GB, H, S])
        Pr = sb("Pr", [P, 2, H, S])
        PT = sb("PT", [P, H, S])
        nm, nm8, rsum, rrec = sb("nm", [P, H]), sb("nm8", [P, 2, H]), sb("rsum", [P, 2, H]), sb("rrec", [P, H])
        on = sb("on", [P, GB, H, HD])
        oT, resid, r, x1, x1b, x1T, y, yh = (sb(n, [P, GB, D]) for n in ("oT", "resid", "r", "x1", "x1b", "x1T", "y", "yh"))
        qm, u, v, th, cs = (sb(n, [P, GB, NQ]) for n in ("qm", "u", "v", "th", "cs"))
        qe, qeT = sb("qe", [P, P]), sb("qeT", [P, P])

        cos_b, den_b = ps("cos_b", [P, 4, S]), ps("den_b", [P, 4, S])
        s_b = ps("s_b", [P, H, S])
        pt_b, o_b, mA, mB = ps("pt_b", [P, 4, S]), ps("o_b", [P, GB, H, HD]), ps("mA", [P, 512]), ps("mB", [P, 512])

        weights_in, zeroed, placed = sem("weights_in"), sem("zeroed"), sem("placed")
        (sp_waits_met, xn_ready, xnT_ps, xnT_sb, q_ps, q_sb, k_ps, k_sb, v_ps, v_sb, qq_ps, qq_sb, kq_ps, kq_sb, q2_ready, k2_ready, ssq_ps, qn_sb,
         ssk_ps, kn_sb, norm_chain, qqn_ready, kqn_ready, C_in, N_in, K_in, cos_sb, cd_ps, f_sb, f_clamped, sn_sb) = (sem(n) for n in (
             "sp_waits_met", "xn_ready", "xnT_ps", "xnT_sb", "q_ps", "q_sb", "k_ps", "k_sb", "v_ps", "v_sb", "qq_ps", "qq_sb", "kq_ps", "kq_sb", "q2_ready",
             "k2_ready", "ssq_ps", "qn_sb", "ssk_ps", "kn_sb", "norm_chain", "qqn_ready", "kqn_ready", "C_in", "N_in", "K_in", "cos_sb", "cd_ps", "f_sb", "f_clamped", "sn_sb"))
        (s_ps, g_sb, a_sb, nm_sb, nm8_sb, p_sb, t_ps, pt_sb, o_ps, rr_sb, o_sb, resid_ready, oT_ps, oT_sb, wo_ps, r_ready, xh_ready, x1_scaled, x1_ready,
         x1b_ready, xt_ps, xt_sb, qm_ps, qm_sb, v_chain, trig, qe_ready, qe_ps, qeT_sb, ff_ps, y_ready, yh_ready, z_chain, x_out) = (sem(n) for n in (
             "s_ps", "g_sb", "a_sb", "nm_sb", "nm8_sb", "p_sb", "t_ps", "pt_sb", "o_ps", "rr_sb", "o_sb", "resid_ready", "oT_ps", "oT_sb", "wo_ps", "r_ready",
             "xh_ready", "x1_scaled", "x1_ready", "x1b_ready", "xt_ps", "xt_sb", "qm_ps", "qm_sb", "v_chain", "trig", "qe_ready", "qe_ps", "qeT_sb", "ff_ps",
             "y_ready", "yh_ready", "z_chain", "x_out"))

        N_WEIGHTS = 12
        N_ZEROED = 11
        N = n_groups

        def loop(eng, iteration):
            groups_loop(eng, N, iteration, after=2)

        with nc.Block() as block:

            @block.sync
            def _(sp):
                for dst, src in ((wq, q["Wq"]), (wk, q["Wk"]), (wv, q["Wv"]), (wo, q["Wo"]), (bq, q["bq"]), (bk, q["bk"])):
                    sp.dma_start(dst[:, :], src).then_inc(weights_in, 16)
                for dst, src in ((bv, q["bv"]), (bo, q["bo"]), (g1, q["g1"]), (beta1, q["beta1"]), (g2, q["g2"]), (beta2, q["beta2"])):
                    sp.dma_start(dst[:, :], src.broadcast_to([P, D])).then_inc(weights_in, 16)
                sp.wait_ge(zeroed, N_ZEROED)
                for h in range(H):
                    r0 = HD * h
                    sp.dma_start(wc[r0:r0 + HD, r0:r0 + NQ], q["Wc2q"][h]).then_inc(placed, 16)
                    sp.dma_start(bc[r0:r0 + NQ, :], q["bc2q"][h].unsqueeze(1)).then_inc(placed, 16)
                    sp.dma_start(blocks[r0:r0 + HD, r0:r0 + HD], rq[0:HD, 0:HD]).then_inc(placed, 16)

                def spread(dst, src, done):
                    for h in range(H):
                        sp.dma_start(dst[HD * h:HD * (h + 1), h, :], src[HD * h:HD * (h + 1), :]).then_inc(done, 16)

                def iteration(g, k):
                    a, b, ka, kb = g + 2, g + 1, (k + 2) % 3, (k + 1) % 3
                    if does(g, 1, N):
                        sp.wait_ge(k_sb, b + 1)
                        sp.sem_inc(sp_waits_met, 1)
                        if counted(4 * b):
                            sp.wait_ge(s_ps, 4 * b)
                            sp.sem_inc(sp_waits_met, 1)
                        if counted(16 * H * b):
                            sp.wait_ge(K_in, 16 * H * b)
                            sp.sem_inc(sp_waits_met, 1)
                        spread(K_spread, kf[:, kb, :], K_in)
                    if does(g, 2, N):
                        sp.wait_ge(kn_sb, a + 1)
                        sp.sem_inc(sp_waits_met, 1)
                        if counted(8 * a):
                            sp.wait_ge(cd_ps, 8 * a)
                            sp.sem_inc(sp_waits_met, 1)
                        if counted(16 * H * a):
                            sp.wait_ge(N_in, 16 * H * a)
                            sp.sem_inc(sp_waits_met, 1)
                        spread(N_spread, kn16[:, :], N_in)
                        sp.wait_ge(kqn_ready, a + 1)
                        sp.sem_inc(sp_waits_met, 1)
                        if counted(16 * H * a):
                            sp.wait_ge(C_in, 16 * H * a)
                            sp.sem_inc(sp_waits_met, 1)
                        spread(C_spread, kqf[:, :], C_in)

                loop(sp, iteration)

            def inverse_deviation(pool, n, norm):
                pool.wait_ge(norm['stats'], n + 1)
                nc.gpsimd.tensor_tensor(norm["vare"][:, :], norm["mv"][:, :, 1], eps[:, :], ALU.add).then_inc(norm["var"], 1)
                pool.wait_ge(norm['var'], n + 1)
                nc.gpsimd.tensor_tensor(norm["rstd"][:, :], norm["vare"][:, :], minus_half[:, :], ALU.pow).then_inc(norm["ready"], 1)

            def statistics(dve, n, norm, src, src_ready, normed):
                dve.wait_ge(src_ready, n + 1)
                if counted(n):
                    dve.wait_ge(normed, n)
                for j in range(GB):
                    last = nc.vector.bn_stats(norm["stat6"][:, j, :], src[:, j, :])
                last.then_inc(norm["bn"], 1)
                dve.wait_ge(norm['bn'], n + 1)
                nc.vector.tensor_copy(spare[:, :], norm["stat6"][:, 0, 0:1])
                for j in range(GB):
                    last = nc.vector.bn_aggr(norm["mv"][:, j, :], norm["stat6"][:, j, :])
                last.then_inc(norm["stats"], 1)

            def normalise(norm, dst, src, done):
                for j in range(GB):
                    last = nc.vector.tensor_scalar(dst[:, j, :], src[:, j, :], norm["mv"][:, j, 0:1], norm["rstd"][:, j:j + 1], ALU.subtract, ALU.mult)
                last.then_inc(done, 1)

            spare = sb("spare", [P, 1])

            @block.gpsimd
            def _(pool):
                nc.gpsimd.memset(minus_half[:, :], -0.5).then_inc(zeroed, 1)
                nc.gpsimd.memset(eps[:, :], LN_EPS).then_inc(zeroed, 1)
                nc.gpsimd.memset(half_pi[:, :], math.pi / 2).then_inc(zeroed, 1)
                nc.gpsimd.memset(wc[:, :], 0.0).then_inc(zeroed, 1)
                nc.gpsimd.memset(bc[:, :], 0.0).then_inc(zeroed, 1)
                nc.gpsimd.memset(blocks[:, :], 0.0).then_inc(zeroed, 1)
                nc.gpsimd.memset(rq[:, :], 1.0).then_inc(zeroed, 1)
                nc.gpsimd.memset(qe[:, :], 0.0).then_inc(zeroed, 1)
                pool.wait_ge(weights_in, 16 * N_WEIGHTS)
                pool.wait_ge(placed, 16 * 3 * H)
                pool.wait_ge(zeroed, N_ZEROED)

                def by_channel(row):
                    return row[:, :].unsqueeze(1).broadcast_to([P, GB, D])

                def iteration(g, k):
                    a, d, e, ka = g + 2, g - 1, g - 2, (k + 2) % 3
                    if does(g, 2, N):
                        inverse_deviation(pool, a, norms[0])
                    if does(g, -1, N):
                        inverse_deviation(pool, d, norms[1])
                    if does(g, -2, N):
                        inverse_deviation(pool, e, norms[2])
                    if does(g, 2, N):
                        pool.wait_ge(qq_sb, a + 1)
                        if counted(a):
                            pool.wait_ge(qqn_ready, a)
                        nc.gpsimd.tensor_tensor(rq[:, :], qqf[:, :], qqf[:, :], ALU.mult).then_inc(q2_ready, 1)
                        pool.wait_ge(kq_sb, a + 1)
                        if counted(a):
                            pool.wait_ge(kqn_ready, a)
                        nc.gpsimd.tensor_tensor(rk[:, :], kqf[:, :], kqf[:, :], ALU.mult).then_inc(k2_ready, 1)
                    if does(g, -1, N):
                        pool.wait_ge(xh_ready, d + 1)
                        if counted(d):
                            pool.wait_ge(xt_ps, d)
                        nc.gpsimd.tensor_tensor(x1[:, :, :], r[:, :, :], by_channel(g1), ALU.mult).then_inc(x1_scaled, 1)
                        pool.wait_ge(x1_scaled, d + 1)
                        nc.gpsimd.tensor_tensor(x1[:, :, :], x1[:, :, :], by_channel(beta1), ALU.add).then_inc(x1_ready, 1)
                        pool.wait_ge(x1_ready, d + 1)
                        if counted(d):
                            pool.wait_ge(y_ready, d)
                        nc.gpsimd.tensor_tensor(x1b[:, :, :], x1[:, :, :], by_channel(env["b_out"]), ALU.add).then_inc(x1b_ready, 1)
                    if does(g, 0, N):
                        if counted(g):
                            pool.wait_ge(r_ready, g)
                        nc.gpsimd.tensor_tensor(resid[:, :, :], xn[:, k, :, :], by_channel(bo), ALU.add).then_inc(resid_ready, 1)
                    if does(g, -2, N):
                        pool.wait_ge(yh_ready, e + 1)
                        nc.gpsimd.tensor_tensor(yh[:, :, :], yh[:, :, :], by_channel(g2), ALU.mult).then_inc(z_chain, 1)
                        pool.wait_ge(z_chain, 2 * e + 1)
                        nc.gpsimd.tensor_tensor(yh[:, :, :], yh[:, :, :], by_channel(beta2), ALU.add).then_inc(z_chain, 1)
                        pool.wait_ge(z_chain, 2 * e + 2)
                        xg = x[:, bass.ds(GB * e, GB), :]
                        nc.gpsimd.tensor_tensor(xg, xg, yh[:, :, :], ALU.add).then_inc(x_out, 1)

                loop(pool, iteration)
                pool.wait_ge(x_out, N)



            @block.scalar
            def _(act):
                act.wait_ge(weights_in, 16 * N_WEIGHTS)
                act.wait_ge(placed, 16 * 3 * H)
                act.wait_ge(zeroed, N_ZEROED)

                def cosines(g, b, j, half):
                    n = 8 * b + 2 * j + half
                    act.wait_ge(cd_ps, n + 1)
                    if counted(GB * g + j + 1):
                        act.wait_ge(g_sb, GB * g + j + 1)
                    nc.scalar.activation(F[:, j, 4 * half:4 * half + 4, :], cos_b[:, :, :], ACT.Copy).then_inc(cos_sb, 1)

                def iteration(g, k):
                    a, b, d, e, ka = g + 2, g + 1, g - 1, g - 2, (k + 2) % 3
                    A, B, C, DD, E = (does(g, s, N) for s in (2, 1, 0, -1, -2))
                    for j in range(GB):
                        if C:
                            n = GB * g + j
                            act.wait_ge(nm8_sb, n + 1)
                            if counted(n - 1):
                                act.wait_ge(o_sb, n - 1)
                            for h in range(H):
                                last = nc.scalar.activation(Pr[:, j % 2, h, :], Pr[:, j % 2, h, :], ACT.Exp, bias=nm8[:, j % 2, h:h + 1], scale=0.125,
                                                            accum_out=rsum[:, j % 2, h:h + 1])
                            last.then_inc(p_sb, 1)
                        for half in range(2):
                            if C:
                                act.wait_ge(t_ps, 2 * n + half + 1)
                                if half == 0:
                                    if counted(n):
                                        act.wait_ge(o_ps, n)
                                nc.scalar.activation(PT[:, 4 * half:4 * half + 4, :], pt_b[:, :, :], ACT.Copy).then_inc(pt_sb, 1)
                            if B:
                                cosines(g, b, j, half)
                        if j == 0:
                            if DD:
                                act.wait_ge(oT_ps, d + 1)
                                if counted(d):
                                    act.wait_ge(wo_ps, d)
                                nc.scalar.activation(oT[:, :, :].rearrange("p a b -> p (a b)"), mB[:, :], ACT.Copy).then_inc(oT_sb, 1)
                            if A:
                                act.wait_ge(xnT_ps, a + 1)
                                if counted(a):
                                    act.wait_ge(v_ps, a)
                                nc.scalar.activation(xnT[:, :], mA[:, :], ACT.Copy).then_inc(xnT_sb, 1)
                            if E:
                                act.wait_ge(qe_ps, e + 1)
                                if counted(e):
                                    act.wait_ge(ff_ps, e)
                                nc.scalar.activation(qeT[:, :], mA[:, 0:P], ACT.Copy).then_inc(qeT_sb, 1)
                        if j == 0 and A:
                            act.wait_ge(q_ps, a + 1)
                            if counted(4 * (a - 2)):
                                act.wait_ge(s_ps, 4 * (a - 2))
                            nc.scalar.activation(qf[:, ka, :], mB[:, :], ACT.Identity, bias=bq[:, 0:1]).then_inc(q_sb, 1)
                            act.wait_ge(k_ps, a + 1)
                            if counted(16 * H * (a - 2)):
                                act.wait_ge(K_in, 16 * H * (a - 2))
                            nc.scalar.activation(kf[:, ka, :], mA[:, :], ACT.Identity, bias=bk[:, 0:1]).then_inc(k_sb, 1)
                        if j == 1 and A:
                            act.wait_ge(qq_ps, a + 1)
                            if counted(a):
                                act.wait_ge(qqn_ready, a)
                            nc.scalar.activation(qqf[:, :], mA[:, :], ACT.Identity, bias=bc[:, 0:1]).then_inc(qq_sb, 1)
                            act.wait_ge(kq_ps, a + 1)
                            if counted(16 * H * a):
                                act.wait_ge(C_in, 16 * H * a)
                            nc.scalar.activation(kqf[:, :], mB[:, :], ACT.Identity, bias=bc[:, 0:1]).then_inc(kq_sb, 1)
                        if j == 2:
                            if A:
                                act.wait_ge(ssq_ps, a + 1)
                                if counted(8 * (a - 2)):
                                    act.wait_ge(cd_ps, 8 * (a - 2))
                                nc.scalar.activation(qn[:, ka, :], mA[:, :], ACT.Sqrt).then_inc(qn_sb, 1)
                                act.wait_ge(ssk_ps, a + 1)
                                if counted(16 * H * a):
                                    act.wait_ge(N_in, 16 * H * a)
                                if counted(a):
                                    act.wait_ge(kqn_ready, a)
                                nc.scalar.activation(kn16[:, :], mB[:, :], ACT.Sqrt, scale=2.0 ** -8).then_inc(kn_sb, 1)
                            if DD:
                                act.wait_ge(xt_ps, d + 1)
                                if counted(d):
                                    act.wait_ge(qm_ps, d)
                                nc.scalar.activation(x1T[:, :, :].rearrange("p a b -> p (a b)"), mB[:, :], ACT.Copy).then_inc(xt_sb, 1)
                    if DD:
                        act.wait_ge(v_chain, 4 * d + 4)
                        if counted(d):
                            act.wait_ge(qe_ready, d)
                        nc.scalar.activation(th[:, :, :], qm[:, :, :], ACT.Tanh).then_inc(trig, 1)
                        nc.scalar.activation(cs[:, :, :], v[:, :, :], ACT.Sin, bias=half_pi[:, 0:1], scale=-2 * math.pi).then_inc(trig, 1)
                    if B:
                        for j in range(GB):
                            act.wait_ge(f_clamped, GB * b + j + 1)
                            if counted(GB * g + j + 1):
                                act.wait_ge(a_sb, GB * g + j + 1)
                            nc.scalar.activation(sn[:, j, :, :], F[:, j, :, :], ACT.Sin, scale=PI_BELOW).then_inc(sn_sb, 1)

                loop(act, iteration)

            @block.vector
            def _(dve):
                for t in (K_spread, C_spread, N_spread):
                    nc.vector.memset(t[:, :, :], 0.0).then_inc(zeroed, 1)
                dve.wait_ge(weights_in, 16 * N_WEIGHTS)
                dve.wait_ge(placed, 16 * 3 * H)
                dve.wait_ge(zeroed, N_ZEROED)

                def logits(g, j):
                    n = GB * g + j
                    dve.wait_ge(sn_sb, n + 1)
                    nc.vector.scalar_tensor_tensor(sn[:, j, :, :], sn[:, j, :, :], 10.0, F[:, j, :, :], ALU.add, ALU.mult).then_inc(g_sb, 1)
                    dve.wait_ge(g_sb, n + 1)
                    dve.wait_ge(s_ps, n + 1)
                    if counted(2 * (n - 1)):
                        dve.wait_ge(t_ps, 2 * (n - 1))
                    nc.vector.scalar_tensor_tensor(Pr[:, j % 2, :, :], sn[:, j, :, :], 0.4, s_b[:, :, :], ALU.mult, ALU.add).then_inc(a_sb, 1)

                def shift(g, j):
                    n = GB * g + j
                    dve.wait_ge(a_sb, n + 1)
                    if counted(n):
                        dve.wait_ge(nm8_sb, n)
                    nc.vector.tensor_reduce(nm[:, :], Pr[:, j % 2, :, :], axis=AX.X, op=ALU.max, negate=True).then_inc(nm_sb, 1)
                    dve.wait_ge(nm_sb, n + 1)
                    if counted(n - 1):
                        dve.wait_ge(p_sb, n - 1)
                    nc.vector.tensor_scalar(nm8[:, j % 2, :], nm[:, :], 0.125, 0.0, ALU.mult, ALU.add).then_inc(nm8_sb, 1)

                def fidelity(g, b, j, half):
                    n = 8 * b + 2 * j + half
                    fh = F[:, j, 4 * half:4 * half + 4, :]
                    dve.wait_ge(cos_sb, n + 1)
                    nc.vector.scalar_tensor_tensor(fh, den_b[:, :, :], EPS_COS, fh, ALU.min, ALU.mult).then_inc(f_sb, 1)

                def iteration(g, k):
                    a, b, d, e, ka, kb = g + 2, g + 1, g - 1, g - 2, (k + 2) % 3, (k + 1) % 3
                    A, B, C, DD, E = (does(g, s, N) for s in (2, 1, 0, -1, -2))
                    if E:
                        dve.wait_ge(trig, 2 * e + 2)
                        if counted(e):
                            dve.wait_ge(qe_ps, e)
                        nc.vector.tensor_tensor(qe[:, 0:GB * NQ].rearrange("p (a b) -> p a b", a=GB), th[:, :, :], cs[:, :, :], ALU.mult).then_inc(qe_ready, 1)
                    if C:
                        logits(g, 0)
                        shift(g, 0)
                    if A:
                        if counted(a):
                            dve.wait_ge(xn_ready, a)
                        for j in range(GB):
                            last = nc.vector.bn_stats(norms[0]["stat6"][:, j, :], x[:, bass.ds(GB * a + j, 1), :].rearrange("p o c -> p (o c)"))
                        last.then_inc(norms[0]["bn"], 1)
                        dve.wait_ge(norms[0]['bn'], a + 1)
                        nc.vector.tensor_copy(spare[:, :], norms[0]["stat6"][:, 0, 0:1])
                        for j in range(GB):
                            last = nc.vector.bn_aggr(norms[0]["mv"][:, j, :], norms[0]["stat6"][:, j, :])
                        last.then_inc(norms[0]["stats"], 1)
                    if A:
                        dve.wait_ge(norms[0]['ready'], a + 1)
                        if counted(a - 2):
                            dve.wait_ge(resid_ready, a - 2)
                        for j in range(GB):
                            last = nc.vector.tensor_scalar(xn[:, ka, j, :], x[:, bass.ds(GB * a + j, 1), :].rearrange("p o c -> p (o c)"),
                                                           norms[0]["mv"][:, j, 0:1], norms[0]["rstd"][:, j:j + 1], ALU.subtract, ALU.mult)
                        last.then_inc(xn_ready, 1)
                    for j in range(GB):
                        if j == 2:
                            if DD:
                                dve.wait_ge(norms[1]['ready'], d + 1)
                                normalise(norms[1], r, r, xh_ready)
                            if E:
                                dve.wait_ge(norms[2]['ready'], e + 1)
                                if counted(e):
                                    dve.wait_ge(x_out, e)
                                normalise(norms[2], yh, y, yh_ready)
                        if j == 3 and A:
                            nc.vector.reciprocal(rq[:, :], rq[:, :]).then_inc(norm_chain, 1)
                            dve.wait_ge(norm_chain, 4 * a + 4)
                            nc.vector.tensor_tensor(qqn[:, ka, :], qqf[:, :], rq[:, :], ALU.mult).then_inc(qqn_ready, 1)
                        if C and j < 3:
                            logits(g, j + 1)
                        if B:
                            fidelity(g, b, j, 0)
                        if C and j < 3:
                            shift(g, j + 1)
                        if B:
                            fidelity(g, b, j, 1)
                            dve.wait_ge(f_sb, 8 * b + 2 * j + 2)
                            nc.vector.tensor_scalar(F[:, j, :, :], F[:, j, :, :], 1.0, -1.0, ALU.min, ALU.max).then_inc(f_clamped, 1)
                        if j == 1:
                            if DD:
                                dve.wait_ge(wo_ps, d + 1)
                                dve.wait_ge(resid_ready, d + 1)
                                if counted(d):
                                    dve.wait_ge(x1_scaled, d)
                                nc.vector.tensor_tensor(r[:, :, :], mB[:, :].rearrange("p (a b) -> p a b", a=GB), resid[:, :, :], ALU.add).then_inc(r_ready, 1)
                                statistics(dve, d, norms[1], r, r_ready, xh_ready)
                            if E:
                                dve.wait_ge(ff_ps, e + 1)
                                dve.wait_ge(x1b_ready, e + 1)
                                if counted(e):
                                    dve.wait_ge(yh_ready, e)
                                nc.vector.tensor_tensor(y[:, :, :], mA[:, :].rearrange("p (a b) -> p a b", a=GB), x1b[:, :, :], ALU.add).then_inc(y_ready, 1)
                                statistics(dve, e, norms[2], y, y_ready, yh_ready)
                        if j == 2 and A:
                            dve.wait_ge(v_ps, a + 1)
                            if counted(4 * (a - 2)):
                                dve.wait_ge(o_ps, 4 * (a - 2))
                            nc.vector.tensor_tensor(V[:, ka, :, :], mB[:, :].rearrange("p (a b) -> p a b", a=GB),
                                                    bv[:, :].unsqueeze(1).broadcast_to([P, GB, D]), ALU.add).then_inc(v_sb, 1)
                            dve.wait_ge(kn_sb, a + 1)
                            nc.vector.tensor_scalar(rk[:, :], kn16[:, :], TINY, 1.0, ALU.max, ALU.mult).then_inc(norm_chain, 1)
                            dve.wait_ge(qn_sb, a + 1)
                            nc.vector.tensor_scalar(rq[:, :], qn[:, ka, :], TINY, 1.0, ALU.max, ALU.mult).then_inc(norm_chain, 1)
                            dve.wait_ge(norm_chain, 4 * a + 2)
                            nc.vector.reciprocal(rk[:, :], rk[:, :]).then_inc(norm_chain, 1)
                            dve.wait_ge(norm_chain, 4 * a + 3)
                            nc.vector.scalar_tensor_tensor(kqf[:, :], kqf[:, :], 1.0 / (16 * EPS_COS), rk[:, :], ALU.mult, ALU.mult).then_inc(kqn_ready, 1)
                        if j == 3 and DD:
                            dve.wait_ge(qm_ps, d + 1)
                            if counted(2 * d):
                                dve.wait_ge(trig, 2 * d)
                            nc.vector.tensor_tensor(qm[:, :, :], mB[:, 0:GB * NQ].rearrange("p (a b) -> p a b", a=GB),
                                                    env["b_in"][:, :].unsqueeze(1).broadcast_to([P, GB, NQ]), ALU.add).then_inc(qm_sb, 1)
                            dve.wait_ge(qm_sb, d + 1)
                            nc.vector.tensor_scalar(u[:, :, :], qm[:, :, :], 0.125, MAGIC, ALU.mult, ALU.add).then_inc(v_chain, 1)
                            dve.wait_ge(v_chain, 4 * d + 1)
                            nc.vector.tensor_scalar(u[:, :, :], u[:, :, :], MAGIC, 0.0, ALU.subtract, ALU.add).then_inc(v_chain, 1)
                            dve.wait_ge(v_chain, 4 * d + 2)
                            nc.vector.scalar_tensor_tensor(u[:, :, :], qm[:, :, :], 0.125, u[:, :, :], ALU.mult, ALU.subtract).then_inc(v_chain, 1)
                            dve.wait_ge(v_chain, 4 * d + 3)
                            nc.vector.scalar_tensor_tensor(v[:, :, :], u[:, :, :], -1.0, u[:, :, :], ALU.mult, ALU.max).then_inc(v_chain, 1)
                        if C:
                            n = GB * g + j
                            dve.wait_ge(p_sb, n + 1)
                            if counted(n):
                                dve.wait_ge(o_sb, n)
                            nc.vector.reciprocal(rrec[:, :], rsum[:, j % 2, :]).then_inc(rr_sb, 1)
                            dve.wait_ge(rr_sb, n + 1)
                            dve.wait_ge(o_ps, n + 1)
                            if counted(g):
                                dve.wait_ge(oT_ps, g)
                            nc.vector.tensor_tensor(on[:, j, :, :], o_b[:, j, :, :], rrec[:, :].unsqueeze(2).broadcast_to([P, H, HD]), ALU.mult).then_inc(o_sb, 1)

                loop(dve, iteration)

            @block.tensor
            def _(pe):
                pe.wait_ge(weights_in, 16 * N_WEIGHTS)
                pe.wait_ge(placed, 16 * 3 * H)
                pe.wait_ge(zeroed, N_ZEROED)

                def scores(g, k, j):
                    n = GB * g + j
                    if counted(16 * H * (g + 1)):
                        pe.wait_ge(K_in, 16 * H * (g + 1))
                    if counted(n):
                        pe.wait_ge(a_sb, n)
                    for half in range(2):
                        hs = slice(4 * half, 4 * half + 4)
                        last = nc.tensor.matmul(s_b[:, hs, :], qf[:, k, j * S:(j + 1) * S], K_spread[:, hs, j * S:(j + 1) * S], start=True, stop=True)
                    last.then_inc(s_ps, 1)

                def fidelity_products(b, kb, j, half):
                    pe.wait_ge(C_in, 16 * H * (b + 1))
                    pe.wait_ge(N_in, 16 * H * (b + 1))
                    pe.wait_ge(qqn_ready, b + 1)
                    if counted(8 * b + 2 * j + half):
                        pe.wait_ge(f_sb, 8 * b + 2 * j + half)
                    hs, js = slice(4 * half, 4 * half + 4), slice(j * S, (j + 1) * S)
                    nc.tensor.matmul(cos_b[:, :, :], qqn[:, kb, js], C_spread[:, hs, js], start=True, stop=True)
                    nc.tensor.matmul(den_b[:, :, :], qn[:, kb, js], N_spread[:, hs, js], start=True, stop=True).then_inc(cd_ps, 1)

                def transposed(g, j, half):
                    n = GB * g + j
                    pe.wait_ge(p_sb, n + 1)
                    if counted(2 * n + half):
                        pe.wait_ge(pt_sb, 2 * n + half)
                    for h in range(4):
                        last = nc.tensor.transpose(pt_b[:, h, :], Pr[:, j % 2, 4 * half + h, :], ident[:, :])
                    last.then_inc(t_ps, 1)

                def four_transposes(bank, src, done):
                    for j in range(GB):
                        last = nc.tensor.transpose(bank[:, j * S:(j + 1) * S], src[:, j, :], ident[:, :])
                    last.then_inc(done, 1)

                def iteration(g, k):
                    a, b, d, e, ka, kb = g + 2, g + 1, g - 1, g - 2, (k + 2) % 3, (k + 1) % 3
                    A, B, C, DD, E = (does(g, s, N) for s in (2, 1, 0, -1, -2))
                    A_done = through(g, 2, N)
                    D_done, E_done = through(g, -1, N), through(g, -2, N)
                    if C:
                        scores(g, k, 0)
                    for j in range(GB):
                        if C and j < 3:
                            scores(g, k, j + 1)
                        for half in range(2):
                            if C:
                                transposed(g, j, half)
                            if B:
                                fidelity_products(b, kb, j, half)
                        if j == 0:
                            if counted(before(g, 2, N)):
                                pe.wait_ge(qn_sb, before(g, 2, N))
                            if counted(before(g, 2, N)):
                                pe.wait_ge(kn_sb, before(g, 2, N))
                            if counted(before(g, -1, N)):
                                pe.wait_ge(qm_sb, before(g, -1, N))
                            if counted(before(g, -2, N)):
                                pe.wait_ge(y_ready, before(g, -2, N))
                            if DD:
                                pe.wait_ge(o_sb, GB * d + GB)
                                four_transposes(mB, on[:, :, :, :].rearrange("p a h c -> p a (h c)"), oT_ps)
                            if A:
                                pe.wait_ge(xn_ready, a + 1)
                                four_transposes(mA, xn[:, ka, :, :], xnT_ps)
                            if E:
                                pe.wait_ge(qe_ready, e + 1)
                                if counted(A_done):
                                    pe.wait_ge(xnT_sb, A_done)
                                nc.tensor.transpose(mA[:, 0:P], qe[:, :], ident[:, :]).then_inc(qe_ps, 1)
                            if A:
                                pe.wait_ge(xnT_sb, a + 1)
                                if counted(D_done):
                                    pe.wait_ge(oT_sb, D_done)
                                nc.tensor.matmul(mB[:, :], wq[:, :], xnT[:, :], start=True, stop=True).then_inc(q_ps, 1)
                                if counted(E_done):
                                    pe.wait_ge(qeT_sb, E_done)
                                nc.tensor.matmul(mA[:, :], wk[:, :], xnT[:, :], start=True, stop=True).then_inc(k_ps, 1)
                        if j == 1:
                            if DD:
                                pe.wait_ge(oT_sb, d + 1)
                                if counted(A_done):
                                    pe.wait_ge(q_sb, A_done)
                                for i in range(GB):
                                    last = nc.tensor.matmul(mB[:, i * D:(i + 1) * D], oT[:, i, :], wo[:, :], start=True, stop=True)
                                last.then_inc(wo_ps, 1)
                            if A:
                                pe.wait_ge(k_sb, a + 1)
                                nc.tensor.matmul(mA[:, :], wc[:, :], qf[:, ka, :], start=True, stop=True).then_inc(qq_ps, 1)
                                pe.wait_ge(q_sb, a + 1)
                                if counted(D_done):
                                    pe.wait_ge(r_ready, D_done)
                                nc.tensor.matmul(mB[:, :], wc[:, :], kf[:, ka, :], start=True, stop=True).then_inc(kq_ps, 1)
                            if E:
                                pe.wait_ge(qeT_sb, e + 1)
                                if counted(A_done):
                                    pe.wait_ge(k_sb, A_done)
                                if counted(A_done):
                                    pe.wait_ge(qq_sb, A_done)
                                nc.tensor.matmul(mA[:, :], qeT[:, :], env["w_out"][:, :, :], start=True, stop=True).then_inc(ff_ps, 1)
                        if j == 2:
                            if A:
                                pe.wait_ge(kq_sb, a + 1)
                                for i in range(GB):
                                    last = nc.tensor.matmul(mB[:, i * D:(i + 1) * D], xnT[:, i * S:(i + 1) * S], wv[:, :], start=True, stop=True)
                                last.then_inc(v_ps, 1)
                                pe.wait_ge(q2_ready, a + 1)
                                pe.wait_ge(qq_sb, a + 1)
                                if counted(E_done):
                                    pe.wait_ge(y_ready, E_done)
                                nc.tensor.matmul(mA[:, :], blocks[:, :], rq[:, :], start=True, stop=True).then_inc(ssq_ps, 1)
                                pe.wait_ge(k2_ready, a + 1)
                                pe.wait_ge(v_sb, a + 1)
                                nc.tensor.matmul(mB[:, :], blocks[:, :], rk[:, :], start=True, stop=True).then_inc(ssk_ps, 1)
                            if DD:
                                pe.wait_ge(x1_ready, d + 1)
                                if counted(A_done):
                                    pe.wait_ge(kn_sb, A_done)
                                pe.wait_ge(r_ready, d + 1)
                                four_transposes(mB, x1, xt_ps)
                        if j == 3 and DD:
                            pe.wait_ge(xt_sb, d + 1)
                            for i in range(GB):
                                last = nc.tensor.matmul(mB[:, i * NQ:(i + 1) * NQ], x1T[:, i, :], env["w_in"][:, :], start=True, stop=True)
                            last.then_inc(qm_ps, 1)
                        if C:
                            n = GB * g + j
                            pe.wait_ge(pt_sb, 2 * n + 2)
                            pe.wait_ge(v_sb, g + 1)
                            if counted(n):
                                pe.wait_ge(o_sb, n)
                            for h in range(H):
                                last = nc.tensor.matmul(o_b[:, j, h, :], PT[:, h, :], V[:, k, j, h * HD:(h + 1) * HD], start=True, stop=True)
                            last.then_inc(o_ps, 1)

                loop(pe, iteration)


EXPERTS, INNER = 8, 352


def experts(nc, env, n_groups, w):
    x, ident = env["x"], env["ident"]
    rows = [min(P, INNER - P * c) for c in range(-(-INNER // P))]
    CH = len(rows)
    N = n_groups
    NS = GB * N
    NT = NS + EXPERTS
    MAGIC = 1.5 * 2.0 ** 23
    U32 = mybir.dt.uint32
    ctx = ExitStack()
    with ctx:
        def sb(n, shape, dt=F32, stack=ctx):
            return stack.enter_context(nc.sbuf_tensor(f"moe_{n}", shape, dt))

        def sem(n):
            return nc.alloc_semaphore(f"moe_{n}")

        gate, up = sb("gate", [D, EXPERTS, INNER]), sb("up", [D, EXPERTS, INNER])
        down = sb("down", [P, CH, EXPERTS, D])
        xn = sb("xn", [P, NS, D])
        chosen = sb("chosen", [P, NS, EXPERTS])
        slot = sb("slot", [P, NS], U32)
        expert = sb("expert", [P, NT], mybir.dt.int32)
        Xs = nc.dram_tensor("moe_Xs", [NT * P, D], F32, kind="Internal").ap()
        Ys = nc.dram_tensor("moe_Ys", [NT * P, D], F32, kind="Internal").ap()

        route = ExitStack()
        with route:
            def rb(n, shape, dt=F32):
                return sb(n, shape, dt, route)

            router = rb("router", [D, EXPERTS])
            rank = rb("rank", [P, EXPERTS])
            minus_half, eps = rb("minus_half", [P, GB]), rb("eps", [P, GB])
            stat6, mv, vare, rstd, spare = rb("stat6", [P, GB, 6]), rb("mv", [P, GB, 2]), rb("vare", [P, GB]), rb("rstd", [P, GB]), rb("spare", [P, 1])
            fresh, xnT = rb("fresh", [P, 3, GB, D]), rb("xnT", [D, T])
            top, score, first = rb("top", [P, GB]), rb("score", [P, GB, EXPERTS]), rb("first", [P, GB])
            zero = rb("zero", [P, 512])
            t_b = route.enter_context(nc.psum_tensor("moe_t_b", [P, 512], F32))
            l_b = route.enter_context(nc.psum_tensor("moe_l_b", [P, GB, EXPERTS], F32))
            weights_in, router_in, consts, zeroed, down_zero = sem("weights_in"), sem("router_in"), sem("consts"), sem("zeroed"), sem("down_zero")
            bn_done, stats, var_ready, rstd_ready, xn_ready = (sem(n) for n in ("bn_done", "stats", "var_ready", "rstd_ready", "xn_ready"))
            kept = sem("kept")
            xnT_ps, xnT_sb, logits_ps, top_sb, score_sb, first_sb, chosen_sb = (
                sem(n) for n in ("xnT_ps", "xnT_sb", "logits_ps", "top_sb", "score_sb", "first_sb", "chosen_sb"))

            with nc.Block() as block:

                @block.sync
                def _(sp):
                    sp.dma_start(router[:, :], w["router"]).then_inc(router_in, 16)
                    sp.wait_ge(consts, 3 + EXPERTS)
                    sp.dma_start(Xs.rearrange("(p a) c -> p (a c)", p=P), zero[:, :].unsqueeze(1).broadcast_to([P, NT * D // 512, 512])).then_inc(zeroed, 16)
                    sp.dma_start(gate[:, :, :], w["gate"]).then_inc(weights_in, 16)
                    sp.dma_start(up[:, :, :], w["up"]).then_inc(weights_in, 16)
                    sp.wait_ge(down_zero, 1)
                    for c in range(CH):
                        sp.dma_start(down[0:rows[c], c, :, :], w["down"][c * P:c * P + rows[c], :, :]).then_inc(weights_in, 16)
                    sp.wait_ge(weights_in, 16 * (2 + CH))
                    sp.wait_ge(zeroed, 16)

                @block.gpsimd
                def _(pool):
                    nc.gpsimd.memset(minus_half[:, :], -0.5).then_inc(consts, 1)
                    nc.gpsimd.memset(eps[:, :], LN_EPS).then_inc(consts, 1)
                    nc.gpsimd.memset(zero[:, :], 0.0).then_inc(consts, 1)
                    for e in range(EXPERTS):
                        nc.gpsimd.memset(rank[:, e:e + 1], float(EXPERTS - e)).then_inc(consts, 1)
                    pool.wait_ge(consts, 3 + EXPERTS)

                    def iteration(g, k):
                        a = g + 2
                        if does(g, 2, N):
                            pool.wait_ge(stats, a + 1)
                            nc.gpsimd.tensor_tensor(vare[:, :], mv[:, :, 1], eps[:, :], ALU.add).then_inc(var_ready, 1)
                            pool.wait_ge(var_ready, a + 1)
                            nc.gpsimd.tensor_tensor(rstd[:, :], vare[:, :], minus_half[:, :], ALU.pow).then_inc(rstd_ready, 1)

                    groups_loop(pool, N, iteration)

                @block.scalar
                def _(act):
                    def iteration(g, k):
                        b = g + 1
                        if does(g, 1, N):
                            act.wait_ge(xnT_ps, b + 1)
                            if counted(b):
                                act.wait_ge(logits_ps, b)
                            nc.scalar.activation(xnT[:, :], t_b[:, :], ACT.Copy).then_inc(xnT_sb, 1)
                            nc.scalar.activation(xn[:, bass.ds(GB * b, GB), :], fresh[:, (k + 1) % 3, :, :], ACT.Copy).then_inc(kept, 1)

                    groups_loop(act, N, iteration)
                    act.wait_ge(kept, N)

                @block.vector
                def _(dve):
                    nc.vector.memset(down[:, :, :, :], 0.0).then_inc(down_zero, 1)
                    dve.wait_ge(consts, 3 + EXPERTS)

                    def iteration(g, k):
                        a = g + 2
                        if does(g, 2, N):
                            if counted(a):
                                dve.wait_ge(xn_ready, a)
                            for j in range(GB):
                                last = nc.vector.bn_stats(stat6[:, j, :], x[:, bass.ds(GB * a + j, 1), :].rearrange("p o c -> p (o c)"))
                            last.then_inc(bn_done, 1)
                            dve.wait_ge(bn_done, a + 1)
                            nc.vector.tensor_copy(spare[:, :], stat6[:, 0, 0:1])
                            for j in range(GB):
                                last = nc.vector.bn_aggr(mv[:, j, :], stat6[:, j, :])
                            last.then_inc(stats, 1)
                        if does(g, 0, N):
                            dve.wait_ge(logits_ps, g + 1)
                            nc.vector.tensor_reduce(top[:, :], l_b[:, :, :], axis=AX.X, op=ALU.max).then_inc(top_sb, 1)
                            dve.wait_ge(top_sb, g + 1)
                            nc.vector.tensor_tensor(score[:, :, :], l_b[:, :, :], top[:, :].unsqueeze(2).broadcast_to([P, GB, EXPERTS]), ALU.is_equal).then_inc(score_sb, 1)
                            dve.wait_ge(score_sb, 2 * g + 1)
                            nc.vector.tensor_tensor(score[:, :, :], score[:, :, :], rank[:, :].unsqueeze(1).broadcast_to([P, GB, EXPERTS]), ALU.mult).then_inc(score_sb, 1)
                            dve.wait_ge(score_sb, 2 * g + 2)
                            nc.vector.tensor_reduce(first[:, :], score[:, :, :], axis=AX.X, op=ALU.max).then_inc(first_sb, 1)
                            dve.wait_ge(first_sb, g + 1)
                            nc.vector.tensor_tensor(chosen[:, bass.ds(GB * g, GB), :], score[:, :, :],
                                                    first[:, :].unsqueeze(2).broadcast_to([P, GB, EXPERTS]), ALU.is_equal).then_inc(chosen_sb, 1)
                        if does(g, 2, N):
                            dve.wait_ge(rstd_ready, a + 1)
                            if counted(a - 2):
                                dve.wait_ge(kept, a - 2)
                            for j in range(GB):
                                tile = bass.ds(GB * a + j, 1)
                                last = nc.vector.tensor_scalar(fresh[:, (k + 2) % 3, j, :], x[:, tile, :].rearrange("p o c -> p (o c)"),
                                                               mv[:, j, 0:1], rstd[:, j:j + 1], ALU.subtract, ALU.mult)
                            last.then_inc(xn_ready, 1)

                    groups_loop(dve, N, iteration)
                    dve.wait_ge(chosen_sb, N)

                @block.tensor
                def _(pe):
                    pe.wait_ge(router_in, 16)

                    def iteration(g, k):
                        b = g + 1
                        if does(g, 0, N):
                            pe.wait_ge(xnT_sb, g + 1)
                            if counted(2 * g):
                                pe.wait_ge(score_sb, 2 * g)
                            for j in range(GB):
                                last = nc.tensor.matmul(l_b[:, j, :], xnT[:, j * S:(j + 1) * S], router[:, :], start=True, stop=True)
                            last.then_inc(logits_ps, 1)
                        if does(g, 1, N):
                            pe.wait_ge(xn_ready, b + 1)
                            if counted(b):
                                pe.wait_ge(xnT_sb, b)
                            for j in range(GB):
                                last = nc.tensor.transpose(t_b[:, j * S:(j + 1) * S], fresh[:, (k + 1) % 3, j, :], ident[:, :])
                            last.then_inc(xnT_ps, 1)

                    groups_loop(pe, N, iteration)

        ranks = ExitStack()
        with ranks:
            def kb(n, shape, dt=F32):
                return sb(n, shape, dt, ranks)

            earlier = kb("earlier", [P, P])
            earlier_bf, ones_bf, chosen_bf = kb("earlier_bf", [P, P], BF16), kb("ones_bf", [P, P], BF16), kb("chosen_bf", [P, NS, EXPERTS], BF16)
            total = [kb(f"total{i}", [P, NS, EXPERTS]) for i in range(2)]
            size, padded = kb("size", [P, EXPERTS]), kb("padded", [P, EXPERTS])
            base = [kb(f"base{i}", [P, EXPERTS]) for i in range(2)]
            slot_f, index, begun, expert_f = kb("slot_f", [P, NS]), kb("index", [P, P]), kb("begun", [P, NT, EXPERTS]), kb("expert_f", [P, NT])
            within_b, count_b, index_b = (ranks.enter_context(nc.psum_tensor(f"moe_{n}_b", s, F32)) for n, s in
                                          (("within", [P, NS, EXPERTS]), ("count", [P, NS, EXPERTS]), ("index", [P, P])))
            built, copied, counted_ps, step, scattered = sem("built"), sem("copied"), sem("counted_ps"), sem("step"), sem("scattered")

            with nc.Block() as block:

                @block.gpsimd
                def _(pool):
                    nc.gpsimd.memset(earlier[:, :], 0.0).then_inc(built, 1)
                    nc.gpsimd.memset(ones_bf[:, :], 1.0).then_inc(built, 1)
                    pool.wait_ge(built, 2)
                    nc.gpsimd.affine_select(out=earlier[:, :], in_=earlier[:, :], compare_op=ALU.is_ge, fill=1.0,
                                            base=0, pattern=[[-1, P]], channel_multiplier=1).then_inc(built, 1)
                    pool.wait_ge(built, 3)

                @block.tensor
                def _(pe):
                    pe.wait_ge(built, 3)
                    pe.wait_ge(copied, 2)
                    nc.tensor.matmul(within_b[:, :, :], earlier_bf[:, :], chosen_bf[:, :, :], start=True, stop=True).then_inc(counted_ps, 1)
                    nc.tensor.matmul(count_b[:, :, :], ones_bf[:, :], chosen_bf[:, :, :], start=True, stop=True).then_inc(counted_ps, 1)
                    nc.tensor.matmul(index_b[:, :], ones_bf[:, :], earlier_bf[:, :], start=True, stop=True).then_inc(counted_ps, 1)

                @block.vector
                def _(dve):
                    dve.wait_ge(built, 3)
                    nc.vector.tensor_copy(earlier_bf[:, :], earlier[:, :]).then_inc(copied, 1)
                    nc.vector.tensor_copy(chosen_bf[:, :, :], chosen[:, :, :]).then_inc(copied, 1)
                    dve.wait_ge(counted_ps, 3)
                    nc.vector.tensor_copy(total[0][:, :, :], count_b[:, :, :]).then_inc(step, 1)
                    steps = 1
                    src, shift = 0, 1
                    while shift < NS:
                        if counted(steps):
                            dve.wait_ge(step, steps)
                        nc.vector.tensor_copy(total[1 - src][:, 0:shift, :], total[src][:, 0:shift, :]).then_inc(step, 1)
                        nc.vector.tensor_tensor(total[1 - src][:, shift:, :], total[src][:, shift:, :], total[src][:, :NS - shift, :], ALU.add).then_inc(step, 1)
                        steps, src, shift = steps + 2, 1 - src, 2 * shift
                    whole = total[src]
                    if counted(steps):
                        dve.wait_ge(step, steps)
                    nc.vector.tensor_scalar(size[:, :], whole[:, NS - 1, :], 1.0 / P, (P - 1) / (2.0 * P), ALU.mult, ALU.add).then_inc(step, 1)
                    dve.wait_ge(step, steps + 1)
                    nc.vector.tensor_scalar(size[:, :], size[:, :], MAGIC, 1.0, ALU.add, ALU.mult).then_inc(step, 1)
                    dve.wait_ge(step, steps + 2)
                    nc.vector.tensor_scalar(padded[:, :], size[:, :], MAGIC, float(P), ALU.subtract, ALU.mult).then_inc(step, 1)
                    dve.wait_ge(step, steps + 3)
                    nc.vector.tensor_copy(base[0][:, :], padded[:, :]).then_inc(step, 1)
                    steps, at, shift = steps + 4, 0, 1
                    while shift < EXPERTS:
                        if counted(steps):
                            dve.wait_ge(step, steps)
                        nc.vector.tensor_copy(base[1 - at][:, 0:shift], base[at][:, 0:shift]).then_inc(step, 1)
                        nc.vector.tensor_tensor(base[1 - at][:, shift:], base[at][:, shift:], base[at][:, :EXPERTS - shift], ALU.add).then_inc(step, 1)
                        steps, at, shift = steps + 2, 1 - at, 2 * shift
                    if counted(steps):
                        dve.wait_ge(step, steps)
                    start = base[1 - at]
                    nc.vector.tensor_tensor(start[:, :], base[at][:, :], padded[:, :], ALU.subtract).then_inc(step, 1)
                    other = total[1 - src]
                    nc.vector.tensor_tensor(other[:, :, :], whole[:, :, :], count_b[:, :, :], ALU.subtract).then_inc(step, 1)
                    dve.wait_ge(step, steps + 2)
                    nc.vector.tensor_tensor(other[:, :, :], other[:, :, :], start[:, :].unsqueeze(1).broadcast_to([P, NS, EXPERTS]), ALU.add).then_inc(step, 1)
                    nc.vector.tensor_scalar(index[:, :], index_b[:, :], float(P), 0.0, ALU.mult, ALU.add).then_inc(step, 1)
                    dve.wait_ge(step, steps + 4)
                    nc.vector.tensor_tensor(other[:, :, :], other[:, :, :], within_b[:, :, :], ALU.add).then_inc(step, 1)
                    nc.vector.tensor_tensor(begun[:, :, :], index[:, 0:NT].unsqueeze(2).broadcast_to([P, NT, EXPERTS]),
                                            start[:, :].unsqueeze(1).broadcast_to([P, NT, EXPERTS]), ALU.is_ge).then_inc(step, 1)
                    if counted(steps + 6):
                        dve.wait_ge(step, steps + 6)
                    nc.vector.tensor_tensor(other[:, :, :], other[:, :, :], chosen[:, :, :], ALU.mult).then_inc(step, 1)
                    nc.vector.tensor_reduce(expert_f[:, :], begun[:, :, :], axis=AX.X, op=ALU.add).then_inc(step, 1)
                    dve.wait_ge(step, steps + 8)
                    nc.vector.tensor_reduce(slot_f[:, :], other[:, :, :], axis=AX.X, op=ALU.add).then_inc(step, 1)
                    nc.vector.tensor_scalar(expert[:, :], expert_f[:, :], 1.0, 0.0, ALU.subtract, ALU.max).then_inc(step, 1)
                    if counted(steps + 10):
                        dve.wait_ge(step, steps + 10)
                    nc.vector.tensor_copy(slot[:, :], slot_f[:, :]).then_inc(step, 1)
                    if counted(steps + 11):
                        dve.wait_ge(step, steps + 11)

            with nc.Block() as block:

                @block.gpsimd
                def _(pool):
                    for t in range(NS):
                        nc.gpsimd.indirect_dma_start(Xs[:, :], bass.IndirectOffsetOnAxis(ap=slot[:, t:t + 1], axis=0), xn[:, t, :], None).then_inc(scattered, 16)
                    pool.wait_ge(scattered, 16 * NS)

        run = ExitStack()
        with run:
            def eb(n, shape, dt=F32):
                return sb(n, shape, dt, run)

            def pb(n, shape):
                return run.enter_context(nc.psum_tensor(f"moe_{n}", shape, F32))

            xs, xsT = eb("xs", [P, 3, D]), eb("xsT", [D, 3, P])
            gated, hid, hidT = eb("gated", [P, INNER]), eb("hid", [P, 3, CH * P]), eb("hidT", [P, CH, P])
            ys = eb("ys", [P, 3, D])
            xt_b, g_b, u_b, ht_b, y_b = pb("xt_b", [P, P]), pb("g_b", [P, INNER]), pb("u_b", [P, INNER]), pb("ht_b", [P, CH, P]), pb("y_b", [P, D])
            xs_in, xsT_ps, xsT_sb, g_ps, u_ps, gated_sb, hid_sb, hidT_ps, hidT_sb, y_ps, y_sb, y_out, hid_zero, sp_waits_met = (
                sem(n) for n in ("xs_in", "xsT_ps", "xsT_sb", "g_ps", "u_ps", "gated_sb", "hid_sb", "hidT_ps", "hidT_sb", "y_ps", "y_sb", "y_out", "hid_zero", "sp_waits_met"))

            with nc.Block() as block:

                @block.sync
                def _(sp):
                    def iteration(t, k):
                        if does(t, 3, NT):
                            if counted(t + 1):
                                sp.wait_ge(xsT_ps, t + 1)
                                sp.sem_inc(sp_waits_met, 1)
                            if counted(16 * (t + 3)):
                                sp.wait_ge(xs_in, 16 * (t + 3))
                                sp.sem_inc(sp_waits_met, 1)
                            sp.dma_start(xs[:, k, :], Xs[bass.ds(P * (t + 3), P), :]).then_inc(xs_in, 16)
                        if does(t, 0, NT):
                            if counted(t + 1):
                                sp.wait_ge(y_sb, t + 1)
                                sp.sem_inc(sp_waits_met, 1)
                            if counted(16 * t):
                                sp.wait_ge(y_out, 16 * t)
                                sp.sem_inc(sp_waits_met, 1)
                            sp.dma_start(Ys[bass.ds(P * t, P), :], ys[:, k, :]).then_inc(y_out, 16)

                    groups_loop(sp, NT, iteration, ahead=3)
                    sp.wait_ge(y_out, 16 * NT)

                @block.scalar
                def _(act):
                    def iteration(t, k):
                        if does(t, 2, NT):
                            if counted(t + 3):
                                act.wait_ge(xsT_ps, t + 3)
                            if counted(t):
                                act.wait_ge(u_ps, t)
                            nc.scalar.activation(xsT[:, (k + 2) % 3, :], xt_b[:, :], ACT.Copy).then_inc(xsT_sb, 1)
                        if does(t, 0, NT):
                            if counted(t + 1):
                                act.wait_ge(hidT_ps, t + 1)
                            if counted(t):
                                act.wait_ge(y_ps, t)
                            nc.scalar.activation(hidT[:, :, :], ht_b[:, :, :], ACT.Copy).then_inc(hidT_sb, 1)
                        if does(t, 1, NT):
                            if counted(t + 2):
                                act.wait_ge(g_ps, t + 2)
                            if counted(t + 1):
                                act.wait_ge(hid_sb, t + 1)
                            nc.scalar.activation(gated[:, :], g_b[:, :], ACT.Silu).then_inc(gated_sb, 1)

                    groups_loop(act, NT, iteration, ahead=3)

                @block.vector
                def _(dve):
                    nc.vector.memset(hid[:, :, :], 0.0).then_inc(hid_zero, 1)
                    dve.wait_ge(hid_zero, 1)

                    def iteration(t, k):
                        if does(t, 1, NT):
                            if counted(t + 2):
                                dve.wait_ge(gated_sb, t + 2)
                            if counted(t + 2):
                                dve.wait_ge(u_ps, t + 2)
                            if counted(t - 1):
                                dve.wait_ge(hidT_ps, t - 1)
                            nc.vector.tensor_tensor(hid[:, (k + 1) % 3, 0:INNER], gated[:, :], u_b[:, :], ALU.mult).then_inc(hid_sb, 1)
                        if does(t, 0, NT):
                            if counted(t + 1):
                                dve.wait_ge(y_ps, t + 1)
                            if counted(16 * (t - 1)):
                                dve.wait_ge(y_out, 16 * (t - 1))
                            nc.vector.tensor_copy(ys[:, k, :], y_b[:, :]).then_inc(y_sb, 1)

                    groups_loop(dve, NT, iteration, ahead=3)

                @block.tensor
                def _(pe):
                    why = "the table has whole numbers from 0 to 7 only: a count of eight comparisons, less one, and at least 0"

                    def iteration(t, k):
                        if does(t, 2, NT):
                            if counted(16 * (t + 3)):
                                pe.wait_ge(xs_in, 16 * (t + 3))
                            if counted(t + 2):
                                pe.wait_ge(xsT_sb, t + 2)
                            nc.tensor.transpose(xt_b[:, :], xs[:, (k + 2) % 3, :], ident[:, :]).then_inc(xsT_ps, 1)
                        if does(t, 0, NT):
                            if counted(t + 1):
                                pe.wait_ge(hid_sb, t + 1)
                            if counted(t):
                                pe.wait_ge(hidT_sb, t)
                            for c in range(CH):
                                last = nc.tensor.transpose(ht_b[:, c, :], hid[:, k, c * P:(c + 1) * P], ident[:, :])
                            last.then_inc(hidT_ps, 1)
                        if does(t, 1, NT):
                            e = nc.values_load(expert[0:1, bass.ds(t + 1, 1)], engines=[mybir.EngineType.PE], min_val=0, max_val=EXPERTS - 1,
                                               skip_runtime_bounds_check_because=why)
                            if counted(t + 2):
                                pe.wait_ge(xsT_sb, t + 2)
                            if counted(t + 1):
                                pe.wait_ge(gated_sb, t + 1)
                            nc.tensor.matmul(g_b[:, :], xsT[:, (k + 1) % 3, :], gate[:, bass.ds(e, 1), :].rearrange("p o i -> p (o i)"), start=True, stop=True).then_inc(g_ps, 1)
                            if counted(t + 1):
                                pe.wait_ge(hid_sb, t + 1)
                            nc.tensor.matmul(u_b[:, :], xsT[:, (k + 1) % 3, :], up[:, bass.ds(e, 1), :].rearrange("p o i -> p (o i)"), start=True, stop=True).then_inc(u_ps, 1)
                        if does(t, 0, NT):
                            e = nc.values_load(expert[0:1, bass.ds(t, 1)], engines=[mybir.EngineType.PE], min_val=0, max_val=EXPERTS - 1,
                                               skip_runtime_bounds_check_because=why)
                            if counted(t + 1):
                                pe.wait_ge(hidT_sb, t + 1)
                            if counted(t):
                                pe.wait_ge(y_sb, t)
                            for c in range(CH):
                                last = nc.tensor.matmul(y_b[:, :], hidT[:, c, :], down[:, c, bass.ds(e, 1), :].rearrange("p o i -> p (o i)"), start=(c == 0), stop=(c == CH - 1))
                            last.then_inc(y_ps, 1)

                    groups_loop(pe, NT, iteration, ahead=3)

            gathered, x_out = [sem(f"gathered{g}") for g in range(N)], sem("x_out")
            with nc.Block() as block:

                @block.gpsimd
                def _(pool):
                    for t in range(NS):
                        nc.gpsimd.indirect_dma_start(xn[:, t, :], None, Ys[:, :], bass.IndirectOffsetOnAxis(ap=slot[:, t:t + 1], axis=0)).then_inc(gathered[t // GB], 16)

                @block.vector
                def _(dve):
                    for g in range(N):
                        dve.wait_ge(gathered[g], 16 * GB)
                        xg = x[:, GB * g:GB * g + GB, :]
                        nc.vector.tensor_tensor(xg, xg, xn[:, GB * g:GB * g + GB, :], ALU.add).then_inc(x_out, 1)
                    dve.wait_ge(x_out, N)


def load(nc, env, x_in, n_seqs):
    x, ident = env["x"], env["ident"]
    ctx = ExitStack()
    with ctx:
        loaded, ident_set = (nc.alloc_semaphore(f"load_{n}") for n in ("loaded", "ident_set"))
        with nc.Block() as block:

            @block.sync
            def _(sp):
                part = n_seqs // 8
                for i in range(8):
                    r = slice(i * part, (i + 1) * part)
                    sp.dma_start(x[:, r, :], x_in[r, :, :].rearrange("b s c -> s b c")).then_inc(loaded, 16)
                sp.wait_ge(loaded, 16 * 8)

            @block.gpsimd
            def _(pool):
                nc.gpsimd.memset(ident[:, :], 0.0).then_inc(ident_set, 1)
                pool.wait_ge(ident_set, 1)
                nc.gpsimd.affine_select(out=ident[:, :], in_=ident[:, :], compare_op=ALU.not_equal, fill=1.0,
                                        base=0, pattern=[[-1, P]], channel_multiplier=1).then_inc(ident_set, 1)
                pool.wait_ge(ident_set, 2)


def prepare_stacks(nc, env, name):
    QST, KST = env["QST"], env["KST"]
    ctx = ExitStack()
    with ctx:
        ones = ctx.enter_context(nc.sbuf_tensor(f"{name}_ones", [2, T], BF16))
        ones_set, stacks_zero, rows_set = (nc.alloc_semaphore(f"{name}_prepare_{n}") for n in ("ones_set", "stacks_zero", "rows_set"))
        with nc.Block() as block:

            @block.sync
            def _(sp):
                sp.wait_ge(ones_set, 1)
                sp.wait_ge(stacks_zero, 2)
                for p in range(2):
                    r = HALF * p + ROWS
                    sp.dma_start(KST[r:r + 2, :, :, :].rearrange("r a g n -> r (a g) n"),
                                 ones[:, :].unsqueeze(1).broadcast_to([2, 3 * H16 // 2, T])).then_inc(rows_set, 16)
                    sp.dma_start(QST[r + 2:r + 3, :, :, :].rearrange("r a h n -> r (a h) n")[:, p::2, :],
                                 ones[0:1, :].unsqueeze(1).broadcast_to([1, 3 * H16 // 2, T])).then_inc(rows_set, 16)
                sp.wait_ge(rows_set, 64)

            @block.gpsimd
            def _(pool):
                nc.gpsimd.memset(ones[:, :], 1.0).then_inc(ones_set, 1)
                nc.gpsimd.memset(KST[:, :, :, :].rearrange("p a h n -> p (a h n)").bitcast(F32), 0.0).then_inc(stacks_zero, 1)
                pool.wait_ge(ones_set, 1)

            @block.vector
            def _(dve):
                nc.vector.memset(QST[:, :, :, :].rearrange("p a h n -> p (a h n)").bitcast(F32), 0.0).then_inc(stacks_zero, 1)
                dve.wait_ge(stacks_zero, 2)


def store(nc, env, out, n_seqs):
    x = env["x"]
    ctx = ExitStack()
    with ctx:
        stored = nc.alloc_semaphore("stored")
        with nc.Block() as block:

            @block.sync
            def _(sp):
                part = n_seqs // 8
                for i in range(8):
                    r = slice(i * part, (i + 1) * part)
                    sp.dma_start(out[r, :, :].rearrange("b s c -> s b c"), x[:, r, :]).then_inc(stored, 16)
                sp.wait_ge(stored, 16 * 8)


def with_stacks(nc, env, name, phases):
    ctx = ExitStack()
    with ctx:
        env = dict(env)
        env["QST"] = ctx.enter_context(nc.sbuf_tensor(f"{name}_QST", [P, 3, H16, T], BF16))
        env["KST"] = ctx.enter_context(nc.sbuf_tensor(f"{name}_KST", [P, 3, H16 // 2, T], BF16))
        with nc.cleanup_on_exit():
            prepare_stacks(nc, env, name)
        for phase in phases:
            with nc.cleanup_on_exit():
                phase(env)


def plain_phase(nc, n_groups, name, a, names, cross, mask):
    wq, bq, wk, bk, wv, bv, wo, bo = names
    weights = dict(wq=a[wq], wk=a[wk], wv=a[wv], wo=a[wo], bq=a[bq].unsqueeze(1), bk=a[bk].unsqueeze(1), bv=a[bv].unsqueeze(0), bo=a[bo].unsqueeze(0))
    if cross:
        weights["context"] = a["ctx_1024"]
    if mask == "given":
        weights["mask"] = a["mask_Bx1x1xS2_bk0"].rearrange("b i j t -> i (b j t)")
    return lambda env: plain_attention(nc, env, name, n_groups, cross, weights, mask)


def build(nc, a, out, n_seqs=64, phases=("a0", "x0", "moe", "a1", "x1", "ffn")):
    ctx = ExitStack()
    with ctx:
        env = {
            "x": ctx.enter_context(nc.sbuf_tensor("x", [P, n_seqs, D], F32)),
            "ident": ctx.enter_context(nc.sbuf_tensor("ident", [P, P], F32)),
        }
        n_groups = n_seqs // GB
        with nc.cleanup_on_exit():
            load(nc, env, a["x"], n_seqs)
        if "a0" in phases:
            with nc.cleanup_on_exit():
                w = {n: a[f"L0_attn_{n}"] for n in ("Wq", "Wk", "Wv", "Wo", "Wc2q", "bc2q", "Wm", "W2", "b1", "bqo", "bm", "b2")}
                w.update({n: a[f"L0_attn_{n}"].unsqueeze(0) for n in ("bo", "g1", "beta1", "g2", "beta2")})
                w.update(W1T=a["L0_attn_W1"], WqoT=a["L0_attn_Wqo"], bq=a["L0_attn_bq"].rearrange("h d -> (h d)").unsqueeze(1),
                         bk=a["L0_attn_bk"].rearrange("h d -> (h d)").unsqueeze(1), bv=a["L0_attn_bv"].rearrange("h d -> (h d)").unsqueeze(0))
                quantum_block(nc, env, n_groups, w)
        if "x0" in phases:
            with_stacks(nc, env, "x0", [plain_phase(nc, n_groups, "x0", a, [f"L0_xattn_{n}" for n in ("Wq", "bq", "Wk", "bk", "Wv", "bv", "Wo", "bo")], True, None)])
        if "moe" in phases:
            with nc.cleanup_on_exit():
                experts(nc, env, n_groups, dict(router=a["L0_ffn_router_w"], gate=a["L0_ffn_gate_w"], up=a["L0_ffn_up_w"], down=a["L0_ffn_down_w"]))
        layer1 = []
        if "a1" in phases:
            layer1.append(plain_phase(nc, n_groups, "a1", a, [f"L1_attn_{n}" for n in ("wq_w", "wq_b", "wk_w", "wk_b", "wv_w", "wv_b", "wo_w", "wo_b")], False, "zero_key"))
        if "x1" in phases:
            layer1.append(plain_phase(nc, n_groups, "x1", a, [f"L1_xattn_{n}" for n in ("Wq", "bq", "Wk", "bk", "Wv", "bv", "Wc", "bc")], True, "given"))
        if layer1:
            with_stacks(nc, env, "layer1", layer1)
        if "ffn" in phases:
            with nc.cleanup_on_exit():
                ternary_ffn(nc, env, n_groups, dict(w1=a["L1_ffn_w1"], w2=a["L1_ffn_w2"], b1=a["L1_ffn_b1"].unsqueeze(0), b2=a["L1_ffn_b2"].unsqueeze(0)))
        store(nc, env, out, n_seqs)


TRANSPOSED = {"L1_attn_wq_w", "L1_attn_wk_w", "L1_attn_wv_w", "L1_attn_wo_w", "L1_xattn_Wq", "L1_xattn_Wk", "L1_xattn_Wv", "L1_xattn_Wc",
              "L1_ffn_w1", "L1_ffn_w2", "L0_attn_W1", "L0_attn_Wqo", "L0_ffn_router_w"}


def layout(name, value):
    if name in TRANSPOSED:
        value = value.T
    elif name in ("L0_attn_Wq", "L0_attn_Wk", "L0_attn_Wv"):
        value = value.transpose(1, 0, 2).reshape(D, D)
    elif name in ("L0_ffn_gate_w", "L0_ffn_up_w"):
        value = value.transpose(2, 0, 1)
    elif name == "L0_ffn_down_w":
        value = value.transpose(2, 0, 1)
    return np.ascontiguousarray(value)


def kernel(**inputs):
    import concourse.bacc as bacc
    from concourse.bass_utils import run_bass_kernel_spmd

    nc = bacc.Bacc("TRN2", target_bir_lowering=False, num_devices=1)
    arrays, args = {}, {}
    for name, value in inputs.items():
        arrays[f"in_{name}"] = layout(name, np.asarray(value))
        args[name] = nc.dram_tensor(f"in_{name}", arrays[f"in_{name}"].shape, mybir.dt.from_np(arrays[f"in_{name}"].dtype), kind="ExternalInput").ap()
    shape = inputs["x"].shape
    out = nc.dram_tensor("out", shape, F32, kind="ExternalOutput").ap()
    build(nc, args, out, n_seqs=shape[0])
    return run_bass_kernel_spmd(nc, [arrays], core_ids=[0]).results[0]["out"]
```
